# Optimizing a Trainium2 kernel written in Bass

```python
import numpy as np
import jax
import jax.numpy as jnp

def _softmax(x, axis=-1):
    return jax.nn.softmax(x, axis=axis)

def _gelu(x):
    return jax.nn.gelu(x, approximate=True)

def _silu(x):
    return jax.nn.silu(x)

def _sigmoid(x):
    return jax.nn.sigmoid(x)

def _layernorm(x, axis=-1, eps=1e-05):
    m = jnp.mean(x, axis=axis, keepdims=True)
    v = jnp.var(x, axis=axis, keepdims=True)
    return (x - m) / jnp.sqrt(v + eps)

def _scatter_add(tgt, idx, src, axis=0):
    return tgt.at[idx].add(src)

def _segment_sum(src, seg, n):
    return jax.ops.segment_sum(src, seg, n)
kernel_name = 'mk_flamingo_gated_d4_seqx_r8_f7ed8c'

def setup_inputs(seed: int=0):
    np.random.seed(seed)
    _w = jnp.asarray

    def _rec_inputs():
        import jax
        import jax.numpy as jnp
        _rk = jax.random.key(seed)
        x = 7.22e-05 + 1 * jax.random.normal(jax.random.fold_in(_rk, 1), (4, 256, 128), jnp.float32)
        _lenS = 256 - jax.random.randint(jax.random.fold_in(_rk, 7), (4,), 0, max(1, 256 // 4) + 1, jnp.int32)
        _lenS2 = 256 - jax.random.randint(jax.random.fold_in(_rk, 8), (4,), 0, max(1, 256 // 4) + 1, jnp.int32)
        _ctx_1024P = jax.random.normal(jax.random.fold_in(_rk, 11), (4, 16, 128), jnp.float32)
        _ctx_1024c = jax.random.dirichlet(jax.random.fold_in(_rk, 511), 0.3 * jnp.ones((16,), jnp.float32), (4, 256))
        _ctx_1024t = jnp.einsum('bsk,bkd->bsd', _ctx_1024c, _ctx_1024P)
        _ctx_1024t = _ctx_1024t * jax.lax.rsqrt(jnp.mean(jnp.square(_ctx_1024t)) + 1e-12) * 0.953939
        ctx_1024 = 4.13588e-05 + 0.999923 * (_ctx_1024t + 0.3 * jax.random.normal(jax.random.fold_in(_rk, 611), (4, 256, 128), jnp.float32))
        _validS = jnp.arange(256)[None, :] < _lenS[:, None]
        _validS2 = jnp.arange(256)[None, :] < _lenS2[:, None]
        _causal = jnp.tril(jnp.ones((256, 256), dtype=bool))
        mask_BxS_bf1 = jnp.ones((4, 256), dtype=bool)
        mask_Bx1xSxS2_if1 = jnp.where(jnp.ones((4, 1, 256, 256), dtype=bool), 1, 0).astype(jnp.int32)
        _g = jax.random.normal(jax.random.fold_in(_rk, 9001), (2, 4), jnp.float32)
        _g = jnp.sign(_g) * jnp.maximum(jnp.abs(_g), 1.0) + (_g == 0) * 1.0
        g_xattn = _g[0]
        g_ffn = _g[1]
        return (x, ctx_1024, _lenS2, mask_BxS_bf1, mask_Bx1xSxS2_if1, g_xattn, g_ffn)
    x, ctx_1024, _lenS2, mask_BxS_bf1, mask_Bx1xSxS2_if1, g_xattn, g_ffn = _rec_inputs()

    def _L0_xattn_setup():
        import jax, jax.numpy as jnp
        import numpy as np
        BS, SEQ, D_MODEL, NHEADS = (4, 256, 128, 16)
        D_K = D_MODEL // NHEADS
        NEG_INF = -1000000000.0
        key = jax.random.key(seed)
        k1, k2, k3, k4, k5 = jax.random.split(key, 5)
        Q = jax.random.normal(k1, (BS, SEQ, D_MODEL), dtype=jnp.float32)
        K = jax.random.normal(k2, (BS, SEQ, D_MODEL), dtype=jnp.float32)
        V = jax.random.normal(k3, (BS, SEQ, D_MODEL), dtype=jnp.float32)
        Wq = jax.random.normal(k4, (D_MODEL, D_MODEL), dtype=jnp.float32) * D_MODEL ** (-0.5)
        lens = jax.random.randint(k5, (BS,), 1, SEQ + 1, dtype=jnp.int32)
        return {'Q': Q, 'K': K, 'V': V, 'Wq': Wq, 'lens': lens}
    _L0_xattn_all = _L0_xattn_setup()
    _L0_xattn_in = {k: v for k, v in _L0_xattn_all.items() if k in ('Wq',)}
    del _L0_xattn_all

    def _L0_ffn_setup():
        import jax, jax.numpy as jnp
        import numpy as np
        E = 8
        key = jax.random.key(seed)
        k0, k1, k2, k3 = jax.random.split(key, 4)
        B, S, H, F = (4, 512, 128, 512)
        x = jax.random.normal(k0, (B, S, H), jnp.float32)
        Wr = jax.random.normal(k1, (E, H), jnp.float32) * 0.02
        W1 = jax.random.normal(k2, (E, H, F), jnp.float32) * 0.02
        b1 = jnp.zeros((E, F), jnp.float32)
        W2 = jax.random.normal(k3, (E, F, H), jnp.float32) * 0.02
        b2 = jnp.zeros((E, H), jnp.float32)
        return {'x': x, 'Wr': Wr, 'W1': W1, 'b1': b1, 'W2': W2, 'b2': b2}
    _L0_ffn_all = _L0_ffn_setup()
    _L0_ffn_in = {k: v for k, v in _L0_ffn_all.items() if k in ('Wr', 'W1', 'b1', 'W2', 'b2')}
    del _L0_ffn_all

    def _L1_xattn_setup():
        import jax, jax.numpy as jnp
        import numpy as np
        B, T, D = (8, 256, 128)
        key = jax.random.key(seed)
        kq, kk, kv = jax.random.split(key, 3)
        return {'query': jax.random.normal(kq, (B, T, D), dtype=jnp.float32), 'key': jax.random.normal(kk, (B, T, D), dtype=jnp.float32), 'value': jax.random.normal(kv, (B, T, D), dtype=jnp.float32)}
    _L1_xattn_all = _L1_xattn_setup()
    _L1_xattn_in = {k: v for k, v in _L1_xattn_all.items() if k in ()}
    del _L1_xattn_all

    def _L1_ffn_setup():
        import jax, jax.numpy as jnp
        import numpy as np
        B, L, D = (2, 256, 128)
        E = 15
        H = D * 1
        K = 3
        T = 1.0
        key = jax.random.key(seed)
        ks = jax.random.split(key, 12)
        s = 0.02
        return {'x': jax.random.normal(ks[0], (B, L, D), dtype=jnp.float32), 'router_W': jax.random.normal(ks[1], (D, E), dtype=jnp.float32) * s, 'router_b': jnp.zeros((E,), dtype=jnp.float32), 'sW1': jax.random.normal(ks[2], (D, H), dtype=jnp.float32) * s, 'sb1': jnp.zeros((H,), dtype=jnp.float32), 'sW2': jax.random.normal(ks[3], (H, D), dtype=jnp.float32) * s, 'sb2': jnp.zeros((D,), dtype=jnp.float32), 'eW1': jax.random.normal(ks[4], (E, D, H), dtype=jnp.float32) * s, 'eb1': jnp.zeros((E, H), dtype=jnp.float32), 'eW2': jax.random.normal(ks[5], (E, H, D), dtype=jnp.float32) * s, 'eb2': jnp.zeros((E, D), dtype=jnp.float32)}
    _L1_ffn_all = _L1_ffn_setup()
    _L1_ffn_in = {k: v for k, v in _L1_ffn_all.items() if k in ('router_W', 'router_b', 'sW1', 'sb1', 'sW2', 'sb2', 'eW1', 'eb1', 'eW2', 'eb2')}
    del _L1_ffn_all

    def _L2_xattn_setup():
        import jax, jax.numpy as jnp
        import numpy as np
        L = 2
        D = 128
        HS = 128
        NH = 16
        DH = 64
        FF = 512
        ROT = 32
        B, SQ, SK = (64, 128, 64)
        EPS = 1e-08

        def rmsnorm(x, w):
            norm = jnp.sqrt(jnp.sum(x * x, axis=-1, keepdims=True)) * x.shape[-1] ** (-0.5)
            return x / jnp.maximum(norm, EPS) * w

        def rope_freqs(n):
            inv_freq = 1.0 / 10000.0 ** (jnp.arange(0, ROT, 2, dtype=jnp.float32) / ROT)
            f = jnp.arange(n, dtype=jnp.float32)[:, None] * inv_freq[None, :]
            return jnp.concatenate([f, f], axis=-1)[None, None]

        def apply_rope(t, freqs):
            rd = freqs.shape[-1]
            t1, tp = (t[..., :rd], t[..., rd:])
            half = rd // 2
            a, b = (t1[..., :half], t1[..., half:])
            rot = jnp.concatenate([-b, a], axis=-1)
            t1 = t1 * jnp.cos(freqs) + rot * jnp.sin(freqs)
            return jnp.concatenate([t1, tp], axis=-1)

        def attention(x, ctx, Wq, Wk, Wv, Wo, bo, pe_q, pe_k, mask):
            b, n, _ = x.shape
            m = ctx.shape[1]
            q = (x @ Wq).reshape(b, n, NH, DH).transpose(0, 2, 1, 3) * DH ** (-0.5)
            k = (ctx @ Wk).reshape(b, m, NH, DH).transpose(0, 2, 1, 3)
            v = (ctx @ Wv).reshape(b, m, NH, DH).transpose(0, 2, 1, 3)
            q = apply_rope(q, pe_q)
            k = apply_rope(k, pe_k)
            sim = jnp.einsum('bhid,bhjd->bhij', q, k)
            if mask is not None:
                sim = jnp.where(mask[:, None, None, :], sim, -jnp.finfo(sim.dtype).max)
            attn = jax.nn.softmax(sim, axis=-1)
            out = jnp.einsum('bhij,bhjd->bhid', attn, v)
            out = out.transpose(0, 2, 1, 3).reshape(b, n, NH * DH)
            return out @ Wo + bo
        key = jax.random.key(seed)
        ks = jax.random.split(key, 24)
        s = 0.02
        inp = {'x': jax.random.normal(ks[0], (B, SQ, D), jnp.float32), 'chunked_seq': jax.random.normal(ks[1], (B, SK, HS), jnp.float32), 'mask': jnp.ones((B, SQ), dtype=bool), 'attn_norm_w': jnp.ones((L, D), jnp.float32), 'Wq': jax.random.normal(ks[2], (L, D, NH * DH), jnp.float32) * s, 'Wk': jax.random.normal(ks[3], (L, D, NH * DH), jnp.float32) * s, 'Wv': jax.random.normal(ks[4], (L, D, NH * DH), jnp.float32) * s, 'Wo': jax.random.normal(ks[5], (L, NH * DH, D), jnp.float32) * s, 'bo': jnp.zeros((L, D), jnp.float32), 'cross_norm_w': jnp.ones((L, D), jnp.float32), 'cWq': jax.random.normal(ks[6], (L, D, NH * DH), jnp.float32) * s, 'cWk': jax.random.normal(ks[7], (HS, NH * DH), jnp.float32) * s if False else jax.random.normal(ks[7], (L, HS, NH * DH), jnp.float32) * s, 'cWv': jax.random.normal(ks[8], (L, HS, NH * DH), jnp.float32) * s, 'cWo': jax.random.normal(ks[9], (L, NH * DH, D), jnp.float32) * s, 'cbo': jnp.zeros((L, D), jnp.float32), 'ff_norm_w': jnp.ones((L, D), jnp.float32), 'ff_w1': jax.random.normal(ks[10], (L, D, FF), jnp.float32) * s, 'ff_b1': jnp.zeros((L, FF), jnp.float32), 'ff_w2': jax.random.normal(ks[11], (L, FF, D), jnp.float32) * s, 'ff_b2': jnp.zeros((L, D), jnp.float32), 'norm_out_w': jnp.ones((D,), jnp.float32), 'proj_w': jax.random.normal(ks[12], (D, HS), jnp.float32) * s, 'proj_b': jnp.zeros((HS,), jnp.float32)}
        return inp
    _L2_xattn_all = _L2_xattn_setup()
    _L2_xattn_in = {k: v for k, v in _L2_xattn_all.items() if k in ('attn_norm_w', 'Wq', 'Wk', 'Wv', 'Wo', 'bo', 'cross_norm_w', 'cWq', 'cWk', 'cWv', 'cWo', 'cbo', 'ff_norm_w', 'ff_w1', 'ff_b1', 'ff_w2', 'ff_b2', 'norm_out_w', 'proj_w', 'proj_b')}
    del _L2_xattn_all

    def _L2_ffn_setup():
        import jax, jax.numpy as jnp
        import numpy as np
        key = jax.random.key(seed)
        kx, kw = jax.random.split(key)
        x = jax.random.normal(kx, (32, 512, 128), dtype=jnp.float32)
        weight = jax.random.normal(kw, (128, 128), dtype=jnp.float32) * 0.01
        return {'x': x, 'weight': weight}
    _L2_ffn_all = _L2_ffn_setup()
    _L2_ffn_in = {k: v for k, v in _L2_ffn_all.items() if k in ('weight',)}
    del _L2_ffn_all

    def _L3_xattn_setup():
        import jax, jax.numpy as jnp
        import numpy as np
        B, S, H, NH = (2, 256, 128, 16)
        DK = H // NH

        def _split_heads(x):
            b, s, _ = x.shape
            return x.reshape(b, s, NH, DK).transpose(0, 2, 1, 3)
        key = jax.random.key(seed)
        ks = jax.random.split(key, 10)
        init = lambda k, shape: jax.random.normal(k, shape, dtype=jnp.float32) * 0.02
        return {'query': jax.random.normal(ks[0], (B, S, H), dtype=jnp.float32), 'key': jax.random.normal(ks[1], (B, S, H), dtype=jnp.float32), 'attn_mask': jnp.ones((B, 1, S, S), dtype=jnp.int32), 'Wq': init(ks[2], (H, H)), 'bq': init(ks[3], (H,)), 'Wk': init(ks[4], (H, H)), 'bk': init(ks[5], (H,)), 'Wv': init(ks[6], (H, H)), 'bv': init(ks[7], (H,)), 'Wo': init(ks[8], (H, H)), 'bo': init(ks[9], (H,))}
    _L3_xattn_all = _L3_xattn_setup()
    _L3_xattn_in = {k: v for k, v in _L3_xattn_all.items() if k in ('Wq', 'bq', 'Wk', 'bk', 'Wv', 'bv', 'Wo', 'bo')}
    del _L3_xattn_all

    def _L3_ffn_setup():
        import jax, jax.numpy as jnp
        import numpy as np
        B, S, H = (4, 256, 128)
        E, K = (8, 2)
        I_R, I_S = (4 * H, 8 * H)
        CAP_FACTOR = 1.25
        SCALE = 1.0
        key = jax.random.key(seed)
        ks = jax.random.split(key, 9)
        std = 0.02
        return {'x': jax.random.normal(ks[0], (B, S, H), jnp.float32), 'router_w': std * jax.random.normal(ks[1], (E, H), jnp.float32), 'rg': std * jax.random.normal(ks[2], (E, H, I_R), jnp.float32), 'ru': std * jax.random.normal(ks[3], (E, H, I_R), jnp.float32), 'rd': std * jax.random.normal(ks[4], (E, I_R, H), jnp.float32), 'sg': std * jax.random.normal(ks[5], (H, I_S), jnp.float32), 'su': std * jax.random.normal(ks[6], (H, I_S), jnp.float32), 'sd': std * jax.random.normal(ks[7], (I_S, H), jnp.float32)}
    _L3_ffn_all = _L3_ffn_setup()
    _L3_ffn_in = {k: v for k, v in _L3_ffn_all.items() if k in ('router_w', 'rg', 'ru', 'rd', 'sg', 'su', 'sd')}
    del _L3_ffn_all
    return {'x': x, 'ctx_1024': ctx_1024, '_lenS2': _lenS2, 'mask_BxS_bf1': mask_BxS_bf1, 'mask_Bx1xSxS2_if1': mask_Bx1xSxS2_if1, 'g_xattn': g_xattn, 'g_ffn': g_ffn, 'L0_xattn_Wq': _L0_xattn_in['Wq'], 'L0_ffn_Wr': _L0_ffn_in['Wr'], 'L0_ffn_W1': _L0_ffn_in['W1'], 'L0_ffn_b1': _L0_ffn_in['b1'], 'L0_ffn_W2': _L0_ffn_in['W2'], 'L0_ffn_b2': _L0_ffn_in['b2'], 'L1_ffn_router_W': _L1_ffn_in['router_W'], 'L1_ffn_router_b': _L1_ffn_in['router_b'], 'L1_ffn_sW1': _L1_ffn_in['sW1'], 'L1_ffn_sb1': _L1_ffn_in['sb1'], 'L1_ffn_sW2': _L1_ffn_in['sW2'], 'L1_ffn_sb2': _L1_ffn_in['sb2'], 'L1_ffn_eW1': _L1_ffn_in['eW1'], 'L1_ffn_eb1': _L1_ffn_in['eb1'], 'L1_ffn_eW2': _L1_ffn_in['eW2'], 'L1_ffn_eb2': _L1_ffn_in['eb2'], 'L2_xattn_attn_norm_w': _L2_xattn_in['attn_norm_w'], 'L2_xattn_Wq': _L2_xattn_in['Wq'], 'L2_xattn_Wk': _L2_xattn_in['Wk'], 'L2_xattn_Wv': _L2_xattn_in['Wv'], 'L2_xattn_Wo': _L2_xattn_in['Wo'], 'L2_xattn_bo': _L2_xattn_in['bo'], 'L2_xattn_cross_norm_w': _L2_xattn_in['cross_norm_w'], 'L2_xattn_cWq': _L2_xattn_in['cWq'], 'L2_xattn_cWk': _L2_xattn_in['cWk'], 'L2_xattn_cWv': _L2_xattn_in['cWv'], 'L2_xattn_cWo': _L2_xattn_in['cWo'], 'L2_xattn_cbo': _L2_xattn_in['cbo'], 'L2_xattn_ff_norm_w': _L2_xattn_in['ff_norm_w'], 'L2_xattn_ff_w1': _L2_xattn_in['ff_w1'], 'L2_xattn_ff_b1': _L2_xattn_in['ff_b1'], 'L2_xattn_ff_w2': _L2_xattn_in['ff_w2'], 'L2_xattn_ff_b2': _L2_xattn_in['ff_b2'], 'L2_xattn_norm_out_w': _L2_xattn_in['norm_out_w'], 'L2_xattn_proj_w': _L2_xattn_in['proj_w'], 'L2_xattn_proj_b': _L2_xattn_in['proj_b'], 'L2_ffn_weight': _L2_ffn_in['weight'], 'L3_xattn_Wq': _L3_xattn_in['Wq'], 'L3_xattn_bq': _L3_xattn_in['bq'], 'L3_xattn_Wk': _L3_xattn_in['Wk'], 'L3_xattn_bk': _L3_xattn_in['bk'], 'L3_xattn_Wv': _L3_xattn_in['Wv'], 'L3_xattn_bv': _L3_xattn_in['bv'], 'L3_xattn_Wo': _L3_xattn_in['Wo'], 'L3_xattn_bo': _L3_xattn_in['bo'], 'L3_ffn_router_w': _L3_ffn_in['router_w'], 'L3_ffn_rg': _L3_ffn_in['rg'], 'L3_ffn_ru': _L3_ffn_in['ru'], 'L3_ffn_rd': _L3_ffn_in['rd'], 'L3_ffn_sg': _L3_ffn_in['sg'], 'L3_ffn_su': _L3_ffn_in['su'], 'L3_ffn_sd': _L3_ffn_in['sd']}

def reference(x, ctx_1024, _lenS2, mask_BxS_bf1, mask_Bx1xSxS2_if1, g_xattn, g_ffn, L0_xattn_Wq, L0_ffn_Wr, L0_ffn_W1, L0_ffn_b1, L0_ffn_W2, L0_ffn_b2, L1_ffn_router_W, L1_ffn_router_b, L1_ffn_sW1, L1_ffn_sb1, L1_ffn_sW2, L1_ffn_sb2, L1_ffn_eW1, L1_ffn_eb1, L1_ffn_eW2, L1_ffn_eb2, L2_xattn_attn_norm_w, L2_xattn_Wq, L2_xattn_Wk, L2_xattn_Wv, L2_xattn_Wo, L2_xattn_bo, L2_xattn_cross_norm_w, L2_xattn_cWq, L2_xattn_cWk, L2_xattn_cWv, L2_xattn_cWo, L2_xattn_cbo, L2_xattn_ff_norm_w, L2_xattn_ff_w1, L2_xattn_ff_b1, L2_xattn_ff_w2, L2_xattn_ff_b2, L2_xattn_norm_out_w, L2_xattn_proj_w, L2_xattn_proj_b, L2_ffn_weight, L3_xattn_Wq, L3_xattn_bq, L3_xattn_Wk, L3_xattn_bk, L3_xattn_Wv, L3_xattn_bv, L3_xattn_Wo, L3_xattn_bo, L3_ffn_router_w, L3_ffn_rg, L3_ffn_ru, L3_ffn_rd, L3_ffn_sg, L3_ffn_su, L3_ffn_sd):
    import jax
    import jax.numpy as jnp

    def _L0_xattn_ref(Q, K, V, Wq, lens):
        import jax, jax.numpy as jnp
        import numpy as np
        BS, SEQ, D_MODEL, NHEADS = (4, 256, 128, 16)
        D_K = D_MODEL // NHEADS
        NEG_INF = -1000000000.0
        bs = Q.shape[0]

        def proj(x):
            y = x @ Wq.T
            return y.reshape(bs, -1, NHEADS, D_K).transpose(0, 2, 1, 3)
        q = proj(Q)
        k = proj(K)
        v = proj(V)
        score = jnp.einsum('bhqd,bhkd->bhqk', q, k) / jnp.sqrt(jnp.float32(D_MODEL))
        key_valid = jnp.arange(SEQ)[None, :] < lens[:, None]
        score = jnp.where(key_valid[:, None, None, :], score, NEG_INF)
        attn = jax.nn.softmax(score, axis=-1)
        out = jnp.einsum('bhqk,bhkd->bhqd', attn, v)
        out = out.transpose(0, 2, 1, 3).reshape(bs, -1, D_MODEL)
        return out

    def _L0_ffn_ref(x, Wr, W1, b1, W2, b2):
        import jax, jax.numpy as jnp
        import numpy as np
        E = 8
        B, S, H = x.shape
        xf = x.reshape(-1, H)
        probs = jax.nn.softmax(xf @ Wr.T, axis=-1)
        eid = E - 1
        h = jax.nn.gelu(xf @ W1[eid] + b1[eid], approximate=False)
        y = (h @ W2[eid] + b2[eid]) * probs[:, eid:eid + 1]
        return y.reshape(B, S, H)

    def _L1_xattn_ref(query, key, value):
        import jax, jax.numpy as jnp
        import numpy as np
        B, T, D = (8, 256, 128)
        d = query.shape[-1]
        scores = jnp.einsum('bqd,bkd->bqk', query, key) * d ** (-0.5)
        tril = jnp.tril(jnp.ones((query.shape[1], key.shape[1]), dtype=bool))
        scores = jnp.where(tril, scores, -jnp.inf)
        attn = jax.nn.softmax(scores, axis=-1)
        return jnp.einsum('bqk,bkd->bqd', attn, value)

    def _L1_ffn_ref(x, router_W, router_b, sW1, sb1, sW2, sb2, eW1, eb1, eW2, eb2):
        import jax, jax.numpy as jnp
        import numpy as np
        B, L, D = (2, 256, 128)
        E = 15
        H = D * 1
        K = 3
        T = 1.0
        b, l, d = x.shape
        n = b * l
        xt = x.reshape(n, d)
        shared = jax.nn.relu(xt @ sW1 + sb1) @ sW2 + sb2
        logits = xt @ router_W + router_b
        probs = jax.nn.softmax(logits / T, axis=-1)
        top_p, top_i = jax.lax.top_k(probs, K)
        cw = jnp.zeros((n, E), dtype=probs.dtype)
        cw = cw.at[jnp.arange(n)[:, None], top_i].set(top_p)
        h = jax.nn.relu(jnp.einsum('nd,edh->neh', xt, eW1) + eb1)
        ye = jnp.einsum('neh,ehd->ned', h, eW2) + eb2
        routed = jnp.einsum('ned,ne->nd', ye, cw)
        return (shared + routed).reshape(b, l, d)

    def _L2_xattn_ref(x, chunked_seq, mask, attn_norm_w, Wq, Wk, Wv, Wo, bo, cross_norm_w, cWq, cWk, cWv, cWo, cbo, ff_norm_w, ff_w1, ff_b1, ff_w2, ff_b2, norm_out_w, proj_w, proj_b):
        import jax, jax.numpy as jnp
        import numpy as np
        L = 2
        D = 128
        HS = 128
        NH = 16
        DH = 64
        FF = 512
        ROT = 32
        B, SQ, SK = (64, 128, 64)
        EPS = 1e-08

        def rmsnorm(x, w):
            norm = jnp.sqrt(jnp.sum(x * x, axis=-1, keepdims=True)) * x.shape[-1] ** (-0.5)
            return x / jnp.maximum(norm, EPS) * w

        def rope_freqs(n):
            inv_freq = 1.0 / 10000.0 ** (jnp.arange(0, ROT, 2, dtype=jnp.float32) / ROT)
            f = jnp.arange(n, dtype=jnp.float32)[:, None] * inv_freq[None, :]
            return jnp.concatenate([f, f], axis=-1)[None, None]

        def apply_rope(t, freqs):
            rd = freqs.shape[-1]
            t1, tp = (t[..., :rd], t[..., rd:])
            half = rd // 2
            a, b = (t1[..., :half], t1[..., half:])
            rot = jnp.concatenate([-b, a], axis=-1)
            t1 = t1 * jnp.cos(freqs) + rot * jnp.sin(freqs)
            return jnp.concatenate([t1, tp], axis=-1)

        def attention(x, ctx, Wq, Wk, Wv, Wo, bo, pe_q, pe_k, mask):
            b, n, _ = x.shape
            m = ctx.shape[1]
            q = (x @ Wq).reshape(b, n, NH, DH).transpose(0, 2, 1, 3) * DH ** (-0.5)
            k = (ctx @ Wk).reshape(b, m, NH, DH).transpose(0, 2, 1, 3)
            v = (ctx @ Wv).reshape(b, m, NH, DH).transpose(0, 2, 1, 3)
            q = apply_rope(q, pe_q)
            k = apply_rope(k, pe_k)
            sim = jnp.einsum('bhid,bhjd->bhij', q, k)
            if mask is not None:
                sim = jnp.where(mask[:, None, None, :], sim, -jnp.finfo(sim.dtype).max)
            attn = jax.nn.softmax(sim, axis=-1)
            out = jnp.einsum('bhij,bhjd->bhid', attn, v)
            out = out.transpose(0, 2, 1, 3).reshape(b, n, NH * DH)
            return out @ Wo + bo
        pe_q = rope_freqs(x.shape[-2])
        pe_k = rope_freqs(chunked_seq.shape[-2])
        for l in range(L):
            h = rmsnorm(x, attn_norm_w[l])
            x = attention(h, h, Wq[l], Wk[l], Wv[l], Wo[l], bo[l], pe_q, pe_q, mask) + x
            h = rmsnorm(x, cross_norm_w[l])
            x = attention(h, chunked_seq, cWq[l], cWk[l], cWv[l], cWo[l], cbo[l], pe_q, pe_k, None) + x
            h = rmsnorm(x, ff_norm_w[l])
            x = jax.nn.gelu(h @ ff_w1[l] + ff_b1[l], approximate=False) @ ff_w2[l] + ff_b2[l] + x
        x = rmsnorm(x, norm_out_w)
        return x @ proj_w + proj_b

    def _L2_ffn_ref(x, weight):
        import jax, jax.numpy as jnp
        import numpy as np
        b_weight = jnp.sign(weight)
        return jnp.einsum('bsi,oi->bso', x, b_weight)

    def _L3_xattn_ref(query, key, attn_mask, Wq, bq, Wk, bk, Wv, bv, Wo, bo):
        import jax, jax.numpy as jnp
        import numpy as np
        B, S, H, NH = (2, 256, 128, 16)
        DK = H // NH

        def _split_heads(x):
            b, s, _ = x.shape
            return x.reshape(b, s, NH, DK).transpose(0, 2, 1, 3)
        q = _split_heads(query @ Wq.T + bq)
        k = _split_heads(key @ Wk.T + bk)
        v = _split_heads(key @ Wv.T + bv)
        scores = jnp.einsum('bhqd,bhkd->bhqk', q, k) / jnp.sqrt(jnp.float32(DK))
        scores = jnp.where(attn_mask == 0, jnp.float32(-60000.0), scores)
        weights = jax.nn.softmax(scores, axis=-1)
        out = jnp.einsum('bhqk,bhkd->bhqd', weights, v)
        out = out.transpose(0, 2, 1, 3).reshape(query.shape[0], -1, H)
        return out @ Wo.T + bo

    def _L3_ffn_ref(x, router_w, rg, ru, rd, sg, su, sd):
        import jax, jax.numpy as jnp
        import numpy as np
        B, S, H = (4, 256, 128)
        E, K = (8, 2)
        I_R, I_S = (4 * H, 8 * H)
        CAP_FACTOR = 1.25
        SCALE = 1.0
        b, s, h = x.shape
        T = b * s
        capacity = max(int(CAP_FACTOR * T / E), 1)
        xf = x.reshape(T, h)
        eps = jnp.finfo(x.dtype).eps
        xn = xf * jax.lax.rsqrt(jnp.mean(xf * xf, axis=-1, keepdims=True) + eps)
        logits = xn @ router_w.T
        probs = jax.nn.softmax(logits, axis=-1)
        topk_p, topk_i = jax.lax.top_k(probs, K)
        rw = topk_p / jnp.sum(topk_p, axis=-1, keepdims=True)
        one_hot = jax.nn.one_hot(topk_i, E, dtype=x.dtype)
        mask = one_hot.sum(1)
        wdense = (one_hot * rw[..., None]).sum(1)
        sel = mask.T.astype(bool)
        order = jnp.argsort(~sel, axis=1, stable=True)
        dispatch = order[:, :capacity]
        count = sel.sum(axis=1)
        valid = (jnp.arange(capacity)[None, :] < count[:, None]).astype(x.dtype)
        xg = xf[dispatch]
        gate = jax.nn.silu(jnp.einsum('ech,ehi->eci', xg, rg))
        up = jnp.einsum('ech,ehi->eci', xg, ru)
        eout = jnp.einsum('eci,eih->ech', gate * up, rd)
        w = jnp.take_along_axis(wdense.T, dispatch, axis=1)
        contrib = eout * (w * valid)[..., None]
        routed = jnp.zeros_like(xf).at[dispatch.reshape(-1)].add(contrib.reshape(-1, h))
        shared = jax.nn.silu(x @ sg) * (x @ su) @ sd
        return shared + SCALE * routed.reshape(b, s, h)
    x = x + jnp.tanh(g_xattn[0]) * _L0_xattn_ref(_layernorm(x, axis=-1), ctx_1024, ctx_1024, L0_xattn_Wq, _lenS2)
    x = x + jnp.tanh(g_ffn[0]) * _L0_ffn_ref(_layernorm(x, axis=-1), L0_ffn_Wr, L0_ffn_W1, L0_ffn_b1, L0_ffn_W2, L0_ffn_b2)
    x = x + jnp.tanh(g_xattn[1]) * _L1_xattn_ref(_layernorm(x, axis=-1), ctx_1024, ctx_1024)
    x = x + jnp.tanh(g_ffn[1]) * _L1_ffn_ref(_layernorm(x, axis=-1), L1_ffn_router_W, L1_ffn_router_b, L1_ffn_sW1, L1_ffn_sb1, L1_ffn_sW2, L1_ffn_sb2, L1_ffn_eW1, L1_ffn_eb1, L1_ffn_eW2, L1_ffn_eb2)
    x = x + jnp.tanh(g_xattn[2]) * _L2_xattn_ref(_layernorm(x, axis=-1), ctx_1024, mask_BxS_bf1, L2_xattn_attn_norm_w, L2_xattn_Wq, L2_xattn_Wk, L2_xattn_Wv, L2_xattn_Wo, L2_xattn_bo, L2_xattn_cross_norm_w, L2_xattn_cWq, L2_xattn_cWk, L2_xattn_cWv, L2_xattn_cWo, L2_xattn_cbo, L2_xattn_ff_norm_w, L2_xattn_ff_w1, L2_xattn_ff_b1, L2_xattn_ff_w2, L2_xattn_ff_b2, L2_xattn_norm_out_w, L2_xattn_proj_w, L2_xattn_proj_b)
    x = x + jnp.tanh(g_ffn[2]) * _L2_ffn_ref(_layernorm(x, axis=-1), L2_ffn_weight)
    x = x + jnp.tanh(g_xattn[3]) * _L3_xattn_ref(_layernorm(x, axis=-1), ctx_1024, mask_Bx1xSxS2_if1, L3_xattn_Wq, L3_xattn_bq, L3_xattn_Wk, L3_xattn_bk, L3_xattn_Wv, L3_xattn_bv, L3_xattn_Wo, L3_xattn_bo)
    x = x + jnp.tanh(g_ffn[3]) * _L3_ffn_ref(_layernorm(x, axis=-1), L3_ffn_router_w, L3_ffn_rg, L3_ffn_ru, L3_ffn_rd, L3_ffn_sg, L3_ffn_su, L3_ffn_sd)
    return x

_drawn_inputs = setup_inputs


def setup_inputs(seed=0):
    import zlib

    import numpy as np

    out = dict(_drawn_inputs(seed))
    spreads = {'L0_ffn_b1': (0.0, 0.8),
     'L0_ffn_b2': (0.0, 0.8),
     'L1_ffn_router_b': (0.0, 0.8),
     'L1_ffn_sb1': (0.0, 0.761),
     'L1_ffn_sb2': (0.0, 0.1),
     'L1_ffn_eb1': (0.0, 0.8),
     'L1_ffn_eb2': (0.0, 0.623),
     'L2_xattn_attn_norm_w': (1.0, 0.6),
     'L2_xattn_bo': (0.0, 0.398),
     'L2_xattn_cross_norm_w': (1.0, 0.6),
     'L2_xattn_cbo': (0.0, 0.416),
     'L2_xattn_ff_norm_w': (1.0, 0.6),
     'L2_xattn_ff_b1': (0.0, 0.8),
     'L2_xattn_ff_b2': (0.0, 0.405),
     'L2_xattn_norm_out_w': (1.0, 0.549),
     'L2_xattn_proj_b': (0.0, 0.1)}
    factors = {'g_ffn': 8.0,
     'L0_ffn_Wr': 8.0,
     'L0_ffn_W1': 8.0,
     'L0_ffn_W2': 8.0,
     'L1_ffn_router_W': 4.994,
     'L1_ffn_eW1': 8.0,
     'L1_ffn_eW2': 8.0,
     'L2_xattn_Wq': 8.0,
     'L2_xattn_Wk': 8.0,
     'L2_xattn_Wv': 3.082,
     'L2_xattn_Wo': 3.3,
     'L2_xattn_cWq': 8.0,
     'L2_xattn_cWk': 8.0,
     'L2_xattn_cWv': 4.133,
     'L2_xattn_cWo': 3.922,
     'L2_xattn_ff_w1': 5.215,
     'L2_xattn_ff_w2': 4.785,
     'L3_xattn_Wq': 8.0,
     'L3_xattn_bq': 8.0,
     'L3_xattn_Wk': 8.0,
     'L3_xattn_bk': 8.0,
     'L3_xattn_Wv': 8.0,
     'L3_xattn_bv': 8.0,
     'L3_xattn_Wo': 8.0,
     'L3_xattn_bo': 8.0,
     'L3_ffn_router_w': 8.0,
     'L3_ffn_rg': 8.0,
     'L3_ffn_ru': 8.0,
     'L3_ffn_rd': 8.0,
     'L3_ffn_sg': 8.0,
     'L3_ffn_su': 8.0,
     'L3_ffn_sd': 8.0}
    for name, (base, spread) in spreads.items():
        noise = np.random.default_rng([zlib.crc32(name.encode()), seed]).standard_normal(out[name].shape)
        drawn = base * np.exp(spread * noise) if base else spread * noise
        out[name] = jnp.asarray(drawn.astype(out[name].dtype))
    for name, factor in factors.items():
        out[name] = (out[name] * factor).astype(out[name].dtype)
    return out
```

```python
from contextlib import ExitStack

import concourse.bass as bass
from concourse import mybir
from concourse.alu_op_type import AluOpType as ALU

F32 = mybir.dt.float32
BF16 = mybir.dt.bfloat16
I32 = mybir.dt.int32
U8 = mybir.dt.uint8
ACT = mybir.ActivationFunctionType
AX = mybir.AxisListType

P = 128
B, S, D = 4, 256, 128
HALVES = 2
NB = B // HALVES
QT = S // P
NT = NB * QT
TOK = NT * P
TILES = B * S // P
HEADS = 16
DK = D // HEADS
PAD = 32
GN = D * PAD // DK // P
DH = 64
INNER = HEADS * DH
FT = INNER // P
ROT = 32
FF = 512
E1, K1 = 15, 3
E3, K3 = 8, 2
CAP = int(1.25 * B * S / E3)
MASKED = -1.0e30


SEMS = 24


class Core:

    def __init__(self):
        self.stage = 0

    def semaphores(self, nc, names):
        self.stage += 1
        before = self.sems[(self.stage + 1) % 2]
        nc.gpsimd.sem_clear(range(before[0].num, before[-1].num + 1))
        return self.sems[self.stage % 2][:len(names)]


def allocate(nc, ctx):
    c = Core()
    c.sems = [[nc.alloc_semaphore(f"set{j}_{i}") for i in range(SEMS)] for j in range(2)]

    def sb(name, shape, dt=F32):
        return ctx.enter_context(nc.sbuf_tensor(name, shape, dt))

    c.ident = sb("ident", [P, P])
    c.ident_bf = sb("ident_bf", [P, P], BF16)
    c.ones_bf = sb("ones_bf", [P, P], BF16)
    c.tri_bf = sb("tri_bf", [P, P], BF16)
    c.iota = sb("iota", [P, S])
    c.rope = sb("rope", [P, QT, 2 * ROT])
    c.gate = sb("gate", [P, 8])
    c.x = sb("x_res", [P, NT, D])
    c.u = sb("u_res", [P, NT, D])
    c.ub = sb("u_biased", [P, NT, D])
    c.y = sb("y_norm", [P, TILES, D])
    c.xT = sb("xT", [P, TOK])
    c.ctx = sb("ctx_tok", [P, NT, D])
    c.ctxT = sb("ctxT", [P, TOK])
    c.stats = sb("stats", [P, TILES, 6])
    c.mv = sb("mv", [P, TILES, 2])
    c.rstd = sb("rstd", [P, TILES])
    c.msq = sb("msq", [P, TILES])
    c.newton = sb("newton", [P, TILES])
    c.qT = sb("qT", [P, FT, TOK])
    c.kT = sb("kT", [P, FT, TOK])
    c.v = sb("v_tok", [P, NT, INNER])
    c.oT = sb("oT", [P, FT, TOK])
    c.roped = sb("roped", [P, 2, INNER])
    c.rot = sb("rot_tmp", [P, HEADS, ROT])
    c.probs = sb("probs", [P, 3, QT, S])
    c.probsT = sb("probsT", [P, 2, 2 * S])
    c.mx = sb("row_max", [P, 3, QT])
    c.nmx = sb("neg_max", [P, 3, QT])
    c.rsum = sb("row_sum", [P, 3, QT])
    c.rinv = sb("row_inv", [P, 3, QT])
    c.len_i = sb("len_i", [P, NB], I32)
    c.len_f = sb("len_f", [P, NB])
    c.mask_u8 = sb("mask_u8", [P, NB, S], U8)
    c.mask_i32 = sb("mask_i32", [P, NT, S], I32)
    c.m_len = sb("m_len", [P, NB, S], BF16)
    c.m_causal = sb("m_causal", [P, QT, S], BF16)
    c.m_key = sb("m_key", [P, NB, S], BF16)
    c.m_full = sb("m_full", [P, NT, S], BF16)
    c.raw = sb("raw_w", [P, 8, P])
    c.w0 = sb("w0_pad", [P, GN * P])
    c.wr0 = sb("wr0", [P, 8])
    c.w1_0 = sb("w1_0", [P, FF])
    c.b1_0 = sb("b1_0", [P, FF // P])
    c.w2_0 = sb("w2_0", [P, FF // P, D])
    c.b2_0 = sb("b2_0", [P, D])
    c.wr1 = sb("wr1", [P, E1])
    c.br1 = sb("br1", [P, E1])
    c.ew1 = sb("ew1", [P, E1 + 1, D])
    c.eb1 = sb("eb1", [P, E1 + 1])
    c.ew2 = sb("ew2", [P, E1 + 1, D])
    c.eb2 = sb("eb2", [E1 + 1, D])
    c.wa = sb("w_attn", [P, 2, 4 * INNER])
    c.wff1 = sb("wff1", [P, FF])
    c.wff2 = sb("wff2", [P, FF // P, D])
    c.bff1 = sb("bff1", [P, FF // P])
    c.bff2 = sb("bff2", [P, D])
    c.bo2 = sb("bo2", [P, 4, D])
    c.nw = sb("norm_w", [P, 7])
    c.proj = sb("proj", [P, D])
    c.projb = sb("projb", [P, D])
    c.signT = sb("signT", [P, D])
    c.neg = sb("neg", [P, D])
    c.w3 = sb("w3_pad", [P, 3, GN * P])
    c.b3 = sb("b3_pad", [P, 3, GN])
    c.wo3 = sb("wo3_pad", [P, GN, D])
    c.bo3 = sb("bo3", [P, D])
    c.lg = sb("logits", [P, TILES, 16])
    c.ex = sb("router_exp", [P, TILES, 16])
    c.rm = sb("router_max", [P, TILES])
    c.rs = sb("router_sum", [P, TILES])
    c.pr = sb("router_probs", [P, TILES, 16])
    c.top = sb("router_top", [P, TILES, 8])
    c.rest = sb("router_rest", [P, TILES, 16])
    c.sel = sb("router_sel", [P, TILES, 16])
    c.cw = sb("router_w", [P, TILES, 16])
    c.cwT = sb("router_wT", [16, TOK])
    c.acc = sb("acc", [P, NT, D])
    c.wr3 = sb("wr3", [P, E3])
    c.selb = sb("sel_bf", [P, TILES, E3], BF16)
    c.before = sb("sel_before", [P, TILES, E3], BF16)
    c.x3 = sb("x3", [P, TILES, D])
    c.ps = [ctx.enter_context(nc.psum_tensor(f"bank{i}", [P, 512], F32)) for i in range(8)]
    return c


class Chain:

    def __init__(self, eng, sem):
        self.eng, self.sem, self.n = eng, sem, 0

    def mark(self, ins):
        self.n += 1
        ins.then_inc(self.sem, 1)

    def link(self, ins):
        self.mark(ins)
        self.eng.wait_ge(self.sem, self.n)



def stage_setup(nc, c, A):
    with ExitStack() as ctx:
        loaded, consts, tables, wt, wt_free, chain_v, chain_g, bias_loaded = c.semaphores(nc, (
                "su_loaded", "su_consts", "su_zeroed", "su_transposed", "su_bank_free", "su_dve", "su_pool", "su_bias"))
        loads = [0]
        block = ctx.enter_context(nc.Block())

        @block.sync
        def _(sp):
            def load(dst, src):
                sp.dma_start(dst, src).then_inc(loaded, 16)
                loads[0] += 16
            raw = c.raw
            load(raw[:, 0, :], A["L0_xattn_Wq"])
            load(raw[:, 1, :], A["L3_xattn_Wq"])
            load(raw[:, 2, :], A["L3_xattn_Wk"])
            load(raw[:, 3, :], A["L3_xattn_Wv"])
            load(raw[:, 4, :], A["L3_xattn_Wo"])
            load(raw[:, 5, :], A["L2_ffn_weight"])
            load(raw[0:8, 6, :], A["L0_ffn_Wr"])
            load(raw[0:8, 7, :], A["L3_ffn_router_w"])
            load(c.gate[:, 0:4], A["g_xattn"].partition_broadcast(P))
            load(c.gate[:, 4:8], A["g_ffn"].partition_broadcast(P))
            load(c.rope[:, :, :], A["rope_table"].rearrange("(t p) n -> p t n", p=P))
            load(c.w1_0[:, :], A["L0_ffn_W1"][7])
            load(c.b1_0[:, :], A["L0_ffn_b1"][7].rearrange("(t p) -> p t", p=P))
            load(c.w2_0[:, :, :], A["L0_ffn_W2"][7].rearrange("(t p) n -> p t n", p=P))
            load(c.b2_0[:, :], A["L0_ffn_b2"][7].partition_broadcast(P))
            load(c.wr1[:, :], A["L1_ffn_router_W"])
            load(c.br1[:, :], A["L1_ffn_router_b"].partition_broadcast(P))
            load(c.ew1[:, 0:E1, :], A["L1_ffn_eW1"].rearrange("e p n -> p e n"))
            load(c.ew1[:, E1, :], A["L1_ffn_sW1"])
            load(c.eb1[:, 0:E1], A["L1_ffn_eb1"].rearrange("e p -> p e"))
            load(c.eb1[:, E1:E1 + 1], A["L1_ffn_sb1"].rearrange("(p a) -> p a", a=1))
            load(c.ew2[:, 0:E1, :], A["L1_ffn_eW2"].rearrange("e p n -> p e n"))
            load(c.ew2[:, E1, :], A["L1_ffn_sW2"])
            load(c.eb2[0:E1, :], A["L1_ffn_eb2"])
            load(c.eb2[E1:E1 + 1, :], A["L1_ffn_sb2"].rearrange("(a n) -> a n", a=1))
            for l in range(2):
                load(c.bo2[:, 2 * l, :], A["L2_xattn_bo"][l].partition_broadcast(P))
                load(c.bo2[:, 2 * l + 1, :], A["L2_xattn_cbo"][l].partition_broadcast(P))
                for j, n in enumerate(("attn_norm_w", "cross_norm_w", "ff_norm_w")):
                    load(c.nw[:, 3 * l + j:3 * l + j + 1], A["L2_xattn_" + n][l].rearrange("(p a) -> p a", a=1))
            load(c.nw[:, 6:7], A["L2_xattn_norm_out_w"].rearrange("(p a) -> p a", a=1))
            load(c.proj[:, :], A["L2_xattn_proj_w"])
            load(c.projb[:, :], A["L2_xattn_proj_b"].partition_broadcast(P))
            load(c.bo3[:, :], A["L3_xattn_bo"].partition_broadcast(P))
            sp.wait_ge(tables, 1)
            for j, n in enumerate(("bq", "bk", "bv")):
                for h in range(4):
                    sp.dma_start(c.b3[PAD * h:PAD * h + DK, j, :],
                                 A["L3_xattn_" + n].rearrange("(g h d) -> h d g", h=4, d=DK)[h]).then_inc(bias_loaded, 16)
            sp.wait_ge(loaded, loads[0])
            sp.wait_ge(bias_loaded, 12 * 16)

        @block.gpsimd
        def _(pool):
            g = Chain(pool, chain_g)
            pool.memset(c.b3[:, :, :], 0.0).then_inc(tables, 1)
            g.mark(pool.memset(c.ident[:, :], 0.0))
            g.mark(pool.memset(c.ident_bf[:, :], 0.0))
            g.mark(pool.memset(c.tri_bf[:, :], 1.0))
            g.mark(pool.memset(c.m_causal[:, :, :], 0.0))
            g.link(pool.memset(c.ones_bf[:, :], 1.0))
            for m in (c.ident, c.ident_bf):
                pool.affine_select(out=m[:, :], in_=m[:, :], compare_op=ALU.not_equal, fill=1.0, base=0,
                                   pattern=[[-1, P]], channel_multiplier=1).then_inc(consts, 1)
            pool.affine_select(out=c.tri_bf[:, :], in_=c.tri_bf[:, :], compare_op=ALU.is_ge, fill=0.0, base=0,
                               pattern=[[1, P]], channel_multiplier=-1)
            pool.affine_select(out=c.m_causal[:, :, :], in_=c.m_causal[:, :, :], compare_op=ALU.is_ge, fill=MASKED,
                               base=0, pattern=[[P, QT], [-1, S]], channel_multiplier=1)
            pool.iota(c.iota[:, :], pattern=[[1, S]], base=0, channel_multiplier=0,
                      allow_small_or_imprecise_dtypes=True)

        @block.tensor
        def _(pe):
            pe.wait_ge(consts, 2)
            pe.wait_ge(loaded, loads[0])
            for j in range(8):
                n = P if j < 6 else 8
                pe.transpose(c.ps[j][:, 0:n], c.raw[0:n, j, :], c.ident[0:n, 0:n]).then_inc(wt, 1)
            pe.wait_ge(wt_free, 1)
            for g in range(GN):
                pe.transpose(c.ps[4][:, g * P:(g + 1) * P], c.oT[:, 0, g * P:(g + 1) * P],
                             c.ident[:, :]).then_inc(wt, 1)

        @block.vector
        def _(dve):
            v = Chain(dve, chain_v)
            v.mark(dve.memset(c.w0[:, :], 0.0))
            v.mark(dve.memset(c.w3[:, :, :], 0.0))
            v.link(dve.memset(c.oT[:, 0, :], 0.0))
            dve.wait_ge(loaded, loads[0])

            def spread(dst, src):
                return dve.tensor_copy(dst.rearrange("p (h d) -> p h d", d=PAD)[:, :, 0:DK],
                                       src.rearrange("p (h d) -> p h d", d=DK))
            spread(c.oT[:, 0, :], c.raw[:, 4, :]).then_inc(wt_free, 1)
            dve.wait_ge(wt, 8)
            spread(c.w0[:, :], c.ps[0][:, 0:P])
            for j in range(3):
                spread(c.w3[:, j, :], c.ps[1 + j][:, 0:P])
            v.mark(dve.tensor_scalar(c.signT[:, :], c.ps[5][:, 0:P], 0.0, None, ALU.is_gt))
            v.link(dve.tensor_scalar(c.neg[:, :], c.ps[5][:, 0:P], 0.0, None, ALU.is_lt))
            dve.tensor_tensor(c.signT[:, :], c.signT[:, :], c.neg[:, :], ALU.subtract)
            dve.tensor_copy(c.wr0[:, :], c.ps[6][:, 0:8])
            dve.tensor_copy(c.wr3[:, :], c.ps[7][:, 0:8])
            dve.wait_ge(wt, 8 + GN)
            dve.tensor_copy(c.wo3[:, :, :], c.ps[4][:, 0:GN * P].rearrange("p (g n) -> p g n", g=GN))

        @block.scalar
        def _(act):
            act.wait_ge(loaded, loads[0])
            act.activation(c.gate[:, :], c.gate[:, :], ACT.Tanh)


def stage_load(nc, c, A, half):
    with ExitStack() as ctx:
        loaded, loaded_ctx, tr, chain_v, lenf = c.semaphores(nc, (
            "ld_masks", "ld_ctx", "ld_transposed", "ld_dve", "ld_len"))
        block = ctx.enter_context(nc.Block())

        @block.sync
        def _(sp):
            def rows(a):
                return a.rearrange("b (t p) f -> p (b t) f", p=P)[:, bass.ds(half * NT, NT), :]
            sp.dma_start(c.ctx[:, :, :], rows(A["ctx_1024"])).then_inc(loaded_ctx, 16)
            sp.dma_start(c.x[:, :, :], rows(A["x"])).then_inc(loaded, 16)
            sp.dma_start(c.len_i[:, :], A["_lenS2"][bass.ds(half * NB, NB)].partition_broadcast(P)).then_inc(loaded, 16)
            sp.dma_start(c.mask_u8[:, :, :],
                         A["mask_BxS_bf1"][bass.ds(half * NB, NB), :].partition_broadcast(P)).then_inc(loaded, 16)
            sp.dma_start(c.mask_i32[:, :, :],
                         A["mask_Bx1xSxS2_if1"].rearrange("b a (t p) k -> p (b a t) k", p=P)[:, bass.ds(half * NT, NT), :]
                         ).then_inc(loaded, 16)
            sp.wait_ge(loaded, 64)

        @block.tensor
        def _(pe):
            pe.wait_ge(loaded_ctx, 16)
            for t in range(NT):
                pe.transpose(c.ps[0][:, t * P:(t + 1) * P], c.ctx[:, t, :], c.ident[:, :]).then_inc(tr, 1)

        @block.scalar
        def _(act):
            act.wait_ge(tr, NT)
            act.copy(c.ctxT[:, :], c.ps[0][:, :])

        @block.vector
        def _(dve):
            dve.wait_ge(loaded, 64)
            dve.tensor_copy(c.len_f[:, :], c.len_i[:, :]).then_inc(lenf, 1)
            dve.wait_ge(lenf, 1)
            for b in range(NB):
                dve.tensor_scalar(c.m_len[:, b, :], c.iota[:, :], c.len_f[:, b:b + 1], MASKED, ALU.is_ge, ALU.mult)
            dve.tensor_scalar(c.m_key[:, :, :], c.mask_u8[:, :, :], 0.0, MASKED, ALU.is_equal, ALU.mult)
            dve.tensor_scalar(c.m_full[:, :, :], c.mask_i32[:, :, :], 0.0, MASKED, ALU.is_equal, ALU.mult)



def rsqrt_steps(dve, v, c, n):
    ms, r, t = c.msq[:, 0:n], c.rstd[:, 0:n], c.newton[:, 0:n]
    v.link(dve.tensor_scalar(t.bitcast(I32), ms.bitcast(I32), 1, None, ALU.logical_shift_right))
    v.link(dve.tensor_scalar(r.bitcast(I32), t.bitcast(I32), -1.0, float(0x5F3759DF), ALU.mult, ALU.add))
    for _ in range(3):
        v.link(dve.tensor_tensor(t, r, r, ALU.mult))
        v.link(dve.scalar_tensor_tensor(out=t, in0=t, scalar=-0.5, in1=ms, op0=ALU.mult, op1=ALU.mult))
        v.link(dve.scalar_tensor_tensor(out=r, in0=t, scalar=1.5, in1=r, op0=ALU.add, op1=ALU.mult))


def norm_steps(dve, v, c, src, dst, n, kind, ready):
    for t in range(n):
        v.mark(dve.bn_stats(c.stats[:, t, :], src[:, t, :]))
    dve.wait_ge(v.sem, v.n)
    for t in range(n):
        v.mark(dve.bn_aggr(c.mv[:, t, :], c.stats[:, t, :]))
    dve.wait_ge(v.sem, v.n)
    mean, var, ms = c.mv[:, 0:n, 0], c.mv[:, 0:n, 1], c.msq[:, 0:n]
    if kind == "layer":
        v.link(dve.tensor_scalar(ms, var, 1e-5, None, ALU.add))
    else:
        v.link(dve.tensor_tensor(ms, mean, mean, ALU.mult))
        v.link(dve.tensor_tensor(ms, ms, var, ALU.add))
        if kind == "rms":
            v.link(dve.tensor_scalar(ms, ms, 1e-16, None, ALU.max))
        else:
            v.link(dve.tensor_scalar(ms, ms, 1.1920929e-07, None, ALU.add))
    rsqrt_steps(dve, v, c, n)
    for t in range(n):
        if kind == "layer":
            dve.tensor_scalar(dst[:, t, :], src[:, t, :], c.mv[:, t, 0:1], c.rstd[:, t:t + 1],
                              ALU.subtract, ALU.mult).then_inc(ready, 1)
        else:
            dve.tensor_scalar(dst[:, t, :], src[:, t, :], c.rstd[:, t:t + 1], None, ALU.mult).then_inc(ready, 1)


def stage_norm(nc, c, src, kind, weight=None, inner=False):
    with ExitStack() as ctx:
        ready, ready_u, tr, chain_v = c.semaphores(nc, (
            "nm_ready", "nm_inner", "nm_transposed", "nm_dve"))
        block = ctx.enter_context(nc.Block())

        @block.vector
        def _(dve):
            v = Chain(dve, chain_v)
            s = src
            if inner:
                norm_steps(dve, v, c, src, c.u, NT, "layer", ready_u)
                dve.wait_ge(ready_u, NT)
                s = c.u
            norm_steps(dve, v, c, s, c.y, NT, kind, ready)

        @block.tensor
        def _(pe):
            for t in range(NT):
                pe.wait_ge(ready, t + 1)
                pe.transpose(c.ps[t // 2][:, (t % 2) * P:(t % 2 + 1) * P], c.y[:, t, :], c.ident[:, :]).then_inc(tr, 1)

        @block.scalar
        def _(act):
            for j in range(NT // 2):
                act.wait_ge(tr, 2 * j + 2)
                act.activation(c.xT[:, j * 2 * P:(j + 1) * 2 * P], c.ps[j][:, 0:2 * P], ACT.Copy,
                               scale=1.0 if weight is None else weight)



def stage_narrow_qkv(nc, c, wq, wk, wv, bias):
    with ExitStack() as ctx:
        done, freed = c.semaphores(nc, ("nq_done", "nq_freed"))
        block = ctx.enter_context(nc.Block())
        jobs = [(c.qT, wq, c.xT, g) for g in range(GN)] + [(c.kT, wk, c.ctxT, g) for g in range(GN)]

        @block.tensor
        def _(pe):
            for i, (_, w, x, g) in enumerate(jobs):
                pe.matmul(c.ps[i][:, :], w[:, g * P:(g + 1) * P], x[:, :], start=True, stop=True).then_inc(done, 1)
            for t in range(NT):
                pe.wait_ge(freed, t + 1)
                pe.matmul(c.ps[t][:, :], c.ctxT[:, t * P:(t + 1) * P], wv, start=True, stop=True).then_inc(done, 1)

        @block.scalar
        def _(act):
            for i, (dst, _, _, g) in enumerate(jobs):
                act.wait_ge(done, i + 1)
                b = 0.0 if bias is None else bias[:, i // GN, g:g + 1]
                act.activation(dst[:, g, :], c.ps[i][:, :], ACT.Identity, bias=b).then_inc(freed, 1)
            for t in range(NT):
                act.wait_ge(done, len(jobs) + t + 1)
                act.activation(c.v[:, t, 0:GN * P], c.ps[t][:, :], ACT.Copy)


def stage_wide_qkv(nc, c, w, kv):
    wq, wk, wv = (w[:, j * INNER:(j + 1) * INNER] for j in range(3))
    with ExitStack() as ctx:
        proj, passed, vdone, roped, rchain, tr, tfree = c.semaphores(nc, (
            "wq_proj", "wq_passed", "wq_vcopied", "wq_roped", "wq_dve", "wq_transposed", "wq_tfree"))
        block = ctx.enter_context(nc.Block())
        units = [(j, t) for t in range(NT) for j in range(2)]
        n = len(units)

        @block.tensor
        def _(pe):
            for i in range(n + 1):
                if i < n:
                    j, t = units[i]
                    x = kv if j else c.xT
                    if i >= 2:
                        pe.wait_ge(roped, i - 1)
                        pe.wait_ge(passed, i - 1)
                    for m in range(2):
                        mm = pe.matmul(c.ps[2 * (i % 2) + m][:, :], x[:, t * P:(t + 1) * P],
                                       (wk if j else wq)[:, m * 512:(m + 1) * 512], start=True, stop=True)
                    mm.then_inc(proj, 1)
                    if j:
                        if t:
                            pe.wait_ge(vdone, t)
                        for m in range(2):
                            mm = pe.matmul(c.ps[6 + m][:, :], kv[:, t * P:(t + 1) * P], wv[:, m * 512:(m + 1) * 512],
                                           start=True, stop=True)
                        mm.then_inc(proj, 1)
                if i >= 1:
                    k = i - 1
                    pe.wait_ge(roped, k + 1)
                    pe.wait_ge(passed, k + 1)
                    for m in range(2):
                        if 2 * k + m >= 2:
                            pe.wait_ge(tfree, 2 * k + m - 1)
                        for f in range(4):
                            mm = pe.transpose(c.ps[4 + m][:, f * P:(f + 1) * P],
                                              c.roped[:, k % 2, (4 * m + f) * P:(4 * m + f + 1) * P], c.ident[:, :])
                        mm.then_inc(tr, 1)

        @block.scalar
        def _(act):
            def transposed_out(k):
                j, t = units[k]
                for m in range(2):
                    act.wait_ge(tr, 2 * k + m + 1)
                    act.copy((c.kT if j else c.qT)[:, 4 * m:4 * m + 4, t * P:(t + 1) * P],
                             c.ps[4 + m][:, :].rearrange("p (f n) -> p f n", f=4)).then_inc(tfree, 1)
            for i in range(n + 1):
                if i < n:
                    j, t = units[i]
                    act.wait_ge(proj, i + t + 1)
                    if i >= 2:
                        act.wait_ge(tr, 2 * i - 2)
                    act.wait_ge(roped, i + 1)
                    for m in range(2):
                        cp = act.copy(c.roped[:, i % 2, m * 512:(m + 1) * 512]
                                      .rearrange("p (h d) -> p h d", d=DH)[:, :, ROT:DH],
                                      c.ps[2 * (i % 2) + m][:, :].rearrange("p (h d) -> p h d", d=DH)[:, :, ROT:DH])
                    cp.then_inc(passed, 1)
                    if j:
                        act.wait_ge(proj, i + t + 2)
                        for m in range(2):
                            cp = act.copy(c.v[:, t, m * 512:(m + 1) * 512], c.ps[6 + m][:, :])
                        cp.then_inc(vdone, 1)
                if i >= 1:
                    transposed_out(i - 1)

        @block.vector
        def _(dve):
            v = Chain(dve, rchain)
            half = ROT // 2
            for i, (j, t) in enumerate(units):
                dve.wait_ge(proj, i + t + 1)
                if i >= 2:
                    dve.wait_ge(tr, 2 * i - 2)
                if i >= 1:
                    dve.wait_ge(roped, i)
                cos = c.rope[:, t % QT, 0:ROT]
                sin = c.rope[:, t % QT, ROT:2 * ROT]

                def over_heads(a):
                    return a.rearrange("p (h d) -> p h d", h=1).to_broadcast([P, HEADS // 2, a.shape[-1]])
                for m in range(2):
                    src = c.ps[2 * (i % 2) + m][:, :].rearrange("p (h d) -> p h d", d=DH)
                    dst = c.roped[:, i % 2, m * 512:(m + 1) * 512].rearrange("p (h d) -> p h d", d=DH)
                    tmp = c.rot[:, m * 8:(m + 1) * 8, :]
                    v.mark(dve.tensor_tensor(dst[:, :, 0:ROT], src[:, :, 0:ROT], over_heads(cos), ALU.mult))
                    v.mark(dve.tensor_tensor(tmp[:, :, 0:half], src[:, :, half:ROT], over_heads(sin[:, 0:half]),
                                             ALU.mult))
                    v.mark(dve.tensor_tensor(tmp[:, :, half:ROT], src[:, :, 0:half], over_heads(sin[:, half:ROT]),
                                             ALU.mult))
                dve.wait_ge(v.sem, v.n)
                full = c.roped[:, i % 2, :].rearrange("p (h d) -> p h d", d=DH)[:, :, 0:ROT]
                dve.tensor_tensor(full, full, c.rot[:, :, :], ALU.add).then_inc(roped, 1)


def stage_heads(nc, c, units, per_group, scale, out_bias=None):
    n = len(units)
    with ExitStack() as ctx:
        scored, mchain, biased, exped, rchain, normed, turned, copied, mixed, out_free = c.semaphores(nc, (
                "hd_scored", "hd_max", "hd_negmax", "hd_exp", "hd_rinv", "hd_normed", "hd_turned", "hd_copied",
                "hd_mixed", "hd_outfree"))
        block = ctx.enter_context(nc.Block())
        scores = [c.ps[i] for i in range(3)]
        turns = [c.ps[3 + i] for i in range(2)]
        outs = [c.ps[5 + i] for i in range(2)]

        @block.tensor
        def _(pe):
            for i in range(n + 3):
                if i < n:
                    q, k, _, _, mask, _ = units[i]
                    if i >= 3:
                        pe.wait_ge(exped, 2 * (i - 2))
                    for t in range(QT):
                        o = scores[i % 3][:, t * S:(t + 1) * S]
                        mm = pe.matmul(o, q(t), k, start=True, stop=mask is None)
                        if mask is not None:
                            mm = pe.matmul(o, c.ident_bf[:, :], mask(t), start=False, stop=True)
                    mm.then_inc(scored, 1)
                if 2 <= i < n + 2:
                    j = i - 2
                    pe.wait_ge(normed, QT * (j + 1))
                    if j >= 2:
                        pe.wait_ge(copied, j - 1)
                    for kt in range(QT):
                        for t in range(QT):
                            mm = pe.transpose(turns[j % 2][:, kt * S + t * P:kt * S + (t + 1) * P],
                                              c.probs[:, j % 3, t, kt * P:(kt + 1) * P], c.ident[:, :])
                    mm.then_inc(turned, 1)
                if i >= 3:
                    j = i - 3
                    _, _, v, rows, _, _ = units[j]
                    g = j // per_group
                    pe.wait_ge(copied, j + 1)
                    if j % per_group == 0 and g >= 2:
                        pe.wait_ge(out_free, g - 1)
                    for kt in range(QT):
                        mm = pe.matmul(outs[g % 2][rows, 0:S], v(kt), c.probsT[:, j % 2, kt * S:(kt + 1) * S],
                                       start=(kt == 0), stop=(kt == QT - 1))
                    mm.then_inc(mixed, 1)

        @block.vector
        def _(dve):
            r = Chain(dve, rchain)
            for i in range(n + 4):
                if i < n:
                    dve.wait_ge(scored, i + 1)
                    if i >= 3:
                        dve.wait_ge(exped, 2 * (i - 2))
                    dve.tensor_reduce(c.mx[:, i % 3, :], scores[i % 3][:, :].rearrange("p (t k) -> p t k", t=QT),
                                      AX.X, ALU.max).then_inc(mchain, 1)
                    dve.wait_ge(mchain, i + 1)
                    dve.tensor_scalar(c.nmx[:, i % 3, :], c.mx[:, i % 3, :], -scale, None, ALU.mult).then_inc(biased, 1)
                if 1 <= i < n + 1:
                    j = i - 1
                    dve.wait_ge(exped, 2 * (j + 1))
                    r.link(dve.reciprocal(c.rinv[:, j % 3, :], c.rsum[:, j % 3, :]))
                    for t in range(QT):
                        dve.tensor_scalar(c.probs[:, j % 3, t, :], c.probs[:, j % 3, t, :], c.rinv[:, j % 3, t:t + 1],
                                          None, ALU.mult).then_inc(normed, 1)
                if i >= 4 and (i - 4) % per_group == per_group - 1:
                    j = i - 4
                    dve.wait_ge(mixed, j + 1)
                    dst = units[j][5]
                    src = outs[j // per_group % 2][:, 0:S]
                    if out_bias is None:
                        dve.tensor_copy(dst, src).then_inc(out_free, 1)
                    else:
                        dve.tensor_scalar(dst, src, out_bias(j // per_group), None, ALU.add).then_inc(out_free, 1)

        @block.scalar
        def _(act):
            for i in range(n + 2):
                if i < n:
                    act.wait_ge(biased, i + 1)
                    if i >= 3:
                        act.wait_ge(turned, i - 2)
                    for t in range(QT):
                        act.activation(c.probs[:, i % 3, t, :], scores[i % 3][:, t * S:(t + 1) * S], ACT.Exp,
                                       bias=c.nmx[:, i % 3, t:t + 1], scale=scale,
                                       accum_out=c.rsum[:, i % 3, t:t + 1]).then_inc(exped, 1)
                if i >= 2:
                    j = i - 2
                    act.wait_ge(turned, j + 1)
                    if j >= 2:
                        act.wait_ge(mixed, j - 1)
                    act.copy(c.probsT[:, j % 2, :], turns[j % 2][:, :]).then_inc(copied, 1)


def narrow_units(c, mask):
    def unit(b, h):
        g, r = h // 4, PAD * (h % 4)
        return (lambda t: c.qT[r:r + PAD, g, (b * QT + t) * P:(b * QT + t + 1) * P],
                c.kT[r:r + PAD, g, b * S:(b + 1) * S],
                lambda kt: c.v[:, b * QT + kt, g * P + r:g * P + r + PAD],
                slice(r, r + PAD), lambda t: mask(b, t), c.oT[:, g, b * S:(b + 1) * S])
    return [unit(b, h) for b in range(NB) for h in range(HEADS)]


def wide_units(c, mask):
    def unit(b, h):
        g, r = h // 2, DH * (h % 2)
        return (lambda t: c.qT[r:r + DH, g, (b * QT + t) * P:(b * QT + t + 1) * P],
                c.kT[r:r + DH, g, b * S:(b + 1) * S],
                lambda kt: c.v[:, b * QT + kt, h * DH:(h + 1) * DH],
                slice(r, r + DH), mask and (lambda t: mask(b, t)), c.oT[:, g, b * S:(b + 1) * S])
    return [unit(b, h) for b in range(NB) for h in range(HEADS)]


def single_units(c):
    def unit(b):
        return (lambda t: c.xT[:, (b * QT + t) * P:(b * QT + t + 1) * P], c.ctxT[:, b * S:(b + 1) * S],
                lambda kt: c.ctx[:, b * QT + kt, :], slice(0, P), lambda t: c.m_causal[:, t, :],
                c.oT[:, 0, b * S:(b + 1) * S])
    return [unit(b) for b in range(NB)]


def stage_turn_back(nc, c, groups, width, gate):
    with ExitStack() as ctx:
        tr, freed = c.semaphores(nc, ("tb_turned", "tb_freed"))
        block = ctx.enter_context(nc.Block())

        @block.tensor
        def _(pe):
            for t in range(NT):
                for g in range(groups):
                    mm = pe.transpose(c.ps[t][:, g * P:(g + 1) * P], c.oT[:, g, t * P:(t + 1) * P], c.ident[:, :])
                mm.then_inc(tr, 1)

        @block.vector
        def _(dve):
            for t in range(NT):
                dve.wait_ge(tr, t + 1)
                src = c.ps[t][:, 0:groups * P]
                dst = c.x[:, t, :]
                if width < P:
                    src = src.rearrange("p (h d) -> p h d", d=PAD)[:, :, 0:width]
                    dst = dst.rearrange("p (h d) -> p h d", d=width)
                dve.scalar_tensor_tensor(out=dst, in0=src, scalar=gate, in1=dst, op0=ALU.mult, op1=ALU.add)


def stage_out(nc, c, w, tiles, res, bias, gate):
    with ExitStack() as ctx:
        done, chain_v = c.semaphores(nc, ("op_done", "op_dve"))
        block = ctx.enter_context(nc.Block())

        @block.tensor
        def _(pe):
            for t in range(NT):
                for f in range(tiles):
                    mm = pe.matmul(c.ps[t][:, 0:D], c.oT[:, f, t * P:(t + 1) * P], w[:, f, :],
                                   start=(f == 0), stop=(f == tiles - 1))
                mm.then_inc(done, 1)

        @block.vector
        def _(dve):
            add_residual(dve, Chain(dve, chain_v), c, done, res, bias, gate)


def add_residual(dve, v, c, done, res, bias, gate):
    for t in range(NT):
        dve.wait_ge(done, t + 1)
        v.link(dve.tensor_tensor(c.acc[:, t, :], c.ps[t][:, 0:D], bias, ALU.add))
        if gate is None:
            dve.tensor_tensor(res[:, t, :], c.acc[:, t, :], res[:, t, :], ALU.add)
        else:
            dve.scalar_tensor_tensor(out=res[:, t, :], in0=c.acc[:, t, :], scalar=gate(t), in1=res[:, t, :],
                                     op0=ALU.mult, op1=ALU.add)



def stage_gelu_ffn(nc, c, w1, b1, w2, b2, res, gate, loads=None):
    nf = FF // P
    with ExitStack() as ctx:
        loaded, up, act_done, done, chain_v = c.semaphores(nc, (
            "ff_loaded", "ff_up", "ff_gelu", "ff_done", "ff_dve"))
        block = ctx.enter_context(nc.Block())

        if loads:
            @block.sync
            def _(sp):
                for dst, src in loads:
                    sp.dma_start(dst, src).then_inc(loaded, 16)

        @block.tensor
        def _(pe):
            if loads:
                pe.wait_ge(loaded, 16 * len(loads))
            for f in range(nf):
                pe.matmul(c.ps[4 + f][:, :], w1[:, f * P:(f + 1) * P], c.xT[:, :], start=True, stop=True).then_inc(up, 1)
            for f in range(nf):
                pe.wait_ge(act_done, f + 1)
                for t in range(NT):
                    mm = pe.matmul(c.ps[t][:, 0:D], c.qT[:, f, t * P:(t + 1) * P], w2[:, f, :],
                                   start=(f == 0), stop=(f == nf - 1))
                    if f == nf - 1:
                        mm.then_inc(done, 1)

        @block.scalar
        def _(act):
            if loads:
                act.wait_ge(loaded, 16 * len(loads))
            for f in range(nf):
                act.wait_ge(up, f + 1)
                act.activation(c.qT[:, f, :], c.ps[4 + f][:, :], ACT.Gelu, bias=b1[:, f:f + 1]).then_inc(act_done, 1)

        @block.vector
        def _(dve):
            if loads:
                dve.wait_ge(loaded, 16 * len(loads))
            add_residual(dve, Chain(dve, chain_v), c, done, res, b2, gate)


def softmax_steps(dve, v, c, n, e, logits_to, exped):
    lg, ex, pr = (a[:, 0:n, 0:e] for a in (c.lg, c.ex, c.pr))

    def wide(a):
        return a[:, 0:n].rearrange("p (n a) -> p n a", a=1).to_broadcast([P, n, e])
    v.link(dve.tensor_reduce(c.rm[:, 0:n], lg, AX.X, ALU.max))
    dve.tensor_tensor(lg, lg, wide(c.rm), ALU.subtract).then_inc(logits_to, 1)
    dve.wait_ge(exped, 1)
    v.link(dve.tensor_reduce(c.rs[:, 0:n], ex, AX.X, ALU.add))
    v.link(dve.reciprocal(c.rs[:, 0:n], c.rs[:, 0:n]))
    v.link(dve.tensor_tensor(pr, ex, wide(c.rs), ALU.mult))


def stage_router0(nc, c):
    e = 8
    with ExitStack() as ctx:
        done, centred, exped, chain_v = c.semaphores(nc, (
            "r0_done", "r0_centred", "r0_exp", "r0_dve"))
        block = ctx.enter_context(nc.Block())

        @block.tensor
        def _(pe):
            for t in range(NT):
                mm = pe.matmul(c.ps[0][:, t * 16:t * 16 + e], c.xT[:, t * P:(t + 1) * P], c.wr0[:, :], start=True, stop=True)
            mm.then_inc(done, 1)

        @block.scalar
        def _(act):
            act.wait_ge(centred, 1)
            act.activation(c.ex[:, 0:NT, 0:e], c.lg[:, 0:NT, 0:e], ACT.Exp).then_inc(exped, 1)

        @block.vector
        def _(dve):
            v = Chain(dve, chain_v)
            dve.wait_ge(done, 1)
            v.link(dve.tensor_copy(c.lg[:, 0:NT, 0:e],
                                   c.ps[0][:, 0:16 * NT].rearrange("p (t e) -> p t e", e=16)[:, :, 0:e]))
            softmax_steps(dve, v, c, NT, e, centred, exped)
            dve.tensor_scalar(c.cw[:, 0:NT, 0:1], c.pr[:, 0:NT, e - 1:e], c.gate[:, 4:5], None, ALU.mult)


def top_steps(dve, v, c, n, e, k):
    for t in range(n):
        v.mark(dve.max(c.top[:, t, :], c.pr[:, t, 0:e]))
    dve.wait_ge(v.sem, v.n)
    for j in range(k, 8):
        v.mark(dve.memset(c.top[:, 0:n, j:j + 1], -2.0))
    dve.wait_ge(v.sem, v.n)
    for t in range(n):
        v.mark(dve.match_replace(c.rest[:, t, 0:e], c.top[:, t, :], c.pr[:, t, 0:e], -1.0))
    dve.wait_ge(v.sem, v.n)
    v.link(dve.tensor_scalar(c.sel[:, 0:n, 0:e], c.rest[:, 0:n, 0:e], -1.0, None, ALU.is_equal))


def stage_moe1(nc, c):
    ne = E1 + 1
    with ExitStack() as ctx:
        done, centred, exped, chain_v, weighted, wt, wtc, up, act_done, down, used, cleared = c.semaphores(nc, (
                "m1_logits", "m1_centred", "m1_exp", "m1_dve", "m1_weights", "m1_wt", "m1_wtcopied", "m1_up",
                "m1_relu", "m1_down", "m1_used", "m1_acc"))
        block = ctx.enter_context(nc.Block())

        @block.tensor
        def _(pe):
            for t in range(NT):
                mm = pe.matmul(c.ps[0][:, t * 16:t * 16 + E1], c.xT[:, t * P:(t + 1) * P], c.wr1[:, :], start=True, stop=True)
            mm.then_inc(done, 1)

            def up_proj(e):
                if e >= 2:
                    pe.wait_ge(act_done, e - 1)
                pe.matmul(c.ps[2 + e % 2][:, :], c.ew1[:, e, :], c.xT[:, :], start=True, stop=True).then_inc(up, 1)
            up_proj(0)
            for e in range(ne):
                if e + 1 < ne:
                    up_proj(e + 1)
                pe.wait_ge(act_done, e + 1)
                if e >= 2:
                    pe.wait_ge(used, NT * (e - 1))
                for t in range(NT):
                    mm = pe.matmul(c.ps[4 + e % 2][:, t * P:(t + 1) * P], c.qT[:, e % 2, t * P:(t + 1) * P],
                                   c.ew2[:, e, :], start=True, stop=True)
                mm.then_inc(down, 1)
            pe.wait_ge(weighted, 1)
            for t in range(NT):
                mm = pe.transpose(c.ps[1][0:ne, t * P:(t + 1) * P], c.cw[:, t, :], c.ident[:, :])
            mm.then_inc(wt, 1)
            pe.wait_ge(wtc, 1)
            for t in range(NT):
                mm = pe.matmul(c.ps[6][:, t * P:(t + 1) * P], c.cwT[:, t * P:(t + 1) * P], c.eb2[:, :],
                               start=True, stop=True)
            mm.then_inc(down, 1)

        @block.scalar
        def _(act):
            act.wait_ge(centred, 1)
            act.activation(c.ex[:, 0:NT, 0:E1], c.lg[:, 0:NT, 0:E1], ACT.Exp).then_inc(exped, 1)
            for e in range(ne):
                act.wait_ge(up, e + 1)
                if e >= 2:
                    act.wait_ge(down, e - 1)
                act.activation(c.qT[:, e % 2, :], c.ps[2 + e % 2][:, :], ACT.Relu, bias=c.eb1[:, e:e + 1]).then_inc(act_done, 1)
            act.wait_ge(wt, 1)
            act.copy(c.cwT[:, :], c.ps[1][0:ne, :]).then_inc(wtc, 1)

        @block.vector
        def _(dve):
            v = Chain(dve, chain_v)
            dve.wait_ge(done, 1)
            br = c.br1[:, :].rearrange("p (a e) -> p a e", a=1).to_broadcast([P, NT, E1])
            v.link(dve.tensor_tensor(c.lg[:, 0:NT, 0:E1],
                                     c.ps[0][:, 0:16 * NT].rearrange("p (t e) -> p t e", e=16)[:, :, 0:E1], br, ALU.add))
            softmax_steps(dve, v, c, NT, E1, centred, exped)
            top_steps(dve, v, c, NT, E1, K1)
            v.mark(dve.memset(c.cw[:, 0:NT, E1:ne], 1.0))
            v.link(dve.tensor_tensor(c.cw[:, 0:NT, 0:E1], c.pr[:, 0:NT, 0:E1], c.sel[:, 0:NT, 0:E1], ALU.mult))
            dve.tensor_scalar(c.cw[:, 0:NT, :], c.cw[:, 0:NT, :], c.gate[:, 5:6], None, ALU.mult).then_inc(weighted, 1)
            dve.wait_ge(weighted, 1)
            for e in range(ne):
                dve.wait_ge(down, e + 1)
                if e:
                    dve.wait_ge(used, NT * e)
                for t in range(NT):
                    dve.scalar_tensor_tensor(out=c.x[:, t, :], in0=c.ps[4 + e % 2][:, t * P:(t + 1) * P],
                                             scalar=c.cw[:, t, e:e + 1], in1=c.x[:, t, :],
                                             op0=ALU.mult, op1=ALU.add).then_inc(used, 1)
            dve.wait_ge(down, ne + 1)
            dve.wait_ge(used, NT * ne)
            dve.tensor_tensor(c.x[:, :, :], c.x[:, :, :], c.ps[6][:, :].rearrange("p (t n) -> p t n", t=NT), ALU.add)


def stage_linear(nc, c, w, bias, gate):
    with ExitStack() as ctx:
        done, chain_v = c.semaphores(nc, ("ln_done", "ln_dve"))
        block = ctx.enter_context(nc.Block())

        @block.tensor
        def _(pe):
            for t in range(NT):
                pe.matmul(c.ps[t][:, 0:D], c.xT[:, t * P:(t + 1) * P], w, start=True, stop=True).then_inc(done, 1)

        @block.vector
        def _(dve):
            if bias is None:
                for t in range(NT):
                    dve.wait_ge(done, t + 1)
                    dve.scalar_tensor_tensor(out=c.x[:, t, :], in0=c.ps[t][:, 0:D], scalar=gate, in1=c.x[:, t, :],
                                             op0=ALU.mult, op1=ALU.add)
            else:
                add_residual(dve, Chain(dve, chain_v), c, done, c.x, bias, lambda t: gate)


def stage_keep(nc, c, half):
    with ExitStack() as ctx:
        c.semaphores(nc, ())
        block = ctx.enter_context(nc.Block())

        @block.vector
        def _(dve):
            dve.tensor_copy(c.x3[:, bass.ds(half * NT, NT), :], c.x[:, :, :])



def stage_moe3(nc, c, A, out, weights3):
    nf = FF // P
    ne = E3 + 2
    w, ws = weights3
    xf, xallT = c.y, c.kT[:, 0:2, :]
    xn, xnT = c.v[:, 0, :].rearrange("p (t n) -> p t n", n=D), c.kT[:, 2:4, :]
    with ExitStack() as ctx:
        names = ("m3_xready", "m3_ready", "m3_xturned", "m3_nturned", "m3_copied", "m3_logits", "m3_centred", "m3_exp", "m3_dve",
                 "m3_sel", "m3_count", "m3_w", "m3_g", "m3_u", "m3_silu", "m3_h", "m3_down", "m3_used", "m3_out",
                 "m3_wload_even", "m3_wload_odd")
        (xready, ready, xturned, nturned, copied, lgs, centred, exped, chain_v, selected, counted, weighted, gsem, usem,
         silu, hsem, down, used, stored, *wload) = c.semaphores(nc, names)
        block = ctx.enter_context(nc.Block())
        hidden = c.qT

        steps = [(e, s) for e in range(ne) for s in range(2)]

        def expert(e):
            return w[:, e % 2, :]

        @block.sync
        def _(sp):
            for e in range(ne):
                if e >= 2:
                    sp.wait_ge(down, 2 * (e - 1))
                if e < E3:
                    srcs = (A["L3_ffn_rg"][e], A["L3_ffn_ru"][e], A["L3_ffn_rd"][e])
                else:
                    a = (e - E3) * FF
                    srcs = (A["L3_ffn_sg"][:, a:a + FF], A["L3_ffn_su"][:, a:a + FF], A["L3_ffn_sd"][a:a + FF, :])
                sp.dma_start(expert(e)[:, 0:FF], srcs[0]).then_inc(wload[e % 2], 16)
                sp.dma_start(expert(e)[:, FF:2 * FF], srcs[1]).then_inc(wload[e % 2], 16)
                sp.dma_start(expert(e)[:, 2 * FF:3 * FF].rearrange("p (f n) -> p f n", n=D),
                             srcs[2].rearrange("(f p) n -> p f n", p=P)).then_inc(wload[e % 2], 16)
            sp.wait_ge(used, TILES * ne)
            sp.dma_start(out.rearrange("b (t p) f -> p (b t) f", p=P), c.x3[:, :, :]).then_inc(stored, 16)
            sp.wait_ge(stored, 16)

        @block.tensor
        def _(pe):
            for t in range(TILES):
                pe.wait_ge(xready, t + 1)
                mm = pe.transpose(c.ps[t // 4][:, (t % 4) * P:(t % 4 + 1) * P], xf[:, t, :], c.ident[:, :])
                if t % 4 == 3:
                    mm.then_inc(xturned, 1)
            for t in range(TILES):
                pe.wait_ge(ready, t + 1)
                mm = pe.transpose(c.ps[2 + t // 4][:, (t % 4) * P:(t % 4 + 1) * P], xn[:, t, :], c.ident[:, :])
                if t % 4 == 3:
                    mm.then_inc(nturned, 1)
            pe.wait_ge(copied, 4)
            for t in range(TILES):
                mm = pe.matmul(c.ps[4][:, t * E3:(t + 1) * E3], xnT[:, t // 4, (t % 4) * P:(t % 4 + 1) * P],
                               c.wr3[:, :], start=True, stop=True)
            mm.then_inc(lgs, 1)
            pe.wait_ge(selected, 1)
            pe.matmul(c.ps[5][:, 0:TILES * E3], c.tri_bf[:, :], c.selb[:, :, :].rearrange("p t e -> p (t e)"),
                      start=True, stop=False)
            pe.matmul(c.ps[5][:, 0:TILES * E3], c.ones_bf[:, :], c.before[:, :, :].rearrange("p t e -> p (t e)"),
                      start=False, stop=True).then_inc(counted, 1)

            def up_proj(i):
                e, s = steps[i]
                if s == 0:
                    pe.wait_ge(wload[e % 2], 48 * (e // 2 + 1))
                for f in range(nf):
                    n = i * nf + f
                    if n >= 2:
                        pe.wait_ge(hsem, n - 1)
                    else:
                        pe.wait_ge(weighted, 1)
                    x = xallT[:, s, :]
                    pe.matmul(c.ps[n % 2][:, :], expert(e)[:, f * P:(f + 1) * P], x, start=True, stop=True).then_inc(gsem, 1)
                    pe.matmul(c.ps[2 + n % 2][:, :], expert(e)[:, FF + f * P:FF + (f + 1) * P], x,
                              start=True, stop=True).then_inc(usem, 1)
            up_proj(0)
            for i, (e, s) in enumerate(steps):
                if i + 1 < len(steps):
                    up_proj(i + 1)
                pe.wait_ge(hsem, nf * (i + 1))
                if i >= 2:
                    pe.wait_ge(used, NT * (i - 1))
                for t in range(NT):
                    for f in range(nf):
                        mm = pe.matmul(c.ps[4 + i % 2][:, t * P:(t + 1) * P],
                                       hidden[:, (i % 2) * nf + f, t * P:(t + 1) * P],
                                       expert(e)[:, 2 * FF + f * D:2 * FF + (f + 1) * D],
                                       start=(f == 0), stop=(f == nf - 1))
                mm.then_inc(down, 1)

        @block.scalar
        def _(act):
            for j in range(2):
                act.wait_ge(xturned, j + 1)
                act.copy(xallT[:, j, :], c.ps[j][:, :]).then_inc(copied, 1)
            for j in range(2):
                act.wait_ge(nturned, j + 1)
                act.copy(xnT[:, j, :], c.ps[2 + j][:, :]).then_inc(copied, 1)
            act.wait_ge(centred, 1)
            act.activation(c.ex[:, :, 0:E3], c.lg[:, :, 0:E3], ACT.Exp).then_inc(exped, 1)
            for n in range(len(steps) * nf):
                act.wait_ge(gsem, n + 1)
                if n >= 2:
                    act.wait_ge(hsem, n - 1)
                act.activation(c.probsT[:, n % 2, :], c.ps[n % 2][:, :], ACT.Silu).then_inc(silu, 1)

        @block.vector
        def _(dve):
            v = Chain(dve, chain_v)
            norm_steps(dve, v, c, c.x3, xf, TILES, "layer", xready)
            dve.wait_ge(xready, TILES)
            norm_steps(dve, v, c, xf, xn, TILES, "rms_eps", ready)
            dve.wait_ge(lgs, 1)
            v.link(dve.tensor_copy(c.lg[:, :, 0:E3], c.ps[4][:, 0:TILES * E3].rearrange("p (t e) -> p t e", e=E3)))
            softmax_steps(dve, v, c, TILES, E3, centred, exped)
            top_steps(dve, v, c, TILES, E3, K3)
            v.link(dve.tensor_tensor(c.cw[:, :, 0:E3], c.pr[:, :, 0:E3], c.sel[:, :, 0:E3], ALU.mult))
            v.link(dve.tensor_reduce(c.rs[:, :], c.cw[:, :, 0:E3], AX.X, ALU.add))
            v.link(dve.reciprocal(c.rs[:, :], c.rs[:, :]))
            share = c.rs[:, :].rearrange("p (n a) -> p n a", a=1).to_broadcast([P, TILES, E3])
            v.link(dve.tensor_tensor(c.cw[:, :, 0:E3], c.cw[:, :, 0:E3], share, ALU.mult))
            v.mark(dve.tensor_copy(c.selb[:, :, :], c.sel[:, :, 0:E3]))
            v.link(dve.memset(c.before[:, 0, :], 0.0))
            for t in range(1, TILES):
                last = dve.tensor_tensor(c.before[:, t, :], c.before[:, t - 1, :], c.selb[:, t - 1, :], ALU.add)
                v.link(last)
            dve.memset(c.cw[:, :, E3:ne], 1.0).then_inc(selected, 1)
            dve.wait_ge(counted, 1)
            v.link(dve.tensor_scalar(c.sel[:, :, 0:E3], c.ps[5][:, 0:TILES * E3].rearrange("p (t e) -> p t e", e=E3),
                                     float(CAP), None, ALU.is_le))
            v.link(dve.tensor_tensor(c.cw[:, :, 0:E3], c.cw[:, :, 0:E3], c.sel[:, :, 0:E3], ALU.mult))
            dve.tensor_scalar(c.cw[:, :, 0:ne], c.cw[:, :, 0:ne], c.gate[:, 7:8], None, ALU.mult).then_inc(weighted, 1)
            dve.wait_ge(weighted, 1)

            def gated(i):
                for f in range(nf):
                    n = i * nf + f
                    dve.wait_ge(silu, n + 1)
                    dve.wait_ge(usem, n + 1)
                    if i >= 2:
                        dve.wait_ge(down, i - 1)
                    dve.tensor_tensor(hidden[:, (i % 2) * nf + f, :], c.ps[2 + n % 2][:, :], c.probsT[:, n % 2, :],
                                      ALU.mult).then_inc(hsem, 1)
            gated(0)
            for i, (e, s) in enumerate(steps):
                if i + 1 < len(steps):
                    gated(i + 1)
                dve.wait_ge(down, i + 1)
                if i >= 2:
                    dve.wait_ge(used, NT * (i - 1))
                for t in range(NT):
                    x = c.x3[:, s * NT + t, :]
                    dve.scalar_tensor_tensor(out=x, in0=c.ps[4 + i % 2][:, t * P:(t + 1) * P],
                                             scalar=c.cw[:, s * NT + t, e:e + 1], in1=x,
                                             op0=ALU.mult, op1=ALU.add).then_inc(used, 1)


def flamingo_kernel(nc, A, out):
    with ExitStack() as ctx:
        ctx.enter_context(nc.allow_non_contiguous_dma(reason="bias columns, a few hundred elements"))
        c = allocate(nc, ctx)
        stage_setup(nc, c, A)
        with nc.Fori(0, HALVES) as half:
            stage_load(nc, c, A, half)

            stage_norm(nc, c, c.x, "layer")
            stage_narrow_qkv(nc, c, c.w0, c.w0, c.w0[:, :], None)
            stage_heads(nc, c, narrow_units(c, lambda b, t: c.m_len[:, b, :]), 4, float(D) ** -0.5)
            stage_turn_back(nc, c, GN, DK, c.gate[:, 0:1])
            stage_norm(nc, c, c.x, "layer")
            stage_router0(nc, c)
            stage_gelu_ffn(nc, c, c.w1_0, c.b1_0, c.w2_0, c.b2_0[:, :], c.x, lambda t: c.cw[:, t, 0:1])

            stage_norm(nc, c, c.x, "layer")
            stage_heads(nc, c, single_units(c), 1, float(D) ** -0.5)
            stage_turn_back(nc, c, 1, P, c.gate[:, 1:2])
            stage_norm(nc, c, c.x, "layer")
            stage_moe1(nc, c)

            for l in range(2):
                for cross in range(2):
                    stage_norm(nc, c, c.u if l or cross else c.x, "rms", c.nw[:, 3 * l + cross:3 * l + cross + 1],
                               inner=not (l or cross))
                    w = c.wa[:, cross, :]
                    names = ("cWq", "cWk", "cWv", "cWo") if cross else ("Wq", "Wk", "Wv", "Wo")
                    stage_load_attn(nc, c, w, [A["L2_xattn_" + n][l] for n in names])
                    stage_wide_qkv(nc, c, w, c.ctxT if cross else c.xT)
                    stage_heads(nc, c, wide_units(c, None if cross else lambda b, t: c.m_key[:, b, :]), 2,
                                float(DH) ** -0.5)
                    stage_out(nc, c, w[:, 3 * INNER:].rearrange("p (f n) -> p f n", n=D), FT, c.u,
                              c.bo2[:, 2 * l + cross, :], None)
                stage_norm(nc, c, c.u, "rms", c.nw[:, 3 * l + 2:3 * l + 3])
                stage_gelu_ffn(nc, c, c.wff1, c.bff1, c.wff2, c.bff2[:, :], c.u, None, loads=[
                    (c.wff1[:, :], A["L2_xattn_ff_w1"][l]),
                    (c.wff2[:, :, :], A["L2_xattn_ff_w2"][l].rearrange("(f p) n -> p f n", p=P)),
                    (c.bff1[:, :], A["L2_xattn_ff_b1"][l].rearrange("(f p) -> p f", p=P)),
                    (c.bff2[:, :], A["L2_xattn_ff_b2"][l].partition_broadcast(P))])
            stage_norm(nc, c, c.u, "rms", c.nw[:, 6:7])
            stage_linear(nc, c, c.proj[:, :], c.projb[:, :], c.gate[:, 2:3])
            stage_norm(nc, c, c.x, "layer")
            stage_linear(nc, c, c.signT[:, :], None, c.gate[:, 6:7])

            stage_norm(nc, c, c.x, "layer")
            stage_narrow_qkv(nc, c, c.w3[:, 0, :], c.w3[:, 1, :], c.w3[:, 2, :], c.b3)
            stage_heads(nc, c, narrow_units(c, lambda b, t: c.m_full[:, b * QT + t, :]), 4, float(DK) ** -0.5,
                        out_bias=lambda g: c.b3[:, 2, g % GN:g % GN + 1])
            stage_out(nc, c, c.wo3, GN, c.x, c.bo3[:, :], lambda t: c.gate[:, 3:4])
            stage_keep(nc, c, half)

            nc.gpsimd.sem_clear(range(c.sems[0][0].num, c.sems[1][-1].num + 1))
            nc.all_engine_barrier()

        stage_moe3(nc, c, A, out, (c.wa, None))


def stage_load_attn(nc, c, w, parts):
    with ExitStack() as ctx:
        loaded, = c.semaphores(nc, ("wl_loaded",))
        block = ctx.enter_context(nc.Block())

        @block.sync
        def _(sp):
            for j in range(3):
                sp.dma_start(w[:, j * INNER:(j + 1) * INNER], parts[j]).then_inc(loaded, 16)
            sp.dma_start(w[:, 3 * INNER:].rearrange("p (f n) -> p f n", n=D),
                         parts[3].rearrange("(f p) n -> p f n", p=P)).then_inc(loaded, 16)
            sp.wait_ge(loaded, 64)


def kernel(**inputs):
    import numpy as np
    import concourse.bacc as bacc
    from concourse import mybir as mb
    from concourse.bass_utils import run_bass_kernel_spmd

    nc = bacc.Bacc("TRN2", target_bir_lowering=False, num_devices=1)
    arrays, A = {}, {}

    def give(name, a):
        a = np.ascontiguousarray(a)
        if a.dtype == np.bool_:
            a = a.view(np.uint8)
        arrays[f"in_{name}"] = a
        A[name] = nc.dram_tensor(f"in_{name}", a.shape, mb.dt.from_np(a.dtype), kind="ExternalInput").ap()

    for name, a in inputs.items():
        give(name, a)
    inv = (1.0 / np.float32(10000.0) ** (np.arange(0, ROT, 2, dtype=np.float32) / np.float32(ROT))).astype(np.float32)
    f = np.arange(S, dtype=np.float32)[:, None] * inv[None, :]
    cos, sin = np.cos(f), np.sin(f)
    give("rope_table", np.concatenate([cos, cos, -sin, sin], axis=1).astype(np.float32))
    out = nc.dram_tensor("out_0", (B, S, D), F32, kind="ExternalOutput").ap()
    flamingo_kernel(nc, A, out)
    r = run_bass_kernel_spmd(nc, [arrays], core_ids=[0])
    return r.results[0]["out_0"]
```

```python
from contextlib import ExitStack

import concourse.bass as bass
from concourse import mybir
from concourse.alu_op_type import AluOpType as ALU

F32 = mybir.dt.float32
F32R = mybir.dt.float32r
BF16 = mybir.dt.bfloat16
I32 = mybir.dt.int32
U8 = mybir.dt.uint8
ACT = mybir.ActivationFunctionType
AX = mybir.AxisListType

P = 128
B, S, D = 4, 256, 128
HALVES = 2
NB = B // HALVES
QT = S // P
NT = NB * QT
TOK = NT * P
TILES = B * S // P
HEADS = 16
DK = D // HEADS
PAD = 32
GN = D * PAD // DK // P
DH = 64
INNER = HEADS * DH
FT = INNER // P
ROT = 32
FF = 512
E1, K1 = 15, 3
E3, K3 = 8, 2
CAP = int(1.25 * B * S / E3)
HIGH_BITS = -4096
LOWEST = -3.0e38
MASKED = -1.0e30


NORM_LAG, TURN_LAG, MIX_LAG, OUT_LAG = 2, 3, 5, 6
NS, NTB = 3, 3
FILL = 8
RING = {1: 4, 2: 6, 4: 8}
SEMS = 24


class Core:

    def __init__(self):
        self.stage = 0

    def semaphores(self, nc, names):
        self.stage += 1
        before = self.sems[(self.stage + 1) % 2]
        nc.gpsimd.sem_clear(range(before[0].num, before[-1].num + 1))
        return self.sems[self.stage % 2][:len(names)]


def allocate(nc, ctx):
    c = Core()
    c.sems = [[nc.alloc_semaphore(f"set{j}_{i}") for i in range(SEMS)] for j in range(2)]

    def sb(name, shape, dt=F32):
        return ctx.enter_context(nc.sbuf_tensor(name, shape, dt))

    c.ident = sb("ident", [P, P])
    c.ident_bf = sb("ident_bf", [P, P], BF16)
    c.ones_bf = sb("ones_bf", [P, P], BF16)
    c.tri_bf = sb("tri_bf", [P, P], BF16)
    c.iota = sb("iota", [P, S])
    c.fill_bf = c.iota[:, :].bitcast(BF16)
    c.rope = sb("rope", [P, QT, 2 * ROT])
    c.gate = sb("gate", [P, 8])
    c.x = sb("x_res", [P, NT, D])
    c.u = sb("u_res", [P, NT, D])
    c.y = sb("y_norm", [P, TILES, D])
    c.xT = sb("xT", [P, TOK])
    c.ctx = sb("ctx_tok", [P, NT, D])
    c.ctxT = sb("ctxT", [P, TOK])
    c.stats = sb("stats", [P, TILES, 6])
    c.mv = sb("mv", [P, TILES, 2])
    c.rstd = sb("rstd", [P, TILES])
    c.msq = sb("msq", [P, TILES])
    c.newton = sb("newton", [P, TILES])
    with nc.sbuf_tensor("qparts", [P, GN, TOK], F32R) as c.qparts, \
            nc.sbuf_tensor("kparts", [P, GN, TOK], F32R) as c.kparts:
        pass
    c.qT = sb("qT", [P, FT, TOK])
    c.kT = sb("kT", [P, FT, TOK])
    c.v = sb("v_tok", [P, NT, INNER])
    c.oT = sb("oT", [P, FT, TOK])
    c.roped = sb("roped", [P, 2, INNER])
    c.rot = sb("rot_tmp", [P, HEADS, ROT])
    c.probsT = sb("probsT", [P, 8, 2 * S])
    c.probs = c.roped[:, :, :].rearrange("p j (r t k) -> p (j r) t k", r=2, t=QT)
    c.whole, c.low = (c.roped[:, j, :].rearrange("p (i n) -> p i n", i=2) for j in range(2))
    c.parts = sb("parts", [P, 4])
    c.b3low = sb("b3low", [P, 2, GN])
    c.ones = sb("ones", [P, PAD])
    c.inv = c.rot[:, :, :].rearrange("p h r -> p (h r)")[:, 0:S]
    c.mx = sb("row_max", [P, 3, QT])
    c.nmx = sb("neg_max", [P, 3, QT])
    c.rsum = sb("row_sum", [P, 3, QT])
    c.rinv = sb("row_inv", [P, 3, QT])
    c.len_i = sb("len_i", [P, NB], I32)
    c.len_f = sb("len_f", [P, NB])
    c.mask_u8 = sb("mask_u8", [P, NB, S], U8)
    c.mask_i32 = sb("mask_i32", [P, NT, S], I32)
    c.m_len = sb("m_len", [P, NB, S])
    c.m_causal = sb("m_causal", [P, QT, S])
    c.m_key = sb("m_key", [P, NB, S])
    c.m_full = c.mask_i32[:, :, :].bitcast(F32)
    c.raw = c.v[:, 0, :].rearrange("p (j n) -> p j n", n=P)
    c.w0 = sb("w0_pad", [P, GN * P])
    c.w0r = sb("w0_rep", [P, GN * P])
    c.wr0 = sb("wr0", [P, 8])
    c.w1_0 = sb("w1_0", [P, FF])
    c.b1_0 = sb("b1_0", [P, FF // P])
    c.w2_0 = sb("w2_0", [P, FF // P, D])
    c.b2_0 = sb("b2_0", [P, D])
    c.wr1 = sb("wr1", [P, E1])
    c.br1 = sb("br1", [P, E1])
    c.ew1 = sb("ew1", [P, E1 + 1, D])
    c.eb1 = sb("eb1", [P, E1 + 1])
    c.ew2 = sb("ew2", [P, E1 + 1, D])
    c.eb2 = sb("eb2", [E1 + 1, D])
    c.wa = sb("w_attn", [P, 2, 4 * INNER])
    c.wff1 = sb("wff1", [P, FF])
    c.wff2 = sb("wff2", [P, FF // P, D])
    c.bff1 = sb("bff1", [P, FF // P])
    c.bff2 = sb("bff2", [P, D])
    c.bo2 = sb("bo2", [P, 4, D])
    c.nw = sb("norm_w", [P, 7])
    c.proj = sb("proj", [P, D])
    c.projb = sb("projb", [P, D])
    c.signT = sb("signT", [P, D])
    c.neg = sb("neg", [P, D])
    c.w3 = sb("w3_pad", [P, 3, GN * P])
    c.b3 = sb("b3_pad", [P, 3, GN])
    c.wo3 = sb("wo3_pad", [P, GN, D])
    c.bo3 = sb("bo3", [P, D])
    c.lg = sb("logits", [P, TILES, 16])
    c.ex = sb("router_exp", [P, TILES, 16])
    c.rm = sb("router_max", [P, TILES])
    c.rs = sb("router_sum", [P, TILES])
    c.pr = sb("router_probs", [P, TILES, 16])
    c.top = sb("router_top", [P, TILES, 8])
    c.rest = sb("router_rest", [P, TILES, 16])
    c.sel = sb("router_sel", [P, TILES, 16])
    c.cw = sb("router_w", [P, TILES, 16])
    c.cwT = sb("router_wT", [16, TOK])
    c.acc = sb("acc", [P, NT, D])
    c.wr3 = sb("wr3", [P, E3])
    c.selb = sb("sel_bf", [P, TILES, E3], BF16)
    c.before = sb("sel_before", [P, TILES, E3], BF16)
    c.x3 = sb("x3", [P, TILES, D])
    c.ps = [ctx.enter_context(nc.psum_tensor(f"bank{i}", [P, 512], F32)) for i in range(8)]
    return c


class Chain:

    def __init__(self, eng, sem):
        self.eng, self.sem, self.n = eng, sem, 0

    def mark(self, ins):
        self.n += 1
        ins.then_inc(self.sem, 1)

    def link(self, ins):
        self.mark(ins)
        self.eng.wait_ge(self.sem, self.n)



def stage_setup(nc, c, A):
    with ExitStack() as ctx:
        loaded, consts, tables, wt, wt_free, chain_v, chain_g, bias_loaded = c.semaphores(nc, (
                "su_loaded", "su_consts", "su_zeroed", "su_transposed", "su_bank_free", "su_dve", "su_pool", "su_bias"))
        loads = [0]
        block = ctx.enter_context(nc.Block())

        @block.sync
        def _(sp):
            def load(dst, src):
                sp.dma_start(dst, src).then_inc(loaded, 16)
                loads[0] += 16
            raw = c.raw
            load(raw[:, 0, :], A["L0_xattn_Wq"])
            load(raw[:, 1, :], A["L3_xattn_Wq"])
            load(raw[:, 2, :], A["L3_xattn_Wk"])
            load(raw[:, 3, :], A["L3_xattn_Wv"])
            load(raw[:, 4, :], A["L3_xattn_Wo"])
            load(raw[:, 5, :], A["L2_ffn_weight"])
            load(raw[0:8, 6, :], A["L0_ffn_Wr"])
            load(raw[0:8, 7, :], A["L3_ffn_router_w"])
            load(c.gate[:, 0:4], A["g_xattn"].partition_broadcast(P))
            load(c.gate[:, 4:8], A["g_ffn"].partition_broadcast(P))
            load(c.parts[:, :], A["part_table"])
            load(c.rope[:, :, :], A["rope_table"].rearrange("(t p) n -> p t n", p=P))
            load(c.w1_0[:, :], A["L0_ffn_W1"][7])
            load(c.b1_0[:, :], A["L0_ffn_b1"][7].rearrange("(t p) -> p t", p=P))
            load(c.w2_0[:, :, :], A["L0_ffn_W2"][7].rearrange("(t p) n -> p t n", p=P))
            load(c.b2_0[:, :], A["L0_ffn_b2"][7].partition_broadcast(P))
            load(c.wr1[:, :], A["L1_ffn_router_W"])
            load(c.br1[:, :], A["L1_ffn_router_b"].partition_broadcast(P))
            load(c.ew1[:, 0:E1, :], A["L1_ffn_eW1"].rearrange("e p n -> p e n"))
            load(c.ew1[:, E1, :], A["L1_ffn_sW1"])
            load(c.eb1[:, 0:E1], A["L1_ffn_eb1"].rearrange("e p -> p e"))
            load(c.eb1[:, E1:E1 + 1], A["L1_ffn_sb1"].rearrange("(p a) -> p a", a=1))
            load(c.ew2[:, 0:E1, :], A["L1_ffn_eW2"].rearrange("e p n -> p e n"))
            load(c.ew2[:, E1, :], A["L1_ffn_sW2"])
            load(c.eb2[0:E1, :], A["L1_ffn_eb2"])
            load(c.eb2[E1:E1 + 1, :], A["L1_ffn_sb2"].rearrange("(a n) -> a n", a=1))
            for l in range(2):
                load(c.bo2[:, 2 * l, :], A["L2_xattn_bo"][l].partition_broadcast(P))
                load(c.bo2[:, 2 * l + 1, :], A["L2_xattn_cbo"][l].partition_broadcast(P))
                for j, n in enumerate(("attn_norm_w", "cross_norm_w", "ff_norm_w")):
                    load(c.nw[:, 3 * l + j:3 * l + j + 1], A["L2_xattn_" + n][l].rearrange("(p a) -> p a", a=1))
            load(c.nw[:, 6:7], A["L2_xattn_norm_out_w"].rearrange("(p a) -> p a", a=1))
            load(c.proj[:, :], A["L2_xattn_proj_w"])
            load(c.projb[:, :], A["L2_xattn_proj_b"].partition_broadcast(P))
            load(c.bo3[:, :], A["L3_xattn_bo"].partition_broadcast(P))
            sp.wait_ge(tables, 1)
            for j, n in enumerate(("bq", "bk", "bv")):
                for h in range(4):
                    for r in range(PAD // DK if j < 2 else 1):
                        sp.dma_start(c.b3[PAD * h + DK * r:PAD * h + DK * (r + 1), j, :],
                                     A["L3_xattn_" + n].rearrange("(g h d) -> h d g", h=4, d=DK)[h]
                                     ).then_inc(bias_loaded, 16)
            sp.wait_ge(loaded, loads[0])
            sp.wait_ge(bias_loaded, 36 * 16)

        @block.gpsimd
        def _(pool):
            g = Chain(pool, chain_g)
            pool.memset(c.b3[:, :, :], 0.0).then_inc(tables, 1)
            g.mark(pool.memset(c.ident[:, :], 0.0))
            g.mark(pool.memset(c.ident_bf[:, :], 0.0))
            g.mark(pool.memset(c.tri_bf[:, :], 1.0))
            g.mark(pool.memset(c.m_causal[:, :, :], 0.0))
            g.mark(pool.memset(c.ones[:, :], 1.0))
            g.link(pool.memset(c.ones_bf[:, :], 1.0))
            for m in (c.ident, c.ident_bf):
                pool.affine_select(out=m[:, :], in_=m[:, :], compare_op=ALU.not_equal, fill=1.0, base=0,
                                   pattern=[[-1, P]], channel_multiplier=1).then_inc(consts, 1)
            pool.affine_select(out=c.tri_bf[:, :], in_=c.tri_bf[:, :], compare_op=ALU.is_ge, fill=0.0, base=0,
                               pattern=[[1, P]], channel_multiplier=-1)
            pool.affine_select(out=c.m_causal[:, :, :], in_=c.m_causal[:, :, :], compare_op=ALU.is_ge, fill=MASKED,
                               base=0, pattern=[[P, QT], [-1, S]], channel_multiplier=1)
            pool.iota(c.iota[:, :], pattern=[[1, S]], base=0, channel_multiplier=0,
                      allow_small_or_imprecise_dtypes=True)

        @block.tensor
        def _(pe):
            pe.wait_ge(consts, 2)
            pe.wait_ge(loaded, loads[0])
            for j in range(8):
                n = P if j < 6 else 8
                pe.transpose(c.ps[j][:, 0:n], c.raw[0:n, j, :], c.ident[0:n, 0:n]).then_inc(wt, 1)
            pe.wait_ge(wt_free, 1)
            for g in range(GN):
                pe.transpose(c.ps[4][:, g * P:(g + 1) * P], c.oT[:, 0, g * P:(g + 1) * P],
                             c.ident[:, :]).then_inc(wt, 1)

        @block.vector
        def _(dve):
            v = Chain(dve, chain_v)
            v.mark(dve.memset(c.w0[:, :], 0.0))
            v.mark(dve.memset(c.w3[:, :, :], 0.0))
            v.link(dve.memset(c.oT[:, 0, :], 0.0))
            dve.wait_ge(loaded, loads[0])

            def spread(dst, src):
                return dve.tensor_copy(dst.rearrange("p (h d) -> p h d", d=PAD)[:, :, 0:DK],
                                       src.rearrange("p (h d) -> p h d", d=DK))
            spread(c.oT[:, 0, :], c.raw[:, 4, :]).then_inc(wt_free, 1)
            dve.wait_ge(wt, 8)
            spread(c.w0[:, :], c.ps[0][:, 0:P])
            spread(c.w3[:, 2, :], c.ps[3][:, 0:P])
            for r in range(PAD // DK):
                for dst, src in ((c.w0r[:, :], c.ps[0]), (c.w3[:, 0, :], c.ps[1]), (c.w3[:, 1, :], c.ps[2])):
                    dve.tensor_copy(dst.rearrange("p (h r d) -> p h r d", r=PAD // DK, d=DK)[:, :, r, :],
                                    src[:, 0:P].rearrange("p (h d) -> p h d", d=DK))
            v.mark(dve.tensor_scalar(c.signT[:, :], c.ps[5][:, 0:P], 0.0, None, ALU.is_gt))
            v.link(dve.tensor_scalar(c.neg[:, :], c.ps[5][:, 0:P], 0.0, None, ALU.is_lt))
            dve.tensor_tensor(c.signT[:, :], c.signT[:, :], c.neg[:, :], ALU.subtract)
            dve.tensor_copy(c.wr0[:, :], c.ps[6][:, 0:8])
            dve.tensor_copy(c.wr3[:, :], c.ps[7][:, 0:8])
            dve.wait_ge(bias_loaded, 36 * 16)
            for j in range(2):
                dve.tensor_scalar(c.b3low[:, j, :], c.b3[:, j, :], c.parts[:, 2 * j:2 * j + 1], None, ALU.mult)
            dve.wait_ge(wt, 8 + GN)
            dve.tensor_copy(c.wo3[:, :, :], c.ps[4][:, 0:GN * P].rearrange("p (g n) -> p g n", g=GN))

        @block.scalar
        def _(act):
            act.wait_ge(loaded, loads[0])
            act.activation(c.gate[:, :], c.gate[:, :], ACT.Tanh)


def stage_load(nc, c, A, half):
    with ExitStack() as ctx:
        loaded, loaded_ctx, tr, chain_v, lenf = c.semaphores(nc, (
            "ld_masks", "ld_ctx", "ld_transposed", "ld_dve", "ld_len"))
        block = ctx.enter_context(nc.Block())

        @block.sync
        def _(sp):
            def rows(a):
                return a.rearrange("b (t p) f -> p (b t) f", p=P)[:, bass.ds(half * NT, NT), :]
            sp.dma_start(c.ctx[:, :, :], rows(A["ctx_1024"])).then_inc(loaded_ctx, 16)
            sp.dma_start(c.x[:, :, :], rows(A["x"])).then_inc(loaded, 16)
            sp.dma_start(c.len_i[:, :], A["_lenS2"][bass.ds(half * NB, NB)].partition_broadcast(P)).then_inc(loaded, 16)
            sp.dma_start(c.mask_u8[:, :, :],
                         A["mask_BxS_bf1"][bass.ds(half * NB, NB), :].partition_broadcast(P)).then_inc(loaded, 16)
            sp.dma_start(c.mask_i32[:, :, :],
                         A["mask_Bx1xSxS2_if1"].rearrange("b a (t p) k -> p (b a t) k", p=P)[:, bass.ds(half * NT, NT), :]
                         ).then_inc(loaded, 16)
            sp.wait_ge(loaded, 64)

        @block.tensor
        def _(pe):
            pe.wait_ge(loaded_ctx, 16)
            for t in range(NT):
                pe.transpose(c.ps[0][:, t * P:(t + 1) * P], c.ctx[:, t, :], c.ident[:, :]).then_inc(tr, 1)

        @block.scalar
        def _(act):
            act.wait_ge(tr, NT)
            act.copy(c.ctxT[:, :], c.ps[0][:, :])

        @block.vector
        def _(dve):
            dve.wait_ge(loaded, 64)
            dve.tensor_copy(c.len_f[:, :], c.len_i[:, :]).then_inc(lenf, 1)
            dve.wait_ge(lenf, 1)
            for b in range(NB):
                dve.tensor_scalar(c.m_len[:, b, :], c.iota[:, :], c.len_f[:, b:b + 1], MASKED, ALU.is_ge, ALU.mult)
            dve.tensor_scalar(c.m_key[:, :, :], c.mask_u8[:, :, :], 0.0, MASKED, ALU.is_equal, ALU.mult)
            dve.tensor_scalar(c.m_full[:, :, :], c.mask_i32[:, :, :], 0.0, MASKED, ALU.is_equal, ALU.mult)



def rsqrt_steps(dve, v, c, n):
    ms, r, t = c.msq[:, 0:n], c.rstd[:, 0:n], c.newton[:, 0:n]
    v.link(dve.tensor_scalar(t.bitcast(I32), ms.bitcast(I32), 1, None, ALU.logical_shift_right))
    v.link(dve.tensor_scalar(r.bitcast(I32), t.bitcast(I32), -1.0, float(0x5F3759DF), ALU.mult, ALU.add))
    for _ in range(3):
        v.link(dve.tensor_tensor(t, r, r, ALU.mult))
        v.link(dve.scalar_tensor_tensor(out=t, in0=t, scalar=-0.5, in1=ms, op0=ALU.mult, op1=ALU.mult))
        v.link(dve.scalar_tensor_tensor(out=r, in0=t, scalar=1.5, in1=r, op0=ALU.add, op1=ALU.mult))


def norm_steps(dve, v, c, src, dst, n, kind, ready):
    for t in range(n):
        v.mark(dve.bn_stats(c.stats[:, t, :], src[:, t, :]))
    dve.wait_ge(v.sem, v.n)
    for t in range(n):
        v.mark(dve.bn_aggr(c.mv[:, t, :], c.stats[:, t, :]))
    dve.wait_ge(v.sem, v.n)
    mean, var, ms = c.mv[:, 0:n, 0], c.mv[:, 0:n, 1], c.msq[:, 0:n]
    if kind == "layer":
        v.link(dve.tensor_scalar(ms, var, 1e-5, None, ALU.add))
    else:
        v.link(dve.tensor_tensor(ms, mean, mean, ALU.mult))
        v.link(dve.tensor_tensor(ms, ms, var, ALU.add))
        if kind == "rms":
            v.link(dve.tensor_scalar(ms, ms, 1e-16, None, ALU.max))
        else:
            v.link(dve.tensor_scalar(ms, ms, 1.1920929e-07, None, ALU.add))
    rsqrt_steps(dve, v, c, n)
    for t in range(n):
        if kind == "layer":
            dve.tensor_scalar(dst[:, t, :], src[:, t, :], c.mv[:, t, 0:1], c.rstd[:, t:t + 1],
                              ALU.subtract, ALU.mult).then_inc(ready, 1)
        else:
            dve.tensor_scalar(dst[:, t, :], src[:, t, :], c.rstd[:, t:t + 1], None, ALU.mult).then_inc(ready, 1)


def stage_norm(nc, c, src, kind, weight=None, inner=False):
    with ExitStack() as ctx:
        ready, ready_u, tr, chain_v = c.semaphores(nc, (
            "nm_ready", "nm_inner", "nm_transposed", "nm_dve"))
        block = ctx.enter_context(nc.Block())

        @block.vector
        def _(dve):
            v = Chain(dve, chain_v)
            s = src
            if inner:
                norm_steps(dve, v, c, src, c.u, NT, "layer", ready_u)
                dve.wait_ge(ready_u, NT)
                s = c.u
            norm_steps(dve, v, c, s, c.y, NT, kind, ready)

        @block.tensor
        def _(pe):
            for t in range(NT):
                pe.wait_ge(ready, t + 1)
                pe.transpose(c.ps[t // 2][:, (t % 2) * P:(t % 2 + 1) * P], c.y[:, t, :], c.ident[:, :]).then_inc(tr, 1)

        @block.scalar
        def _(act):
            for j in range(NT // 2):
                act.wait_ge(tr, 2 * j + 2)
                act.activation(c.xT[:, j * 2 * P:(j + 1) * 2 * P], c.ps[j][:, 0:2 * P], ACT.Copy,
                               scale=1.0 if weight is None else weight)



def stage_narrow_qkv(nc, c, wq, wk, wv, bias):
    with ExitStack() as ctx:
        done, freed, whole, low, high, joined = c.semaphores(nc, (
            "nq_done", "nq_freed", "nq_whole", "nq_low", "nq_high", "nq_joined"))
        block = ctx.enter_context(nc.Block())
        jobs = [(c.qparts, wq, c.xT, 0, g) for g in range(GN)] + [(c.kparts, wk, c.ctxT, 1, g) for g in range(GN)]
        n = len(jobs)

        @block.tensor
        def _(pe):
            for i, (_, w, x, _, g) in enumerate(jobs):
                pe.matmul(c.ps[i][:, :], w[:, g * P:(g + 1) * P], x[:, :], start=True, stop=True).then_inc(done, 1)
            for t in range(NT):
                pe.wait_ge(freed, t + 1)
                pe.matmul(c.ps[t][:, :], c.ctxT[:, t * P:(t + 1) * P], wv, start=True, stop=True).then_inc(done, 1)

        @block.scalar
        def _(act):
            for i, (dst, _, _, j, g) in enumerate(jobs):
                act.wait_ge(done, i + 1)
                if i >= 2:
                    act.wait_ge(joined, i - 1)
                b = 0.0 if bias is None else bias[:, j, g:g + 1]
                bl = 0.0 if bias is None else c.b3low[:, j, g:g + 1]
                act.activation(c.whole[:, i % 2, :], c.ps[i][:, :], ACT.Identity, bias=b).then_inc(whole, 1)
                act.activation(c.low[:, i % 2, :], c.ps[i][:, :], ACT.Identity, bias=bl,
                               scale=c.parts[:, 2 * j:2 * j + 1]).then_inc(freed, 1)
            for t in range(NT):
                act.wait_ge(done, n + t + 1)
                act.activation(c.v[:, t, 0:GN * P], c.ps[t][:, :], ACT.Copy)

        @block.vector
        def _(dve):
            for i, (dst, _, _, j, g) in enumerate(jobs):
                dve.wait_ge(whole, i + 1)
                w = c.whole[:, i % 2, :].bitcast(I32)
                dve.tensor_scalar(w, w, HIGH_BITS, None, ALU.bitwise_and).then_inc(high, 1)
                dve.wait_ge(high, i + 1)
                dve.wait_ge(freed, i + 1)
                dve.scalar_tensor_tensor(out=dst[:, g, :], in0=c.whole[:, i % 2, :], scalar=c.parts[:, 2 * j + 1:2 * j + 2],
                                         in1=c.low[:, i % 2, :], op0=ALU.mult, op1=ALU.add).then_inc(joined, 1)


def stage_wide_qkv(nc, c, w, kv):
    wq, wk, wv = (w[:, j * INNER:(j + 1) * INNER] for j in range(3))
    with ExitStack() as ctx:
        proj, passed, vdone, roped, rchain, tr, tfree = c.semaphores(nc, (
            "wq_proj", "wq_passed", "wq_vcopied", "wq_roped", "wq_dve", "wq_transposed", "wq_tfree"))
        block = ctx.enter_context(nc.Block())
        units = [(j, t) for t in range(NT) for j in range(2)]
        n = len(units)

        @block.tensor
        def _(pe):
            for i in range(n + 1):
                if i < n:
                    j, t = units[i]
                    x = kv if j else c.xT
                    if i >= 2:
                        pe.wait_ge(roped, i - 1)
                        pe.wait_ge(passed, i - 1)
                    for m in range(2):
                        mm = pe.matmul(c.ps[2 * (i % 2) + m][:, :], x[:, t * P:(t + 1) * P],
                                       (wk if j else wq)[:, m * 512:(m + 1) * 512], start=True, stop=True)
                    mm.then_inc(proj, 1)
                    if j:
                        if t:
                            pe.wait_ge(vdone, t)
                        for m in range(2):
                            mm = pe.matmul(c.ps[6 + m][:, :], kv[:, t * P:(t + 1) * P], wv[:, m * 512:(m + 1) * 512],
                                           start=True, stop=True)
                        mm.then_inc(proj, 1)
                if i >= 1:
                    k = i - 1
                    pe.wait_ge(roped, k + 1)
                    pe.wait_ge(passed, k + 1)
                    for m in range(2):
                        if 2 * k + m >= 2:
                            pe.wait_ge(tfree, 2 * k + m - 1)
                        for f in range(4):
                            mm = pe.transpose(c.ps[4 + m][:, f * P:(f + 1) * P],
                                              c.roped[:, k % 2, (4 * m + f) * P:(4 * m + f + 1) * P], c.ident[:, :])
                        mm.then_inc(tr, 1)

        @block.scalar
        def _(act):
            def transposed_out(k):
                j, t = units[k]
                for m in range(2):
                    act.wait_ge(tr, 2 * k + m + 1)
                    act.copy((c.kT if j else c.qT)[:, 4 * m:4 * m + 4, t * P:(t + 1) * P],
                             c.ps[4 + m][:, :].rearrange("p (f n) -> p f n", f=4)).then_inc(tfree, 1)
            for i in range(n + 1):
                if i < n:
                    j, t = units[i]
                    act.wait_ge(proj, i + t + 1)
                    if i >= 2:
                        act.wait_ge(tr, 2 * i - 2)
                    act.wait_ge(roped, i + 1)
                    for m in range(2):
                        cp = act.copy(c.roped[:, i % 2, m * 512:(m + 1) * 512]
                                      .rearrange("p (h d) -> p h d", d=DH)[:, :, ROT:DH],
                                      c.ps[2 * (i % 2) + m][:, :].rearrange("p (h d) -> p h d", d=DH)[:, :, ROT:DH])
                    cp.then_inc(passed, 1)
                    if j:
                        act.wait_ge(proj, i + t + 2)
                        for m in range(2):
                            cp = act.copy(c.v[:, t, m * 512:(m + 1) * 512], c.ps[6 + m][:, :])
                        cp.then_inc(vdone, 1)
                if i >= 1:
                    transposed_out(i - 1)

        @block.vector
        def _(dve):
            v = Chain(dve, rchain)
            half = ROT // 2
            for i, (j, t) in enumerate(units):
                dve.wait_ge(proj, i + t + 1)
                if i >= 2:
                    dve.wait_ge(tr, 2 * i - 2)
                if i >= 1:
                    dve.wait_ge(roped, i)
                cos = c.rope[:, t % QT, 0:ROT]
                sin = c.rope[:, t % QT, ROT:2 * ROT]

                def over_heads(a):
                    return a.rearrange("p (h d) -> p h d", h=1).to_broadcast([P, HEADS // 2, a.shape[-1]])
                for m in range(2):
                    src = c.ps[2 * (i % 2) + m][:, :].rearrange("p (h d) -> p h d", d=DH)
                    dst = c.roped[:, i % 2, m * 512:(m + 1) * 512].rearrange("p (h d) -> p h d", d=DH)
                    tmp = c.rot[:, m * 8:(m + 1) * 8, :]
                    v.mark(dve.tensor_tensor(dst[:, :, 0:ROT], src[:, :, 0:ROT], over_heads(cos), ALU.mult))
                    v.mark(dve.tensor_tensor(tmp[:, :, 0:half], src[:, :, half:ROT], over_heads(sin[:, 0:half]),
                                             ALU.mult))
                    v.mark(dve.tensor_tensor(tmp[:, :, half:ROT], src[:, :, 0:half], over_heads(sin[:, half:ROT]),
                                             ALU.mult))
                dve.wait_ge(v.sem, v.n)
                full = c.roped[:, i % 2, :].rearrange("p (h d) -> p h d", d=DH)[:, :, 0:ROT]
                dve.tensor_tensor(full, full, c.rot[:, :, :], ALU.add).then_inc(roped, 1)


def stage_heads(nc, c, units, per_group, scale, out_bias=None, late=False):
    n = len(units)
    split = per_group // 2
    ring = RING[per_group]
    with ExitStack() as ctx:
        scored, mchain, biased, exped, inverted, normed, turned, copied, mixed, out_free = c.semaphores(nc, (
            "hd_scored", "hd_max", "hd_negmax", "hd_exp", "hd_inverted", "hd_normed", "hd_turned", "hd_copied",
            "hd_mixed", "hd_outfree"))
        block = ctx.enter_context(nc.Block())
        scores = [c.ps[i] for i in range(NS)]
        turns = [c.ps[NS + i] for i in range(NTB)]
        outs = [c.ps[6 + i] for i in range(2)]

        @block.tensor
        def _(pe):
            for i in range(n + MIX_LAG + split):
                if i < n:
                    q, k, _, _, _, _ = units[i]
                    if i >= NS:
                        pe.wait_ge(exped, 2 * (i - NS + 1))
                    for t in range(QT):
                        mm = pe.matmul(scores[i % NS][:, t * S:(t + 1) * S], q(t), k, start=True, stop=True)
                    mm.then_inc(scored, 1)
                if i < TURN_LAG:
                    for _ in range(FILL):
                        pe.matmul(outs[1][:, 0:S], c.ones_bf[:, :], c.fill_bf[:, 0:S], start=True, stop=True)
                if 0 <= i - TURN_LAG < n:
                    j = i - TURN_LAG
                    pe.wait_ge(exped if late else normed, QT * (j + 1))
                    if j >= NTB:
                        pe.wait_ge(copied, j - NTB + 1)
                    for kt in range(QT):
                        for t in range(QT):
                            mm = pe.transpose(turns[j % NTB][:, kt * S + t * P:kt * S + (t + 1) * P],
                                              c.probs[:, j % 4, t, kt * P:(kt + 1) * P], c.ident[:, :])
                    mm.then_inc(turned, 1)
                for step in range(2):
                    j = i - MIX_LAG - step * split
                    if j < 0 or j >= n or j % per_group != per_group - 1:
                        continue
                    g = j // per_group
                    if step == 0:
                        pe.wait_ge(copied, j + 1)
                        if g >= 2:
                            pe.wait_ge(out_free, g - 1)
                    at = slice(S, 2 * S) if late and step else slice(0, S)
                    for kt in range(QT) if late else (step,):
                        for u in range(g * per_group, (g + 1) * per_group):
                            _, _, v, rows, _, _ = units[u]
                            mm = pe.matmul(outs[g % 2][rows, at], c.ones[:, :] if late and step else v(kt),
                                           c.probsT[:, u % ring, kt * S:(kt + 1) * S],
                                           start=(kt == 0), stop=(kt == QT - 1))
                    if step:
                        mm.then_inc(mixed, 1)

        @block.vector
        def _(dve):
            for i in range(n + OUT_LAG + split):
                if i < n:
                    mask = units[i][4]
                    dve.wait_ge(scored, i + 1)
                    if i >= 3:
                        dve.wait_ge(exped, 2 * (i - 2))
                    if mask is None:
                        dve.tensor_reduce(c.mx[:, i % 3, :], scores[i % NS][:, :].rearrange("p (t k) -> p t k", t=QT),
                                          AX.X, ALU.max).then_inc(mchain, QT)
                    else:
                        for t in range(QT):
                            s = scores[i % NS][:, t * S:(t + 1) * S]
                            dve.tensor_tensor_reduce(s, s, mask(t), 1.0, LOWEST, ALU.add, ALU.max,
                                                     c.mx[:, i % 3, t:t + 1]).then_inc(mchain, 1)
                j = i - NORM_LAG
                if 0 <= j < n and not late:
                    dve.wait_ge(exped, 2 * (j + 1))
                    dve.reciprocal(c.rinv[:, j % 3, :], c.rsum[:, j % 3, :]).then_inc(inverted, 1)
                if i < n:
                    dve.wait_ge(mchain, QT * (i + 1))
                    dve.tensor_scalar(c.nmx[:, i % 3, :], c.mx[:, i % 3, :], -scale, None, ALU.mult).then_inc(biased, 1)
                if 0 <= j < n and not late:
                    dve.wait_ge(inverted, j + 1)
                    for t in range(QT):
                        dve.tensor_scalar(c.probs[:, j % 4, t, :], c.probs[:, j % 4, t, :], c.rinv[:, j % 3, t:t + 1],
                                          None, ALU.mult).then_inc(normed, 1)
                j = i - OUT_LAG - split
                if 0 <= j < n and j % per_group == per_group - 1:
                    g = j // per_group
                    dve.wait_ge(mixed, g + 1)
                    dst = units[j][5]
                    src = outs[g % 2][:, 0:S]
                    if late:
                        if g:
                            dve.wait_ge(out_free, g)
                        dve.reciprocal(c.inv[:, :], outs[g % 2][:, S:2 * S]).then_inc(inverted, 1)
                        dve.wait_ge(inverted, g + 1)
                        dve.tensor_tensor(dst, src, c.inv[:, :], ALU.mult).then_inc(out_free, 1)
                        if out_bias is not None:
                            dve.wait_ge(out_free, g + 1)
                            dve.tensor_scalar(dst, dst, out_bias(g), None, ALU.add)
                    else:
                        dve.tensor_copy(dst, src).then_inc(out_free, 1)

        @block.scalar
        def _(act):
            for i in range(n + TURN_LAG):
                if i < n:
                    act.wait_ge(biased, i + 1)
                    if i >= 4:
                        act.wait_ge(turned, i - 3)
                    if i >= 3 and not late:
                        act.wait_ge(inverted, i - 2)
                    for t in range(QT):
                        act.activation(c.probs[:, i % 4, t, :], scores[i % NS][:, t * S:(t + 1) * S], ACT.Exp,
                                       bias=c.nmx[:, i % 3, t:t + 1], scale=scale,
                                       accum_out=None if late else c.rsum[:, i % 3, t:t + 1]).then_inc(exped, 1)
                j = i - TURN_LAG
                if j >= 0:
                    act.wait_ge(turned, j + 1)
                    if j >= ring:
                        act.wait_ge(mixed, (j - ring) // per_group + 1)
                    act.copy(c.probsT[:, j % ring, :], turns[j % NTB][:, :]).then_inc(copied, 1)


def narrow_units(c, mask):
    def unit(b, h):
        g, r = h // 4, PAD * (h % 4)
        return (lambda t: c.qparts[r:r + PAD, g, (b * QT + t) * P:(b * QT + t + 1) * P],
                c.kparts[r:r + PAD, g, b * S:(b + 1) * S],
                lambda kt: c.v[:, b * QT + kt, g * P + r:g * P + r + PAD],
                slice(r, r + PAD), lambda t: mask(b, t), c.oT[:, g, b * S:(b + 1) * S])
    return [unit(b, h) for b in range(NB) for h in range(HEADS)]


def wide_units(c, mask):
    def unit(b, h):
        g, r = h // 2, DH * (h % 2)
        return (lambda t: c.qT[r:r + DH, g, (b * QT + t) * P:(b * QT + t + 1) * P],
                c.kT[r:r + DH, g, b * S:(b + 1) * S],
                lambda kt: c.v[:, b * QT + kt, h * DH:(h + 1) * DH],
                slice(r, r + DH), mask and (lambda t: mask(b, t)), c.oT[:, g, b * S:(b + 1) * S])
    return [unit(b, h) for b in range(NB) for h in range(HEADS)]


def single_units(c):
    def unit(b):
        return (lambda t: c.xT[:, (b * QT + t) * P:(b * QT + t + 1) * P], c.ctxT[:, b * S:(b + 1) * S],
                lambda kt: c.ctx[:, b * QT + kt, :], slice(0, P), lambda t: c.m_causal[:, t, :],
                c.oT[:, 0, b * S:(b + 1) * S])
    return [unit(b) for b in range(NB)]


def stage_turn_back(nc, c, groups, width, gate):
    with ExitStack() as ctx:
        tr, freed = c.semaphores(nc, ("tb_turned", "tb_freed"))
        block = ctx.enter_context(nc.Block())

        @block.tensor
        def _(pe):
            for t in range(NT):
                for g in range(groups):
                    mm = pe.transpose(c.ps[t][:, g * P:(g + 1) * P], c.oT[:, g, t * P:(t + 1) * P], c.ident[:, :])
                mm.then_inc(tr, 1)

        @block.vector
        def _(dve):
            for t in range(NT):
                dve.wait_ge(tr, t + 1)
                src = c.ps[t][:, 0:groups * P]
                dst = c.x[:, t, :]
                if width < P:
                    src = src.rearrange("p (h d) -> p h d", d=PAD)[:, :, 0:width]
                    dst = dst.rearrange("p (h d) -> p h d", d=width)
                dve.scalar_tensor_tensor(out=dst, in0=src, scalar=gate, in1=dst, op0=ALU.mult, op1=ALU.add)


def stage_out(nc, c, w, tiles, res, bias, gate):
    with ExitStack() as ctx:
        done, chain_v = c.semaphores(nc, ("op_done", "op_dve"))
        block = ctx.enter_context(nc.Block())

        @block.tensor
        def _(pe):
            for t in range(NT):
                for f in range(tiles):
                    mm = pe.matmul(c.ps[t][:, 0:D], c.oT[:, f, t * P:(t + 1) * P], w[:, f, :],
                                   start=(f == 0), stop=(f == tiles - 1))
                mm.then_inc(done, 1)

        @block.vector
        def _(dve):
            add_residual(dve, Chain(dve, chain_v), c, done, res, bias, gate)


def add_residual(dve, v, c, done, res, bias, gate):
    for t in range(NT):
        dve.wait_ge(done, t + 1)
        v.link(dve.tensor_tensor(c.acc[:, t, :], c.ps[t][:, 0:D], bias, ALU.add))
        if gate is None:
            dve.tensor_tensor(res[:, t, :], c.acc[:, t, :], res[:, t, :], ALU.add)
        else:
            dve.scalar_tensor_tensor(out=res[:, t, :], in0=c.acc[:, t, :], scalar=gate(t), in1=res[:, t, :],
                                     op0=ALU.mult, op1=ALU.add)



def stage_gelu_ffn(nc, c, w1, b1, w2, b2, res, gate, loads=None):
    nf = FF // P
    with ExitStack() as ctx:
        loaded, up, act_done, done, chain_v = c.semaphores(nc, (
            "ff_loaded", "ff_up", "ff_gelu", "ff_done", "ff_dve"))
        block = ctx.enter_context(nc.Block())

        if loads:
            @block.sync
            def _(sp):
                for dst, src in loads:
                    sp.dma_start(dst, src).then_inc(loaded, 16)

        @block.tensor
        def _(pe):
            if loads:
                pe.wait_ge(loaded, 16 * len(loads))
            for f in range(nf):
                pe.matmul(c.ps[4 + f][:, :], w1[:, f * P:(f + 1) * P], c.xT[:, :], start=True, stop=True).then_inc(up, 1)
            for f in range(nf):
                pe.wait_ge(act_done, f + 1)
                for t in range(NT):
                    mm = pe.matmul(c.ps[t][:, 0:D], c.qT[:, f, t * P:(t + 1) * P], w2[:, f, :],
                                   start=(f == 0), stop=(f == nf - 1))
                    if f == nf - 1:
                        mm.then_inc(done, 1)

        @block.scalar
        def _(act):
            if loads:
                act.wait_ge(loaded, 16 * len(loads))
            for f in range(nf):
                act.wait_ge(up, f + 1)
                act.activation(c.qT[:, f, :], c.ps[4 + f][:, :], ACT.Gelu, bias=b1[:, f:f + 1]).then_inc(act_done, 1)

        @block.vector
        def _(dve):
            if loads:
                dve.wait_ge(loaded, 16 * len(loads))
            add_residual(dve, Chain(dve, chain_v), c, done, res, b2, gate)


def softmax_steps(dve, v, c, n, e, logits_to, exped):
    lg, ex, pr = (a[:, 0:n, 0:e] for a in (c.lg, c.ex, c.pr))

    def wide(a):
        return a[:, 0:n].rearrange("p (n a) -> p n a", a=1).to_broadcast([P, n, e])
    v.link(dve.tensor_reduce(c.rm[:, 0:n], lg, AX.X, ALU.max))
    dve.tensor_tensor(lg, lg, wide(c.rm), ALU.subtract).then_inc(logits_to, 1)
    dve.wait_ge(exped, 1)
    v.link(dve.tensor_reduce(c.rs[:, 0:n], ex, AX.X, ALU.add))
    v.link(dve.reciprocal(c.rs[:, 0:n], c.rs[:, 0:n]))
    v.link(dve.tensor_tensor(pr, ex, wide(c.rs), ALU.mult))


def stage_router0(nc, c):
    e = 8
    with ExitStack() as ctx:
        done, centred, exped, chain_v = c.semaphores(nc, (
            "r0_done", "r0_centred", "r0_exp", "r0_dve"))
        block = ctx.enter_context(nc.Block())

        @block.tensor
        def _(pe):
            for t in range(NT):
                mm = pe.matmul(c.ps[0][:, t * 16:t * 16 + e], c.xT[:, t * P:(t + 1) * P], c.wr0[:, :], start=True, stop=True)
            mm.then_inc(done, 1)

        @block.scalar
        def _(act):
            act.wait_ge(centred, 1)
            act.activation(c.ex[:, 0:NT, 0:e], c.lg[:, 0:NT, 0:e], ACT.Exp).then_inc(exped, 1)

        @block.vector
        def _(dve):
            v = Chain(dve, chain_v)
            dve.wait_ge(done, 1)
            v.link(dve.tensor_copy(c.lg[:, 0:NT, 0:e],
                                   c.ps[0][:, 0:16 * NT].rearrange("p (t e) -> p t e", e=16)[:, :, 0:e]))
            softmax_steps(dve, v, c, NT, e, centred, exped)
            dve.tensor_scalar(c.cw[:, 0:NT, 0:1], c.pr[:, 0:NT, e - 1:e], c.gate[:, 4:5], None, ALU.mult)


def top_steps(dve, v, c, n, e, k):
    for t in range(n):
        v.mark(dve.max(c.top[:, t, :], c.pr[:, t, 0:e]))
    dve.wait_ge(v.sem, v.n)
    for j in range(k, 8):
        v.mark(dve.memset(c.top[:, 0:n, j:j + 1], -2.0))
    dve.wait_ge(v.sem, v.n)
    for t in range(n):
        v.mark(dve.match_replace(c.rest[:, t, 0:e], c.top[:, t, :], c.pr[:, t, 0:e], -1.0))
    dve.wait_ge(v.sem, v.n)
    v.link(dve.tensor_scalar(c.sel[:, 0:n, 0:e], c.rest[:, 0:n, 0:e], -1.0, None, ALU.is_equal))


def stage_moe1(nc, c):
    ne = E1 + 1
    with ExitStack() as ctx:
        done, centred, exped, chain_v, weighted, wt, wtc, up, act_done, down, used, cleared = c.semaphores(nc, (
                "m1_logits", "m1_centred", "m1_exp", "m1_dve", "m1_weights", "m1_wt", "m1_wtcopied", "m1_up",
                "m1_relu", "m1_down", "m1_used", "m1_acc"))
        block = ctx.enter_context(nc.Block())

        @block.tensor
        def _(pe):
            for t in range(NT):
                mm = pe.matmul(c.ps[0][:, t * 16:t * 16 + E1], c.xT[:, t * P:(t + 1) * P], c.wr1[:, :], start=True, stop=True)
            mm.then_inc(done, 1)

            def up_proj(e):
                if e >= 2:
                    pe.wait_ge(act_done, e - 1)
                pe.matmul(c.ps[2 + e % 2][:, :], c.ew1[:, e, :], c.xT[:, :], start=True, stop=True).then_inc(up, 1)
            up_proj(0)
            for e in range(ne):
                if e + 1 < ne:
                    up_proj(e + 1)
                pe.wait_ge(act_done, e + 1)
                if e >= 2:
                    pe.wait_ge(used, NT * (e - 1))
                for t in range(NT):
                    mm = pe.matmul(c.ps[4 + e % 2][:, t * P:(t + 1) * P], c.qT[:, e % 2, t * P:(t + 1) * P],
                                   c.ew2[:, e, :], start=True, stop=True)
                mm.then_inc(down, 1)
            pe.wait_ge(weighted, 1)
            for t in range(NT):
                mm = pe.transpose(c.ps[1][0:ne, t * P:(t + 1) * P], c.cw[:, t, :], c.ident[:, :])
            mm.then_inc(wt, 1)
            pe.wait_ge(wtc, 1)
            for t in range(NT):
                mm = pe.matmul(c.ps[6][:, t * P:(t + 1) * P], c.cwT[:, t * P:(t + 1) * P], c.eb2[:, :],
                               start=True, stop=True)
            mm.then_inc(down, 1)

        @block.scalar
        def _(act):
            act.wait_ge(centred, 1)
            act.activation(c.ex[:, 0:NT, 0:E1], c.lg[:, 0:NT, 0:E1], ACT.Exp).then_inc(exped, 1)
            for e in range(ne):
                act.wait_ge(up, e + 1)
                if e >= 2:
                    act.wait_ge(down, e - 1)
                act.activation(c.qT[:, e % 2, :], c.ps[2 + e % 2][:, :], ACT.Relu, bias=c.eb1[:, e:e + 1]).then_inc(act_done, 1)
            act.wait_ge(wt, 1)
            act.copy(c.cwT[:, :], c.ps[1][0:ne, :]).then_inc(wtc, 1)

        @block.vector
        def _(dve):
            v = Chain(dve, chain_v)
            dve.wait_ge(done, 1)
            br = c.br1[:, :].rearrange("p (a e) -> p a e", a=1).to_broadcast([P, NT, E1])
            v.link(dve.tensor_tensor(c.lg[:, 0:NT, 0:E1],
                                     c.ps[0][:, 0:16 * NT].rearrange("p (t e) -> p t e", e=16)[:, :, 0:E1], br, ALU.add))
            softmax_steps(dve, v, c, NT, E1, centred, exped)
            top_steps(dve, v, c, NT, E1, K1)
            v.mark(dve.memset(c.cw[:, 0:NT, E1:ne], 1.0))
            v.link(dve.tensor_tensor(c.cw[:, 0:NT, 0:E1], c.pr[:, 0:NT, 0:E1], c.sel[:, 0:NT, 0:E1], ALU.mult))
            dve.tensor_scalar(c.cw[:, 0:NT, :], c.cw[:, 0:NT, :], c.gate[:, 5:6], None, ALU.mult).then_inc(weighted, 1)
            dve.wait_ge(weighted, 1)
            for e in range(ne):
                dve.wait_ge(down, e + 1)
                if e:
                    dve.wait_ge(used, NT * e)
                for t in range(NT):
                    dve.scalar_tensor_tensor(out=c.x[:, t, :], in0=c.ps[4 + e % 2][:, t * P:(t + 1) * P],
                                             scalar=c.cw[:, t, e:e + 1], in1=c.x[:, t, :],
                                             op0=ALU.mult, op1=ALU.add).then_inc(used, 1)
            dve.wait_ge(down, ne + 1)
            dve.wait_ge(used, NT * ne)
            dve.tensor_tensor(c.x[:, :, :], c.x[:, :, :], c.ps[6][:, :].rearrange("p (t n) -> p t n", t=NT), ALU.add)


def stage_linear(nc, c, w, bias, gate):
    with ExitStack() as ctx:
        done, chain_v = c.semaphores(nc, ("ln_done", "ln_dve"))
        block = ctx.enter_context(nc.Block())

        @block.tensor
        def _(pe):
            for t in range(NT):
                pe.matmul(c.ps[t][:, 0:D], c.xT[:, t * P:(t + 1) * P], w, start=True, stop=True).then_inc(done, 1)

        @block.vector
        def _(dve):
            if bias is None:
                for t in range(NT):
                    dve.wait_ge(done, t + 1)
                    dve.scalar_tensor_tensor(out=c.x[:, t, :], in0=c.ps[t][:, 0:D], scalar=gate, in1=c.x[:, t, :],
                                             op0=ALU.mult, op1=ALU.add)
            else:
                add_residual(dve, Chain(dve, chain_v), c, done, c.x, bias, lambda t: gate)


def stage_keep(nc, c, half):
    with ExitStack() as ctx:
        c.semaphores(nc, ())
        block = ctx.enter_context(nc.Block())

        @block.vector
        def _(dve):
            dve.tensor_copy(c.x3[:, bass.ds(half * NT, NT), :], c.x[:, :, :])



def stage_moe3(nc, c, A, out, weights3):
    nf = FF // P
    ne = E3 + 2
    w, ws = weights3
    xf, xallT = c.y, c.kT[:, 0:2, :]
    xn, xnT = c.v[:, 0, :].rearrange("p (t n) -> p t n", n=D), c.kT[:, 2:4, :]
    with ExitStack() as ctx:
        names = ("m3_xready", "m3_ready", "m3_xturned", "m3_nturned", "m3_copied", "m3_logits", "m3_centred", "m3_exp", "m3_dve",
                 "m3_sel", "m3_count", "m3_w", "m3_g", "m3_u", "m3_silu", "m3_h", "m3_down", "m3_used", "m3_out",
                 "m3_wload_even", "m3_wload_odd")
        (xready, ready, xturned, nturned, copied, lgs, centred, exped, chain_v, selected, counted, weighted, gsem, usem,
         silu, hsem, down, used, stored, *wload) = c.semaphores(nc, names)
        block = ctx.enter_context(nc.Block())
        hidden = c.qT

        steps = [(e, s) for e in range(ne) for s in range(2)]

        def expert(e):
            return w[:, e % 2, :]

        @block.sync
        def _(sp):
            for e in range(ne):
                if e >= 2:
                    sp.wait_ge(down, 2 * (e - 1))
                if e < E3:
                    srcs = (A["L3_ffn_rg"][e], A["L3_ffn_ru"][e], A["L3_ffn_rd"][e])
                else:
                    a = (e - E3) * FF
                    srcs = (A["L3_ffn_sg"][:, a:a + FF], A["L3_ffn_su"][:, a:a + FF], A["L3_ffn_sd"][a:a + FF, :])
                sp.dma_start(expert(e)[:, 0:FF], srcs[0]).then_inc(wload[e % 2], 16)
                sp.dma_start(expert(e)[:, FF:2 * FF], srcs[1]).then_inc(wload[e % 2], 16)
                sp.dma_start(expert(e)[:, 2 * FF:3 * FF].rearrange("p (f n) -> p f n", n=D),
                             srcs[2].rearrange("(f p) n -> p f n", p=P)).then_inc(wload[e % 2], 16)
            sp.wait_ge(used, TILES * ne)
            sp.dma_start(out.rearrange("b (t p) f -> p (b t) f", p=P), c.x3[:, :, :]).then_inc(stored, 16)
            sp.wait_ge(stored, 16)

        @block.tensor
        def _(pe):
            for t in range(TILES):
                pe.wait_ge(xready, t + 1)
                mm = pe.transpose(c.ps[t // 4][:, (t % 4) * P:(t % 4 + 1) * P], xf[:, t, :], c.ident[:, :])
                if t % 4 == 3:
                    mm.then_inc(xturned, 1)
            for t in range(TILES):
                pe.wait_ge(ready, t + 1)
                mm = pe.transpose(c.ps[2 + t // 4][:, (t % 4) * P:(t % 4 + 1) * P], xn[:, t, :], c.ident[:, :])
                if t % 4 == 3:
                    mm.then_inc(nturned, 1)
            pe.wait_ge(copied, 4)
            for t in range(TILES):
                mm = pe.matmul(c.ps[4][:, t * E3:(t + 1) * E3], xnT[:, t // 4, (t % 4) * P:(t % 4 + 1) * P],
                               c.wr3[:, :], start=True, stop=True)
            mm.then_inc(lgs, 1)
            pe.wait_ge(selected, 1)
            pe.matmul(c.ps[5][:, 0:TILES * E3], c.tri_bf[:, :], c.selb[:, :, :].rearrange("p t e -> p (t e)"),
                      start=True, stop=False)
            pe.matmul(c.ps[5][:, 0:TILES * E3], c.ones_bf[:, :], c.before[:, :, :].rearrange("p t e -> p (t e)"),
                      start=False, stop=True).then_inc(counted, 1)

            def up_proj(i):
                e, s = steps[i]
                if s == 0:
                    pe.wait_ge(wload[e % 2], 48 * (e // 2 + 1))
                for f in range(nf):
                    n = i * nf + f
                    if n >= 2:
                        pe.wait_ge(hsem, n - 1)
                    else:
                        pe.wait_ge(weighted, 1)
                    x = xallT[:, s, :]
                    pe.matmul(c.ps[n % 2][:, :], expert(e)[:, f * P:(f + 1) * P], x, start=True, stop=True).then_inc(gsem, 1)
                    pe.matmul(c.ps[2 + n % 2][:, :], expert(e)[:, FF + f * P:FF + (f + 1) * P], x,
                              start=True, stop=True).then_inc(usem, 1)
            up_proj(0)
            for i, (e, s) in enumerate(steps):
                if i + 1 < len(steps):
                    up_proj(i + 1)
                pe.wait_ge(hsem, nf * (i + 1))
                if i >= 2:
                    pe.wait_ge(used, NT * (i - 1))
                for t in range(NT):
                    for f in range(nf):
                        mm = pe.matmul(c.ps[4 + i % 2][:, t * P:(t + 1) * P],
                                       hidden[:, (i % 2) * nf + f, t * P:(t + 1) * P],
                                       expert(e)[:, 2 * FF + f * D:2 * FF + (f + 1) * D],
                                       start=(f == 0), stop=(f == nf - 1))
                mm.then_inc(down, 1)

        @block.scalar
        def _(act):
            for j in range(2):
                act.wait_ge(xturned, j + 1)
                act.copy(xallT[:, j, :], c.ps[j][:, :]).then_inc(copied, 1)
            for j in range(2):
                act.wait_ge(nturned, j + 1)
                act.copy(xnT[:, j, :], c.ps[2 + j][:, :]).then_inc(copied, 1)
            act.wait_ge(centred, 1)
            act.activation(c.ex[:, :, 0:E3], c.lg[:, :, 0:E3], ACT.Exp).then_inc(exped, 1)
            for n in range(len(steps) * nf):
                act.wait_ge(gsem, n + 1)
                if n >= 2:
                    act.wait_ge(hsem, n - 1)
                act.activation(c.probsT[:, n % 2, :], c.ps[n % 2][:, :], ACT.Silu).then_inc(silu, 1)

        @block.vector
        def _(dve):
            v = Chain(dve, chain_v)
            norm_steps(dve, v, c, c.x3, xf, TILES, "layer", xready)
            dve.wait_ge(xready, TILES)
            norm_steps(dve, v, c, xf, xn, TILES, "rms_eps", ready)
            dve.wait_ge(lgs, 1)
            v.link(dve.tensor_copy(c.lg[:, :, 0:E3], c.ps[4][:, 0:TILES * E3].rearrange("p (t e) -> p t e", e=E3)))
            softmax_steps(dve, v, c, TILES, E3, centred, exped)
            top_steps(dve, v, c, TILES, E3, K3)
            v.link(dve.tensor_tensor(c.cw[:, :, 0:E3], c.pr[:, :, 0:E3], c.sel[:, :, 0:E3], ALU.mult))
            v.link(dve.tensor_reduce(c.rs[:, :], c.cw[:, :, 0:E3], AX.X, ALU.add))
            v.link(dve.reciprocal(c.rs[:, :], c.rs[:, :]))
            share = c.rs[:, :].rearrange("p (n a) -> p n a", a=1).to_broadcast([P, TILES, E3])
            v.link(dve.tensor_tensor(c.cw[:, :, 0:E3], c.cw[:, :, 0:E3], share, ALU.mult))
            v.mark(dve.tensor_copy(c.selb[:, :, :], c.sel[:, :, 0:E3]))
            v.link(dve.memset(c.before[:, 0, :], 0.0))
            for t in range(1, TILES):
                last = dve.tensor_tensor(c.before[:, t, :], c.before[:, t - 1, :], c.selb[:, t - 1, :], ALU.add)
                v.link(last)
            dve.memset(c.cw[:, :, E3:ne], 1.0).then_inc(selected, 1)
            dve.wait_ge(counted, 1)
            v.link(dve.tensor_scalar(c.sel[:, :, 0:E3], c.ps[5][:, 0:TILES * E3].rearrange("p (t e) -> p t e", e=E3),
                                     float(CAP), None, ALU.is_le))
            v.link(dve.tensor_tensor(c.cw[:, :, 0:E3], c.cw[:, :, 0:E3], c.sel[:, :, 0:E3], ALU.mult))
            dve.tensor_scalar(c.cw[:, :, 0:ne], c.cw[:, :, 0:ne], c.gate[:, 7:8], None, ALU.mult).then_inc(weighted, 1)
            dve.wait_ge(weighted, 1)

            def gated(i):
                for f in range(nf):
                    n = i * nf + f
                    dve.wait_ge(silu, n + 1)
                    dve.wait_ge(usem, n + 1)
                    if i >= 2:
                        dve.wait_ge(down, i - 1)
                    dve.tensor_tensor(hidden[:, (i % 2) * nf + f, :], c.ps[2 + n % 2][:, :], c.probsT[:, n % 2, :],
                                      ALU.mult).then_inc(hsem, 1)
            gated(0)
            for i, (e, s) in enumerate(steps):
                if i + 1 < len(steps):
                    gated(i + 1)
                dve.wait_ge(down, i + 1)
                if i >= 2:
                    dve.wait_ge(used, NT * (i - 1))
                for t in range(NT):
                    x = c.x3[:, s * NT + t, :]
                    dve.scalar_tensor_tensor(out=x, in0=c.ps[4 + i % 2][:, t * P:(t + 1) * P],
                                             scalar=c.cw[:, s * NT + t, e:e + 1], in1=x,
                                             op0=ALU.mult, op1=ALU.add).then_inc(used, 1)


def flamingo_kernel(nc, A, out):
    with ExitStack() as ctx:
        ctx.enter_context(nc.allow_non_contiguous_dma(reason="bias columns, a few hundred elements"))
        c = allocate(nc, ctx)
        stage_setup(nc, c, A)
        with nc.Fori(0, HALVES) as half:
            stage_load(nc, c, A, half)

            stage_norm(nc, c, c.x, "layer")
            stage_narrow_qkv(nc, c, c.w0r, c.w0r, c.w0[:, :], None)
            stage_heads(nc, c, narrow_units(c, lambda b, t: c.m_len[:, b, :]), 4, float(D) ** -0.5, late=True)
            stage_turn_back(nc, c, GN, DK, c.gate[:, 0:1])
            stage_norm(nc, c, c.x, "layer")
            stage_router0(nc, c)
            stage_gelu_ffn(nc, c, c.w1_0, c.b1_0, c.w2_0, c.b2_0[:, :], c.x, lambda t: c.cw[:, t, 0:1])

            stage_norm(nc, c, c.x, "layer")
            stage_heads(nc, c, single_units(c), 1, float(D) ** -0.5)
            stage_turn_back(nc, c, 1, P, c.gate[:, 1:2])
            stage_norm(nc, c, c.x, "layer")
            stage_moe1(nc, c)

            for l in range(2):
                for cross in range(2):
                    stage_norm(nc, c, c.u if l or cross else c.x, "rms", c.nw[:, 3 * l + cross:3 * l + cross + 1],
                               inner=not (l or cross))
                    w = c.wa[:, cross, :]
                    names = ("cWq", "cWk", "cWv", "cWo") if cross else ("Wq", "Wk", "Wv", "Wo")
                    stage_load_attn(nc, c, w, [A["L2_xattn_" + n][l] for n in names])
                    stage_wide_qkv(nc, c, w, c.ctxT if cross else c.xT)
                    stage_heads(nc, c, wide_units(c, None if cross else lambda b, t: c.m_key[:, b, :]), 2,
                                float(DH) ** -0.5)
                    stage_out(nc, c, w[:, 3 * INNER:].rearrange("p (f n) -> p f n", n=D), FT, c.u,
                              c.bo2[:, 2 * l + cross, :], None)
                stage_norm(nc, c, c.u, "rms", c.nw[:, 3 * l + 2:3 * l + 3])
                stage_gelu_ffn(nc, c, c.wff1, c.bff1, c.wff2, c.bff2[:, :], c.u, None, loads=[
                    (c.wff1[:, :], A["L2_xattn_ff_w1"][l]),
                    (c.wff2[:, :, :], A["L2_xattn_ff_w2"][l].rearrange("(f p) n -> p f n", p=P)),
                    (c.bff1[:, :], A["L2_xattn_ff_b1"][l].rearrange("(f p) -> p f", p=P)),
                    (c.bff2[:, :], A["L2_xattn_ff_b2"][l].partition_broadcast(P))])
            stage_norm(nc, c, c.u, "rms", c.nw[:, 6:7])
            stage_linear(nc, c, c.proj[:, :], c.projb[:, :], c.gate[:, 2:3])
            stage_norm(nc, c, c.x, "layer")
            stage_linear(nc, c, c.signT[:, :], None, c.gate[:, 6:7])

            stage_norm(nc, c, c.x, "layer")
            stage_narrow_qkv(nc, c, c.w3[:, 0, :], c.w3[:, 1, :], c.w3[:, 2, :], c.b3)
            stage_heads(nc, c, narrow_units(c, lambda b, t: c.m_full[:, b * QT + t, :]), 4, float(DK) ** -0.5,
                        out_bias=lambda g: c.b3[:, 2, g % GN:g % GN + 1], late=True)
            stage_out(nc, c, c.wo3, GN, c.x, c.bo3[:, :], lambda t: c.gate[:, 3:4])
            stage_keep(nc, c, half)

            nc.gpsimd.sem_clear(range(c.sems[0][0].num, c.sems[1][-1].num + 1))
            nc.all_engine_barrier()

        stage_moe3(nc, c, A, out, (c.wa, None))


def stage_load_attn(nc, c, w, parts):
    with ExitStack() as ctx:
        loaded, = c.semaphores(nc, ("wl_loaded",))
        block = ctx.enter_context(nc.Block())

        @block.sync
        def _(sp):
            for j in range(3):
                sp.dma_start(w[:, j * INNER:(j + 1) * INNER], parts[j]).then_inc(loaded, 16)
            sp.dma_start(w[:, 3 * INNER:].rearrange("p (f n) -> p f n", n=D),
                         parts[3].rearrange("(f p) n -> p f n", p=P)).then_inc(loaded, 16)
            sp.wait_ge(loaded, 64)


def kernel(**inputs):
    import numpy as np
    import concourse.bacc as bacc
    from concourse import mybir as mb
    from concourse.bass_utils import run_bass_kernel_spmd

    nc = bacc.Bacc("TRN2", target_bir_lowering=False, num_devices=1)
    arrays, A = {}, {}

    def give(name, a):
        a = np.ascontiguousarray(a)
        if a.dtype == np.bool_:
            a = a.view(np.uint8)
        arrays[f"in_{name}"] = a
        A[name] = nc.dram_tensor(f"in_{name}", a.shape, mb.dt.from_np(a.dtype), kind="ExternalInput").ap()

    for name, a in inputs.items():
        give(name, a)
    inv = (1.0 / np.float32(10000.0) ** (np.arange(0, ROT, 2, dtype=np.float32) / np.float32(ROT))).astype(np.float32)
    f = np.arange(S, dtype=np.float32)[:, None] * inv[None, :]
    cos, sin = np.cos(f), np.sin(f)
    give("rope_table", np.concatenate([cos, cos, -sin, sin], axis=1).astype(np.float32))
    row = np.arange(P)
    low_q, low_k = row // (2 * DK) % 2, row // DK % 2
    give("part_table", np.stack([low_q, 1 - 2 * low_q, low_k, 1 - 2 * low_k], axis=1).astype(np.float32))
    out = nc.dram_tensor("out_0", (B, S, D), F32, kind="ExternalOutput").ap()
    flamingo_kernel(nc, A, out)
    r = run_bass_kernel_spmd(nc, [arrays], core_ids=[0])
    return r.results[0]["out_0"]
```

```python
from contextlib import ExitStack

import concourse.bass as bass
from concourse import mybir
from concourse.alu_op_type import AluOpType as ALU

F32 = mybir.dt.float32
F32R = mybir.dt.float32r
BF16 = mybir.dt.bfloat16
I32 = mybir.dt.int32
U8 = mybir.dt.uint8
ACT = mybir.ActivationFunctionType
AX = mybir.AxisListType

P = 128
B, S, D = 4, 256, 128
HALVES = 2
NB = B // HALVES
QT = S // P
NT = NB * QT
TOK = NT * P
TILES = B * S // P
HEADS = 16
DK = D // HEADS
PAD = 32
GN = D * PAD // DK // P
DH = 64
INNER = HEADS * DH
FT = INNER // P
ROT = 32
FF = 512
E1, K1 = 15, 3
E3, K3 = 8, 2
CAP = int(1.25 * B * S / E3)
HIGH_BITS = -4096
LOWEST = -3.0e38
MASKED = -1.0e30


NORM_LAG, TURN_LAG, MIX_LAG, OUT_LAG = 1, 3, 6, 7
NS, NTB = 3, 3
FILL = 3
TAIL_FILL = 8
NORM_FILL = 34
SEMS = 24


class Core:

    def __init__(self):
        self.stage = 0

    def semaphores(self, nc, names):
        self.stage += 1
        before = self.sems[(self.stage + 1) % 2]
        nc.gpsimd.sem_clear(range(before[0].num, before[-1].num + 1))
        return self.sems[self.stage % 2][:len(names)]


def allocate(nc, ctx):
    c = Core()
    c.constants = nc.alloc_semaphore("constants_loaded")
    c.attn_loaded = [nc.alloc_semaphore(f"attn_loaded_{j}") for j in range(2)]
    c.ff_loaded = nc.alloc_semaphore("ff_loaded")
    c.sems = [[nc.alloc_semaphore(f"set{j}_{i}") for i in range(SEMS)] for j in range(2)]

    def sb(name, shape, dt=F32):
        return ctx.enter_context(nc.sbuf_tensor(name, shape, dt))

    c.ident = sb("ident", [P, P])
    c.ident_bf = sb("ident_bf", [P, P], BF16)
    c.ones_bf = sb("ones_bf", [P, P], BF16)
    c.tri_bf = sb("tri_bf", [P, P], BF16)
    c.iota = sb("iota", [P, S])
    c.fill_bf = c.iota[:, :].bitcast(BF16)
    c.slot = sb("slot", [P, 2])
    c.rope = sb("rope", [P, QT, 2 * ROT])
    c.gate = sb("gate", [P, 8])
    c.x = sb("x_res", [P, NT, D])
    c.u = sb("u_res", [P, NT, D])
    c.y = sb("y_norm", [P, TILES, D])
    c.xT = sb("xT", [P, TOK])
    c.ctx = sb("ctx_tok", [P, NT, D])
    c.ctxT = sb("ctxT", [P, TOK])
    c.stats = sb("stats", [P, TILES, 6])
    c.mv = sb("mv", [P, TILES, 2])
    c.rstd = sb("rstd", [P, TILES])
    c.msq = sb("msq", [P, TILES])
    c.newton = sb("newton", [P, TILES])
    c.scaled = sb("scaled", [P, TILES])
    with nc.sbuf_tensor("qparts", [P, GN, TOK], F32R) as c.qparts, \
            nc.sbuf_tensor("kparts", [P, GN, TOK], F32R) as c.kparts:
        pass
    c.qT = sb("qT", [P, FT, TOK])
    with nc.sbuf_tensor("disp", [P, 2, TILES, CAP], F32R) as c.disp:
        pass
    c.kT = sb("kT", [P, FT, TOK])
    c.v = sb("v_tok", [P, NT, INNER])
    c.oT = sb("oT", [P, FT, TOK])
    c.roped = sb("roped", [P, 2, INNER])
    c.rot = sb("rot_tmp", [P, HEADS, ROT])
    c.probsT = sb("probsT", [P, 8, 2 * S])
    c.probs = c.roped[:, :, :].rearrange("p j (r t k) -> p (j r) t k", r=2, t=QT)
    c.whole, c.low = (c.roped[:, j, :].rearrange("p (i n) -> p i n", i=2) for j in range(2))
    c.parts = sb("parts", [P, 4])
    c.b3low = sb("b3low", [P, 2, GN])
    c.ones = sb("ones", [P, PAD])
    c.inv = c.rot[:, :, :].rearrange("p h r -> p (h r)")[:, 0:S]
    c.mx = sb("row_max", [P, 3, QT])
    c.nmx = sb("neg_max", [P, 3, QT])
    c.rsum = sb("row_sum", [P, 3, QT])
    c.rinv = sb("row_inv", [P, 3, QT])
    c.len_i = sb("len_i", [P, NB], I32)
    c.len_f = sb("len_f", [P, NB])
    c.mask_u8 = sb("mask_u8", [P, NB, S], U8)
    c.mask_i32 = sb("mask_i32", [P, NT, S], I32)
    c.m_len = sb("m_len", [P, NB, S])
    c.m_causal = sb("m_causal", [P, QT, S])
    c.pick = c.m_causal[0:E3, :, :].rearrange("p t k -> p (t k)").bitcast(BF16).rearrange("p (e n) -> p e n", e=E3)
    c.m_key = sb("m_key", [P, NB, S])
    c.m_full = c.mask_i32[:, :, :].bitcast(F32)
    c.raw = c.v[:, 0, :].rearrange("p (j n) -> p j n", n=P)
    c.rows = c.v[0:7 + E1 + 1 + 3 * FF // P, 1, 0:D]
    c.brows, c.bspread = c.v[0:3, 2, 0:D], c.v[0:3, 3, 0:GN * P]
    c.w0 = sb("w0_pad", [P, GN * P])
    c.w0r = sb("w0_rep", [P, GN * P])
    c.wr0 = sb("wr0", [P, 8])
    c.w1_0 = sb("w1_0", [P, FF])
    c.w2_0 = sb("w2_0", [P, FF // P, D])
    c.b2_0 = sb("b2_0", [P, D])
    c.wr1 = sb("wr1", [P, E1])
    c.br1 = sb("br1", [P, E1])
    c.ew1 = sb("ew1", [P, E1 + 1, D])
    c.ew2 = sb("ew2", [P, E1 + 1, D])
    c.eb2 = sb("eb2", [E1 + 1, D])
    c.wa = sb("w_attn", [P, 2, 4 * INNER])
    c.wff1 = sb("wff1", [P, FF])
    c.wff2 = sb("wff2", [P, FF // P, D])
    c.bff2 = sb("bff2", [P, D])
    c.bo2 = sb("bo2", [P, 4, D])
    cols = sb("columns", [P, 7 + E1 + 1 + 3 * FF // P])
    c.cols, at = cols, 0
    c.nw, at = cols[:, at:at + 7], at + 7
    c.eb1, at = cols[:, at:at + E1 + 1], at + E1 + 1
    c.b1_0, at = cols[:, at:at + FF // P], at + FF // P
    c.bff1 = cols[:, at:at + 2 * FF // P].rearrange("p (l f) -> p l f", l=2)
    c.proj = sb("proj", [P, D])
    c.projb = sb("projb", [P, D])
    c.signT = sb("signT", [P, D])
    c.neg = sb("neg", [P, D])
    c.w3 = sb("w3_pad", [P, 3, GN * P])
    c.b3 = sb("b3_pad", [P, 3, GN])
    c.wo3 = sb("wo3_pad", [P, GN, D])
    c.bo3 = sb("bo3", [P, D])
    c.lg = sb("logits", [P, TILES, 16])
    c.ex = sb("router_exp", [P, TILES, 16])
    c.rm = sb("router_max", [P, TILES])
    c.rs = sb("router_sum", [P, TILES])
    c.pr = sb("router_probs", [P, TILES, 16])
    c.top = sb("router_top", [P, TILES, 8])
    c.rest = sb("router_rest", [P, TILES, 16])
    c.sel = sb("router_sel", [P, TILES, 16])
    c.cw = sb("router_w", [P, TILES, 16])
    c.cwT = sb("router_wT", [16, TOK])
    c.acc = sb("acc", [P, NT, D])
    c.wr3 = sb("wr3", [P, E3])
    c.selb = sb("sel_bf", [P, TILES, E3], BF16)
    c.before = sb("sel_before", [P, TILES, E3], BF16)
    c.x3 = sb("x3", [P, TILES, D])
    c.ps = [ctx.enter_context(nc.psum_tensor(f"bank{i}", [P, 512], F32)) for i in range(8)]
    return c


class Chain:

    def __init__(self, eng, sem):
        self.eng, self.sem, self.n = eng, sem, 0

    def mark(self, ins):
        self.n += 1
        ins.then_inc(self.sem, 1)

    def link(self, ins):
        self.mark(ins)
        self.eng.wait_ge(self.sem, self.n)



def stage_setup(nc, c, A):
    n_rows = c.cols.shape[1]
    with ExitStack() as ctx:
        loaded, consts, wt, wt_free, turned, chain_v, chain_g = c.semaphores(nc, (
                "su_loaded", "su_consts", "su_transposed", "su_spread", "su_bank_free", "su_dve", "su_pool"))
        loads = [0]
        block = ctx.enter_context(nc.Block())

        @block.sync
        def _(sp):
            def load(dst, src):
                sp.dma_start(dst, src).then_inc(loaded, 16)
                loads[0] += 16
            raw = c.raw
            load(raw[:, 0, :], A["L0_xattn_Wq"])
            load(raw[:, 1, :], A["L3_xattn_Wq"])
            load(raw[:, 2, :], A["L3_xattn_Wk"])
            load(raw[:, 3, :], A["L3_xattn_Wv"])
            load(raw[:, 4, :], A["L3_xattn_Wo"])
            load(raw[:, 5, :], A["L2_ffn_weight"])
            load(raw[0:8, 6, :], A["L0_ffn_Wr"])
            load(raw[0:8, 7, :], A["L3_ffn_router_w"])
            load(c.gate[:, 0:4], A["g_xattn"].partition_broadcast(P))
            load(c.gate[:, 4:8], A["g_ffn"].partition_broadcast(P))
            load(c.parts[:, :], A["part_table"])
            for j, n in enumerate(("bq", "bk", "bv")):
                load(c.brows[j:j + 1, :], A["L3_xattn_" + n].rearrange("(a n) -> a n", a=1))
            at = 0
            for src in (A["L2_xattn_attn_norm_w"], A["L2_xattn_cross_norm_w"], A["L2_xattn_ff_norm_w"],
                        A["L2_xattn_norm_out_w"].rearrange("(a n) -> a n", a=1),
                        A["L1_ffn_eb1"], A["L1_ffn_sb1"].rearrange("(a n) -> a n", a=1),
                        A["L0_ffn_b1"][7].rearrange("(a n) -> a n", n=D),
                        A["L2_xattn_ff_b1"].rearrange("l (a n) -> (l a) n", n=D)):
                load(c.rows[at:at + src.shape[0], :], src)
                at += src.shape[0]
            sp.wait_ge(loaded, loads[0])

        @block.gpsimd
        def _(pool):
            g = Chain(pool, chain_g)
            g.mark(pool.memset(c.ident[:, :], 0.0))
            g.mark(pool.memset(c.ident_bf[:, :], 0.0))
            g.mark(pool.memset(c.tri_bf[:, :], 1.0))
            g.mark(pool.memset(c.m_causal[:, :, :], 0.0))
            g.mark(pool.memset(c.ones[:, :], 1.0))
            g.link(pool.memset(c.ones_bf[:, :], 1.0))
            for m in (c.ident, c.ident_bf):
                pool.affine_select(out=m[:, :], in_=m[:, :], compare_op=ALU.not_equal, fill=1.0, base=0,
                                   pattern=[[-1, P]], channel_multiplier=1).then_inc(consts, 1)
            pool.affine_select(out=c.tri_bf[:, :], in_=c.tri_bf[:, :], compare_op=ALU.is_ge, fill=0.0, base=0,
                               pattern=[[1, P]], channel_multiplier=-1)
            pool.affine_select(out=c.m_causal[:, :, :], in_=c.m_causal[:, :, :], compare_op=ALU.is_ge, fill=MASKED,
                               base=0, pattern=[[P, QT], [-1, S]], channel_multiplier=1)
            pool.iota(c.iota[:, :], pattern=[[1, S]], base=0, channel_multiplier=0,
                      allow_small_or_imprecise_dtypes=True)
            pool.iota(c.slot[:, :], pattern=[[P, 2]], base=0, channel_multiplier=1,
                      allow_small_or_imprecise_dtypes=True)

        @block.tensor
        def _(pe):
            pe.wait_ge(consts, 2)
            pe.wait_ge(loaded, loads[0])
            for j in range(8):
                n = P if j < 6 else 8
                pe.transpose(c.ps[j][:, 0:n], c.raw[0:n, j, :], c.ident[0:n, 0:n]).then_inc(wt, 1)
            pe.wait_ge(wt_free, 2)
            pe.wait_ge(turned, 1)
            for g in range(GN):
                pe.transpose(c.ps[4][:, g * P:(g + 1) * P], c.oT[:, 0, g * P:(g + 1) * P],
                             c.ident[:, :]).then_inc(wt, 1)
                pe.transpose(c.ps[5][:, g * 3:(g + 1) * 3], c.bspread[:, g * P:(g + 1) * P],
                             c.ident[0:3, 0:3]).then_inc(wt, 1)
            pe.transpose(c.ps[6][:, 0:n_rows], c.rows[:, :], c.ident[0:n_rows, 0:n_rows]).then_inc(wt, 1)

        @block.vector
        def _(dve):
            v = Chain(dve, chain_v)
            v.mark(dve.memset(c.w0[:, :], 0.0))
            v.mark(dve.memset(c.w3[:, :, :], 0.0))
            v.link(dve.memset(c.oT[:, 0, :], 0.0))
            dve.wait_ge(loaded, loads[0])

            def spread(dst, src):
                return dve.tensor_copy(dst.rearrange("p (h d) -> p h d", d=PAD)[:, :, 0:DK],
                                       src.rearrange("p (h d) -> p h d", d=DK))
            spread(c.oT[:, 0, :], c.raw[:, 4, :]).then_inc(wt_free, 1)
            dve.tensor_copy(c.bspread.rearrange("p (h r d) -> p h r d", r=PAD // DK, d=DK),
                            c.brows.rearrange("p (h a d) -> p h a d", a=1, d=DK)
                            .to_broadcast([3, D // DK, PAD // DK, DK])).then_inc(wt_free, 1)
            dve.wait_ge(wt, 8)
            spread(c.w0[:, :], c.ps[0][:, 0:P])
            spread(c.w3[:, 2, :], c.ps[3][:, 0:P])
            for r in range(PAD // DK):
                for dst, src in ((c.w0r[:, :], c.ps[0]), (c.w3[:, 0, :], c.ps[1]), (c.w3[:, 1, :], c.ps[2])):
                    dve.tensor_copy(dst.rearrange("p (h r d) -> p h r d", r=PAD // DK, d=DK)[:, :, r, :],
                                    src[:, 0:P].rearrange("p (h d) -> p h d", d=DK))
            v.mark(dve.tensor_scalar(c.signT[:, :], c.ps[5][:, 0:P], 0.0, None, ALU.is_gt))
            v.link(dve.tensor_scalar(c.neg[:, :], c.ps[5][:, 0:P], 0.0, None, ALU.is_lt))
            dve.tensor_tensor(c.signT[:, :], c.signT[:, :], c.neg[:, :], ALU.subtract)
            dve.tensor_copy(c.wr0[:, :], c.ps[6][:, 0:8])
            dve.tensor_copy(c.wr3[:, :], c.ps[7][:, 0:8]).then_inc(turned, 1)
            dve.wait_ge(wt, 8 + 2 * GN + 1)
            v.link(dve.tensor_copy(c.b3[:, :, :].rearrange("p j g -> p g j"),
                                   c.ps[5][:, 0:3 * GN].rearrange("p (g j) -> p g j", j=3)))
            dve.tensor_copy(c.cols[:, :], c.ps[6][:, 0:n_rows])
            for j in range(2):
                dve.tensor_scalar(c.b3low[:, j, :], c.b3[:, j, :], c.parts[:, 2 * j:2 * j + 1], None, ALU.mult)
            dve.tensor_copy(c.wo3[:, :, :], c.ps[4][:, 0:GN * P].rearrange("p (g n) -> p g n", g=GN))

        @block.scalar
        def _(act):
            act.wait_ge(loaded, loads[0])
            act.activation(c.gate[:, :], c.gate[:, :], ACT.Tanh)
            later = []

            def keep(dst, src):
                act.dma_start(dst, src).then_inc(c.constants, 16)
                later.append(dst)
            keep(c.w1_0[:, :], A["L0_ffn_W1"][7])
            keep(c.w2_0[:, :, :], A["L0_ffn_W2"][7].rearrange("(t p) n -> p t n", p=P))
            keep(c.b2_0[:, :], A["L0_ffn_b2"][7].partition_broadcast(P))
            keep(c.wr1[:, :], A["L1_ffn_router_W"])
            keep(c.br1[:, :], A["L1_ffn_router_b"].partition_broadcast(P))
            keep(c.ew1[:, 0:E1, :], A["L1_ffn_eW1"].rearrange("e p n -> p e n"))
            keep(c.ew1[:, E1, :], A["L1_ffn_sW1"])
            keep(c.ew2[:, 0:E1, :], A["L1_ffn_eW2"].rearrange("e p n -> p e n"))
            keep(c.ew2[:, E1, :], A["L1_ffn_sW2"])
            keep(c.eb2[0:E1, :], A["L1_ffn_eb2"])
            keep(c.eb2[E1:E1 + 1, :], A["L1_ffn_sb2"].rearrange("(a n) -> a n", a=1))
            keep(c.rope[:, :, :], A["rope_table"].rearrange("(t p) n -> p t n", p=P))
            for l in range(2):
                keep(c.bo2[:, 2 * l, :], A["L2_xattn_bo"][l].partition_broadcast(P))
                keep(c.bo2[:, 2 * l + 1, :], A["L2_xattn_cbo"][l].partition_broadcast(P))
            keep(c.proj[:, :], A["L2_xattn_proj_w"])
            keep(c.projb[:, :], A["L2_xattn_proj_b"].partition_broadcast(P))
            keep(c.bo3[:, :], A["L3_xattn_bo"].partition_broadcast(P))
            c.n_constants = 16 * len(later)


def stage_load(nc, c, A, half, norm):
    with ExitStack() as ctx:
        loaded, loaded_x, loaded_ctx, tr, turned, chain_v, lenf, *nsems = c.semaphores(nc, (
            "ld_masks", "ld_x", "ld_ctx", "ld_transposed", "ld_copied", "ld_dve", "ld_len") + Norm.NAMES)
        norm.take(nsems)
        block = ctx.enter_context(nc.Block())

        @block.sync
        def _(sp):
            def rows(a):
                return a.rearrange("b (t p) f -> p (b t) f", p=P)[:, bass.ds(half * NT, NT), :]
            sp.dma_start(c.x[:, :, :], rows(A["x"])).then_inc(loaded_x, 16)
            sp.dma_start(c.ctx[:, :, :], rows(A["ctx_1024"])).then_inc(loaded_ctx, 16)
            sp.dma_start(c.len_i[:, :], A["_lenS2"][bass.ds(half * NB, NB)].partition_broadcast(P)).then_inc(loaded, 16)
            sp.dma_start(c.mask_u8[:, :, :],
                         A["mask_BxS_bf1"][bass.ds(half * NB, NB), :].partition_broadcast(P)).then_inc(loaded, 16)
            sp.dma_start(c.mask_i32[:, :, :],
                         A["mask_Bx1xSxS2_if1"].rearrange("b a (t p) k -> p (b a t) k", p=P)[:, bass.ds(half * NT, NT), :]
                         ).then_inc(loaded, 16)
            sp.wait_ge(loaded, 48)

        @block.tensor
        def _(pe):
            pe.wait_ge(loaded_ctx, 16)
            for t in range(NT):
                pe.transpose(c.ps[0][:, t * P:(t + 1) * P], c.ctx[:, t, :], c.ident[:, :]).then_inc(tr, 1)
            pe.wait_ge(turned, 1)
            norm.pe(pe, c)

        @block.scalar
        def _(act):
            act.wait_ge(tr, NT)
            act.copy(c.ctxT[:, :], c.ps[0][:, :]).then_inc(turned, 1)
            norm.act(act, c)

        @block.vector
        def _(dve):
            v = Chain(dve, chain_v)
            dve.wait_ge(loaded_x, 16)
            for t in range(NT):
                v.mark(dve.bn_stats(c.stats[:, t, :], c.x[:, t, :]))
            norm.dve(dve, v, c)
            dve.wait_ge(loaded, 48)
            dve.tensor_copy(c.len_f[:, :], c.len_i[:, :]).then_inc(lenf, 1)
            dve.wait_ge(lenf, 1)
            for b in range(NB):
                dve.tensor_scalar(c.m_len[:, b, :], c.iota[:, :], c.len_f[:, b:b + 1], MASKED, ALU.is_ge, ALU.mult)
            dve.tensor_scalar(c.m_key[:, :, :], c.mask_u8[:, :, :], 0.0, MASKED, ALU.is_equal, ALU.mult)
            dve.tensor_scalar(c.m_full[:, :, :], c.mask_i32[:, :, :], 0.0, MASKED, ALU.is_equal, ALU.mult)



def rsqrt_steps(dve, v, c, n):
    ms, r, t, q = c.msq[:, 0:n], c.rstd[:, 0:n], c.newton[:, 0:n], c.scaled[:, 0:n]
    v.link(dve.tensor_scalar(r.bitcast(I32), ms.bitcast(I32), -0.5, float(0x5F1FFFF9), ALU.mult, ALU.add))
    v.link(dve.tensor_tensor(t, r, r, ALU.mult))
    v.link(dve.scalar_tensor_tensor(out=t, in0=t, scalar=-0.703952253, in1=ms, op0=ALU.mult, op1=ALU.mult))
    v.link(dve.scalar_tensor_tensor(out=r, in0=t, scalar=0.703952253 * 2.38924456, in1=r, op0=ALU.add, op1=ALU.mult))
    v.mark(dve.tensor_scalar(q, r, 0.375, None, ALU.mult))
    v.link(dve.tensor_tensor(t, r, r, ALU.mult))
    v.link(dve.tensor_tensor(t, t, ms, ALU.mult))
    v.link(dve.scalar_tensor_tensor(out=t, in0=t, scalar=-10.0 / 3.0, in1=t, op0=ALU.add, op1=ALU.mult))
    v.link(dve.scalar_tensor_tensor(out=r, in0=t, scalar=5.0, in1=q, op0=ALU.add, op1=ALU.mult))


def norm_steps(dve, v, c, src, dst, n, kind, ready, stats=True):
    if stats:
        for t in range(n):
            v.mark(dve.bn_stats(c.stats[:, t, :], src[:, t, :]))
    dve.wait_ge(v.sem, v.n)
    for t in range(n):
        v.mark(dve.bn_aggr(c.mv[:, t, :], c.stats[:, t, :]))
    dve.wait_ge(v.sem, v.n)
    mean, var, ms = c.mv[:, 0:n, 0], c.mv[:, 0:n, 1], c.msq[:, 0:n]
    if kind == "layer":
        v.link(dve.tensor_scalar(ms, var, 1e-5, None, ALU.add))
    else:
        v.link(dve.tensor_tensor(ms, mean, mean, ALU.mult))
        v.link(dve.tensor_tensor(ms, ms, var, ALU.add))
        if kind == "rms":
            v.link(dve.tensor_scalar(ms, ms, 1e-16, None, ALU.max))
        else:
            v.link(dve.tensor_scalar(ms, ms, 1.1920929e-07, None, ALU.add))
    rsqrt_steps(dve, v, c, n)
    for t in range(n):
        if kind == "layer":
            dve.tensor_scalar(dst[:, t, :], src[:, t, :], c.mv[:, t, 0:1], c.rstd[:, t:t + 1],
                              ALU.subtract, ALU.mult).then_inc(ready, 1)
        else:
            dve.tensor_scalar(dst[:, t, :], src[:, t, :], c.rstd[:, t:t + 1], None, ALU.mult).then_inc(ready, 1)


class Values:
    NAMES = ("va_done", "va_copied")

    def __init__(self, w, cols, loaded=None):
        self.w, self.loaded = w, loaded
        self.jobs = [(t, m * TOK) for t in range(NT) for m in range(cols // TOK)]

    def take(self, sems):
        self.done, self.copied = sems

    def pe(self, pe, c, first, last):
        if first == 0 and self.loaded:
            pe.wait_ge(*self.loaded)
        for i in range(first, last):
            t, m = self.jobs[i]
            if i >= 2:
                pe.wait_ge(self.copied, i - 1)
            pe.matmul(c.ps[4 + i % 2][:, :], c.ctxT[:, t * P:(t + 1) * P], self.w[:, m:m + TOK],
                      start=True, stop=True).then_inc(self.done, 1)

    def act(self, act, c, first, last):
        for i in range(first, last):
            t, m = self.jobs[i]
            act.wait_ge(self.done, i + 1)
            act.copy(c.v[:, t, m:m + TOK], c.ps[4 + i % 2][:, :]).then_inc(self.copied, 1)


class Norm:
    NAMES = ("nm_ready", "nm_inner", "nm_transposed") + Values.NAMES

    def __init__(self, src, kind, weight=None, inner=False, values=None):
        self.src, self.kind, self.weight, self.inner, self.values = src, kind, weight, inner, values
        self.early = len(values.jobs) * 3 // 4 if values else 0

    def take(self, sems):
        self.ready, self.ready_u, self.turned, *rest = sems
        if self.values:
            self.values.take(rest)

    def dve(self, dve, v, c):
        s = self.src
        if self.inner:
            norm_steps(dve, v, c, s, c.u, NT, "layer", self.ready_u, stats=False)
            dve.wait_ge(self.ready_u, NT)
            s = c.u
        norm_steps(dve, v, c, s, c.y, NT, self.kind, self.ready, stats=self.inner)

    def pe(self, pe, c, idle=6):
        if self.values:
            self.values.pe(pe, c, 0, self.early)
        else:
            keep_clock(pe, c, c.ps[idle], NORM_FILL)
        for t in range(NT):
            pe.wait_ge(self.ready, t + 1)
            pe.transpose(c.ps[6 + t // 2][:, (t % 2) * P:(t % 2 + 1) * P], c.y[:, t, :],
                         c.ident[:, :]).then_inc(self.turned, 1)
        if self.values:
            self.values.pe(pe, c, self.early, len(self.values.jobs))

    def act(self, act, c):
        if self.values:
            self.values.act(act, c, 0, self.early)
        for j in range(NT // 2):
            act.wait_ge(self.turned, 2 * j + 2)
            act.activation(c.xT[:, j * 2 * P:(j + 1) * 2 * P], c.ps[6 + j][:, 0:2 * P], ACT.Copy,
                           scale=1.0 if self.weight is None else self.weight)
        if self.values:
            self.values.act(act, c, self.early, len(self.values.jobs))


def residual_stats(dve, v, c, res, t, at):
    dve.wait_ge(v.sem, at)
    v.mark(dve.bn_stats(c.stats[:, t, :], res[:, t, :]))


def keep_clock(pe, c, bank, n):
    for _ in range(n):
        pe.matmul(bank[:, 0:S], c.ones_bf[:, :], c.fill_bf[:, 0:S], start=True, stop=True)


def background_loads(block, fetch, awaited):
    @block.sync
    def _(sp):
        for dst, src, sem in fetch:
            sp.dma_start(dst, src).then_inc(sem, 16)
        for sem, n in awaited:
            sp.wait_ge(sem, n)



def stage_narrow_qkv(nc, c, wq, wk, bias, fetch=(), awaited=()):
    with ExitStack() as ctx:
        done, freed, whole, low, high, joined = c.semaphores(nc, (
            "nq_done", "nq_freed", "nq_whole", "nq_low", "nq_high", "nq_joined"))
        block = ctx.enter_context(nc.Block())
        background_loads(block, fetch, awaited)
        jobs = [(c.kparts, wk, c.ctxT, 1, g) for g in range(GN)] + [(c.qparts, wq, c.xT, 0, g) for g in range(GN)]

        @block.tensor
        def _(pe):
            for i, (_, w, x, _, g) in enumerate(jobs):
                pe.matmul(c.ps[i][:, :], w[:, g * P:(g + 1) * P], x[:, :], start=True, stop=True).then_inc(done, 1)
            pe.wait_ge(freed, 1)
            keep_clock(pe, c, c.ps[0], TAIL_FILL)

        @block.scalar
        def _(act):
            for i, (dst, _, _, j, g) in enumerate(jobs):
                act.wait_ge(done, i + 1)
                if i >= 2:
                    act.wait_ge(joined, i - 1)
                b = 0.0 if bias is None else bias[:, j, g:g + 1]
                bl = 0.0 if bias is None else c.b3low[:, j, g:g + 1]
                act.activation(c.whole[:, i % 2, :], c.ps[i][:, :], ACT.Identity, bias=b).then_inc(whole, 1)
                act.activation(c.low[:, i % 2, :], c.ps[i][:, :], ACT.Identity, bias=bl,
                               scale=c.parts[:, 2 * j:2 * j + 1]).then_inc(freed, 1)

        @block.vector
        def _(dve):
            for i, (dst, _, _, j, g) in enumerate(jobs):
                dve.wait_ge(whole, i + 1)
                w = c.whole[:, i % 2, :].bitcast(I32)
                dve.tensor_scalar(w, w, HIGH_BITS, None, ALU.bitwise_and).then_inc(high, 1)
                dve.wait_ge(high, i + 1)
                dve.wait_ge(freed, i + 1)
                dve.scalar_tensor_tensor(out=dst[:, g, :], in0=c.whole[:, i % 2, :], scalar=c.parts[:, 2 * j + 1:2 * j + 2],
                                         in1=c.low[:, i % 2, :], op0=ALU.mult, op1=ALU.add).then_inc(joined, 1)


def stage_wide_qkv(nc, c, w, cross, fetch=()):
    kv = c.ctxT if cross else c.xT
    wq, wk, wv = (w[:, j * INNER:(j + 1) * INNER] for j in range(3))
    with ExitStack() as ctx:
        proj, passed, vdone, roped, rchain, tr, tfree = c.semaphores(nc, (
            "wq_proj", "wq_passed", "wq_vcopied", "wq_roped", "wq_dve", "wq_transposed", "wq_tfree"))
        block = ctx.enter_context(nc.Block())
        background_loads(block, fetch, ())
        units = [(j, t) for t in range(NT) for j in range(2)]
        n = len(units)

        @block.tensor
        def _(pe):
            for i in range(n + 1):
                if i < n:
                    j, t = units[i]
                    x = kv if j else c.xT
                    if i >= 2:
                        pe.wait_ge(roped, i - 1)
                        pe.wait_ge(passed, i - 1)
                    for m in range(2):
                        mm = pe.matmul(c.ps[2 * (i % 2) + m][:, :], x[:, t * P:(t + 1) * P],
                                       (wk if j else wq)[:, m * 512:(m + 1) * 512], start=True, stop=True)
                    mm.then_inc(proj, 1)
                    if j and not cross:
                        if t:
                            pe.wait_ge(vdone, t)
                        for m in range(2):
                            mm = pe.matmul(c.ps[6 + m][:, :], kv[:, t * P:(t + 1) * P], wv[:, m * 512:(m + 1) * 512],
                                           start=True, stop=True)
                        mm.then_inc(proj, 1)
                if i >= 1:
                    k = i - 1
                    pe.wait_ge(roped, k + 1)
                    pe.wait_ge(passed, k + 1)
                    for m in range(2):
                        if 2 * k + m >= 2:
                            pe.wait_ge(tfree, 2 * k + m - 1)
                        for f in range(4):
                            mm = pe.transpose(c.ps[4 + m][:, f * P:(f + 1) * P],
                                              c.roped[:, k % 2, (4 * m + f) * P:(4 * m + f + 1) * P], c.ident[:, :])
                        mm.then_inc(tr, 1)
            keep_clock(pe, c, c.ps[0], TAIL_FILL)

        @block.scalar
        def _(act):
            def transposed_out(k):
                j, t = units[k]
                for m in range(2):
                    act.wait_ge(tr, 2 * k + m + 1)
                    act.copy((c.kT if j else c.qT)[:, 4 * m:4 * m + 4, t * P:(t + 1) * P],
                             c.ps[4 + m][:, :].rearrange("p (f n) -> p f n", f=4)).then_inc(tfree, 1)
            for i in range(n + 1):
                if i < n:
                    j, t = units[i]
                    act.wait_ge(proj, i + 1 if cross else i + t + 1)
                    if i >= 2:
                        act.wait_ge(tr, 2 * i - 2)
                    for m in range(2):
                        act.wait_ge(rchain, 6 * i + 3 * (m + 1))
                        cp = act.copy(c.roped[:, i % 2, m * 512:(m + 1) * 512]
                                      .rearrange("p (h d) -> p h d", d=DH)[:, :, ROT:DH],
                                      c.ps[2 * (i % 2) + m][:, :].rearrange("p (h d) -> p h d", d=DH)[:, :, ROT:DH])
                    cp.then_inc(passed, 1)
                    if j and not cross:
                        act.wait_ge(proj, i + t + 2)
                        for m in range(2):
                            cp = act.copy(c.v[:, t, m * 512:(m + 1) * 512], c.ps[6 + m][:, :])
                        cp.then_inc(vdone, 1)
                if i >= 1:
                    transposed_out(i - 1)

        @block.vector
        def _(dve):
            v = Chain(dve, rchain)
            half = ROT // 2
            for i, (j, t) in enumerate(units):
                dve.wait_ge(proj, i + 1 if cross else i + t + 1)
                if i >= 2:
                    dve.wait_ge(tr, 2 * i - 2)
                if i >= 1:
                    dve.wait_ge(roped, i)
                cos = c.rope[:, t % QT, 0:ROT]
                sin = c.rope[:, t % QT, ROT:2 * ROT]

                def over_heads(a):
                    return a.rearrange("p (h d) -> p h d", h=1).to_broadcast([P, HEADS // 2, a.shape[-1]])
                for m in range(2):
                    src = c.ps[2 * (i % 2) + m][:, :].rearrange("p (h d) -> p h d", d=DH)
                    dst = c.roped[:, i % 2, m * 512:(m + 1) * 512].rearrange("p (h d) -> p h d", d=DH)
                    tmp = c.rot[:, m * 8:(m + 1) * 8, :]
                    v.mark(dve.tensor_tensor(dst[:, :, 0:ROT], src[:, :, 0:ROT], over_heads(cos), ALU.mult))
                    v.mark(dve.tensor_tensor(tmp[:, :, 0:half], src[:, :, half:ROT], over_heads(sin[:, 0:half]),
                                             ALU.mult))
                    v.mark(dve.tensor_tensor(tmp[:, :, half:ROT], src[:, :, 0:half], over_heads(sin[:, half:ROT]),
                                             ALU.mult))
                dve.wait_ge(v.sem, v.n)
                full = c.roped[:, i % 2, :].rearrange("p (h d) -> p h d", d=DH)[:, :, 0:ROT]
                dve.tensor_tensor(full, full, c.rot[:, :, :], ALU.add).then_inc(roped, 1)


def stage_heads(nc, c, units, per_group, scale, out_bias=None, late=False):
    n = len(units)
    split = per_group // 2
    ring = c.probsT.shape[1]
    with ExitStack() as ctx:
        scored, mchain, biased, exped, inverted, normed, turned, copied, mixed, out_free = c.semaphores(nc, (
            "hd_scored", "hd_max", "hd_negmax", "hd_exp", "hd_inverted", "hd_normed", "hd_turned", "hd_copied",
            "hd_mixed", "hd_outfree"))
        block = ctx.enter_context(nc.Block())
        scores = [c.ps[i] for i in range(NS)]
        turns = [c.ps[NS + i] for i in range(NTB)]
        outs = [c.ps[6 + i] for i in range(2)]

        @block.tensor
        def _(pe):
            for i in range(n + MIX_LAG + split):
                if i < n:
                    q, k, _, _, _, _ = units[i]
                    if i >= NS:
                        pe.wait_ge(exped, 2 * (i - NS + 1))
                    for t in range(QT):
                        mm = pe.matmul(scores[i % NS][:, t * S:(t + 1) * S], q(t), k, start=True, stop=True)
                    mm.then_inc(scored, 1)
                if i < TURN_LAG:
                    keep_clock(pe, c, outs[1], FILL)
                if 0 <= i - TURN_LAG < n:
                    j = i - TURN_LAG
                    pe.wait_ge(exped if late else normed, QT * (j + 1))
                    if j >= NTB:
                        pe.wait_ge(copied, j - NTB + 1)
                    for kt in range(QT):
                        for t in range(QT):
                            mm = pe.transpose(turns[j % NTB][:, kt * S + t * P:kt * S + (t + 1) * P],
                                              c.probs[:, j % 4, t, kt * P:(kt + 1) * P], c.ident[:, :])
                    mm.then_inc(turned, 1)
                for step in range(2):
                    j = i - MIX_LAG - step * split
                    if j < 0 or j >= n or j % per_group != per_group - 1:
                        continue
                    g = j // per_group
                    if step == 0:
                        pe.wait_ge(copied, j + 1)
                        if g >= 2:
                            pe.wait_ge(out_free, g - 1)
                    at = slice(S, 2 * S) if late and step else slice(0, S)
                    for kt in range(QT) if late else (step,):
                        for u in range(g * per_group, (g + 1) * per_group):
                            _, _, v, rows, _, _ = units[u]
                            mm = pe.matmul(outs[g % 2][rows, at], c.ones[:, :] if late and step else v(kt),
                                           c.probsT[:, u % ring, kt * S:(kt + 1) * S],
                                           start=(kt == 0), stop=(kt == QT - 1))
                    if step:
                        mm.then_inc(mixed, 1)

        @block.vector
        def _(dve):
            for i in range(n + OUT_LAG + split + (per_group - 1 if late else 0)):
                if i < n:
                    mask = units[i][4]
                    dve.wait_ge(scored, i + 1)
                    if i >= 3:
                        dve.wait_ge(exped, 2 * (i - 2))
                    if mask is None:
                        dve.tensor_reduce(c.mx[:, i % 3, :], scores[i % NS][:, :].rearrange("p (t k) -> p t k", t=QT),
                                          AX.X, ALU.max).then_inc(mchain, QT)
                    else:
                        for t in range(QT):
                            s = scores[i % NS][:, t * S:(t + 1) * S]
                            dve.tensor_tensor_reduce(s, s, mask(t), 1.0, LOWEST, ALU.add, ALU.max,
                                                     c.mx[:, i % 3, t:t + 1]).then_inc(mchain, 1)
                j = i - NORM_LAG
                if 0 <= j < n and not late:
                    dve.wait_ge(exped, 2 * (j + 1))
                    dve.reciprocal(c.rinv[:, j % 3, :], c.rsum[:, j % 3, :]).then_inc(inverted, 1)
                o = i - OUT_LAG - split - (per_group - 1)
                if late and o >= 0:
                    g, piece = o // per_group, o % per_group
                    at = slice(piece * S // per_group, (piece + 1) * S // per_group)
                    if piece == 0:
                        dve.wait_ge(mixed, g + 1)
                        if g:
                            dve.wait_ge(out_free, g)
                    dve.reciprocal(c.inv[:, at], outs[g % 2][:, S:2 * S][:, at]).then_inc(inverted, 1)
                if i < n:
                    dve.wait_ge(mchain, QT * (i + 1))
                    dve.tensor_scalar(c.nmx[:, i % 3, :], c.mx[:, i % 3, :], -scale, None, ALU.mult).then_inc(biased, 1)
                if 0 <= j < n and not late:
                    dve.wait_ge(inverted, j + 1)
                    for t in range(QT):
                        dve.tensor_scalar(c.probs[:, j % 4, t, :], c.probs[:, j % 4, t, :], c.rinv[:, j % 3, t:t + 1],
                                          None, ALU.mult).then_inc(normed, 1)
                j = i - OUT_LAG - split
                if late and o % per_group == per_group - 1 and o >= 0:
                    g, dst = o // per_group, units[o][5]
                    dve.wait_ge(inverted, o + 1)
                    dve.tensor_tensor(dst, outs[g % 2][:, 0:S], c.inv[:, :], ALU.mult).then_inc(out_free, 1)
                    if out_bias is not None:
                        dve.wait_ge(out_free, g + 1)
                        dve.tensor_scalar(dst, dst, out_bias(g), None, ALU.add)
                if not late and j >= 0 and j % per_group == per_group - 1:
                    g = j // per_group
                    dve.wait_ge(mixed, g + 1)
                    dve.tensor_copy(units[j][5], outs[g % 2][:, 0:S]).then_inc(out_free, 1)

        @block.scalar
        def _(act):
            for i in range(n + TURN_LAG):
                if i < n:
                    act.wait_ge(biased, i + 1)
                    if i >= 4:
                        act.wait_ge(turned, i - 3)
                    if i >= 3 and not late:
                        act.wait_ge(inverted, i - 2)
                    for t in range(QT):
                        act.activation(c.probs[:, i % 4, t, :], scores[i % NS][:, t * S:(t + 1) * S], ACT.Exp,
                                       bias=c.nmx[:, i % 3, t:t + 1], scale=scale,
                                       accum_out=None if late else c.rsum[:, i % 3, t:t + 1]).then_inc(exped, 1)
                j = i - TURN_LAG
                if j >= 0:
                    act.wait_ge(turned, j + 1)
                    if j >= ring:
                        act.wait_ge(mixed, (j - ring) // per_group + 1)
                    act.copy(c.probsT[:, j % ring, :], turns[j % NTB][:, :]).then_inc(copied, 1)


def narrow_units(c, mask):
    def unit(b, h):
        g, r = h // 4, PAD * (h % 4)
        return (lambda t: c.qparts[r:r + PAD, g, (b * QT + t) * P:(b * QT + t + 1) * P],
                c.kparts[r:r + PAD, g, b * S:(b + 1) * S],
                lambda kt: c.v[:, b * QT + kt, g * P + r:g * P + r + PAD],
                slice(r, r + PAD), lambda t: mask(b, t), c.oT[:, g, b * S:(b + 1) * S])
    return [unit(b, h) for b in range(NB) for h in range(HEADS)]


def wide_units(c, mask):
    def unit(b, h):
        g, r = h // 2, DH * (h % 2)
        return (lambda t: c.qT[r:r + DH, g, (b * QT + t) * P:(b * QT + t + 1) * P],
                c.kT[r:r + DH, g, b * S:(b + 1) * S],
                lambda kt: c.v[:, b * QT + kt, h * DH:(h + 1) * DH],
                slice(r, r + DH), mask and (lambda t: mask(b, t)), c.oT[:, g, b * S:(b + 1) * S])
    return [unit(b, h) for b in range(NB) for h in range(HEADS)]


def single_units(c):
    def unit(b):
        return (lambda t: c.xT[:, (b * QT + t) * P:(b * QT + t + 1) * P], c.ctxT[:, b * S:(b + 1) * S],
                lambda kt: c.ctx[:, b * QT + kt, :], slice(0, P), lambda t: c.m_causal[:, t, :],
                c.oT[:, 0, b * S:(b + 1) * S])
    return [unit(b) for b in range(NB)]


def stage_turn_back(nc, c, groups, width, gate, norm):
    with ExitStack() as ctx:
        tr, chain_v, *nsems = c.semaphores(nc, ("tb_turned", "tb_dve") + Norm.NAMES)
        norm.take(nsems)
        block = ctx.enter_context(nc.Block())

        @block.tensor
        def _(pe):
            for t in range(NT):
                for g in range(groups):
                    mm = pe.transpose(c.ps[t][:, g * P:(g + 1) * P], c.oT[:, g, t * P:(t + 1) * P], c.ident[:, :])
                mm.then_inc(tr, 1)
            norm.pe(pe, c)

        @block.scalar
        def _(act):
            norm.act(act, c)

        @block.vector
        def _(dve):
            v = Chain(dve, chain_v)
            for t in range(NT):
                dve.wait_ge(tr, t + 1)
                src = c.ps[t][:, 0:groups * P]
                dst = c.x[:, t, :]
                if width < P:
                    src = src.rearrange("p (h d) -> p h d", d=PAD)[:, :, 0:width]
                    dst = dst.rearrange("p (h d) -> p h d", d=width)
                v.mark(dve.scalar_tensor_tensor(out=dst, in0=src, scalar=gate, in1=dst, op0=ALU.mult, op1=ALU.add))
            for t in range(NT):
                residual_stats(dve, v, c, c.x, t, t + 1)
            norm.dve(dve, v, c)


def stage_out(nc, c, w, tiles, res, bias, gate, norm=None, fetch=(), awaited=(), keep=None):
    with ExitStack() as ctx:
        done, chain_v, *nsems = c.semaphores(nc, ("op_done", "op_dve") + Norm.NAMES)
        block = ctx.enter_context(nc.Block())
        background_loads(block, fetch, awaited)
        if norm:
            norm.take(nsems)

        @block.tensor
        def _(pe):
            for t in range(NT):
                for f in range(tiles):
                    mm = pe.matmul(c.ps[t][:, 0:D], c.oT[:, f, t * P:(t + 1) * P], w[:, f, :],
                                   start=(f == 0), stop=(f == tiles - 1))
                mm.then_inc(done, 1)
            if norm:
                norm.pe(pe, c)

        @block.scalar
        def _(act):
            if norm:
                norm.act(act, c)

        @block.vector
        def _(dve):
            v = Chain(dve, chain_v)
            add_residual(dve, v, c, done, res, bias, gate, norm)
            if keep is not None:
                dve.wait_ge(v.sem, v.n)
                dve.tensor_copy(keep, res[:, :, :])


def add_residual(dve, v, c, done, res, bias, gate, norm):
    for t in range(NT):
        dve.wait_ge(done, t + 1)
        if bias is None:
            v.mark(dve.scalar_tensor_tensor(out=res[:, t, :], in0=c.ps[t][:, 0:D], scalar=gate(t), in1=res[:, t, :],
                                            op0=ALU.mult, op1=ALU.add))
        else:
            v.link(dve.tensor_tensor(c.acc[:, t, :], c.ps[t][:, 0:D], bias, ALU.add))
            if gate is None:
                v.mark(dve.tensor_tensor(res[:, t, :], c.acc[:, t, :], res[:, t, :], ALU.add))
            else:
                v.mark(dve.scalar_tensor_tensor(out=res[:, t, :], in0=c.acc[:, t, :], scalar=gate(t), in1=res[:, t, :],
                                                op0=ALU.mult, op1=ALU.add))
        if norm:
            residual_stats(dve, v, c, res, t, v.n)
    if norm:
        norm.dve(dve, v, c)



def stage_gelu_ffn(nc, c, w1, b1, w2, b2, res, gate, norm, fetch=(), awaited=(), routed=False):
    nf, e = FF // P, 8
    with ExitStack() as ctx:
        up, act_done, done, chain_v, logits, centred, exped, *nsems = c.semaphores(nc, (
            "ff_up", "ff_gelu", "ff_done", "ff_dve", "ff_logits", "ff_centred", "ff_exp") + Norm.NAMES)
        norm.take(nsems)
        block = ctx.enter_context(nc.Block())
        background_loads(block, fetch, awaited)

        @block.tensor
        def _(pe):
            if routed:
                for t in range(NT):
                    mm = pe.matmul(c.ps[0][:, t * 16:t * 16 + e], c.xT[:, t * P:(t + 1) * P], c.wr0[:, :],
                                   start=True, stop=True)
                mm.then_inc(logits, 1)
            for f in range(nf):
                pe.matmul(c.ps[4 + f][:, :], w1[:, f * P:(f + 1) * P], c.xT[:, :], start=True, stop=True).then_inc(up, 1)
            if routed:
                pe.wait_ge(centred, 1)
            for f in range(nf):
                pe.wait_ge(act_done, f + 1)
                for t in range(NT):
                    mm = pe.matmul(c.ps[t][:, 0:D], c.qT[:, f, t * P:(t + 1) * P], w2[:, f, :],
                                   start=(f == 0), stop=(f == nf - 1))
                    if f == nf - 1:
                        mm.then_inc(done, 1)
            norm.pe(pe, c)

        @block.scalar
        def _(act):
            for f in range(nf):
                act.wait_ge(up, f + 1)
                act.activation(c.qT[:, f, :], c.ps[4 + f][:, :], ACT.Gelu, bias=b1[:, f:f + 1]).then_inc(act_done, 1)
            if routed:
                act.wait_ge(centred, 1)
                act.activation(c.ex[:, 0:NT, 0:e], c.lg[:, 0:NT, 0:e], ACT.Exp).then_inc(exped, 1)
            norm.act(act, c)

        @block.vector
        def _(dve):
            v = Chain(dve, chain_v)
            if routed:
                dve.wait_ge(logits, 1)
                v.link(dve.tensor_copy(c.lg[:, 0:NT, 0:e],
                                       c.ps[0][:, 0:16 * NT].rearrange("p (t e) -> p t e", e=16)[:, :, 0:e]))
                softmax_steps(dve, v, c, NT, e, centred, exped)
                v.link(dve.tensor_scalar(c.cw[:, 0:NT, 0:1], c.pr[:, 0:NT, e - 1:e], c.gate[:, 4:5], None, ALU.mult))
            add_residual(dve, v, c, done, res, b2, gate, norm)


def softmax_steps(dve, v, c, n, e, logits_to, exped):
    lg, ex, pr = (a[:, 0:n, 0:e] for a in (c.lg, c.ex, c.pr))

    def wide(a):
        return a[:, 0:n].rearrange("p (n a) -> p n a", a=1).to_broadcast([P, n, e])
    v.link(dve.tensor_reduce(c.rm[:, 0:n], lg, AX.X, ALU.max))
    dve.tensor_tensor(lg, lg, wide(c.rm), ALU.subtract).then_inc(logits_to, 1)
    dve.wait_ge(exped, 1)
    v.link(dve.tensor_reduce(c.rs[:, 0:n], ex, AX.X, ALU.add))
    v.link(dve.reciprocal(c.rs[:, 0:n], c.rs[:, 0:n]))
    v.link(dve.tensor_tensor(pr, ex, wide(c.rs), ALU.mult))


def top_steps(dve, v, c, n, e, k):
    for t in range(n):
        v.mark(dve.max(c.top[:, t, :], c.pr[:, t, 0:e]))
    dve.wait_ge(v.sem, v.n)
    for j in range(k, 8):
        v.mark(dve.memset(c.top[:, 0:n, j:j + 1], -2.0))
    dve.wait_ge(v.sem, v.n)
    for t in range(n):
        v.mark(dve.match_replace(c.rest[:, t, 0:e], c.top[:, t, :], c.pr[:, t, 0:e], -1.0))
    dve.wait_ge(v.sem, v.n)
    v.link(dve.tensor_scalar(c.sel[:, 0:n, 0:e], c.rest[:, 0:n, 0:e], -1.0, None, ALU.is_equal))


def stage_moe1(nc, c, norm, awaited):
    ne = E1 + 1
    with ExitStack() as ctx:
        done, centred, exped, chain_v, weighted, wt, wtc, up, act_done, down, used, *nsems = c.semaphores(nc, (
                "m1_logits", "m1_centred", "m1_exp", "m1_dve", "m1_weights", "m1_wt", "m1_wtcopied", "m1_up",
                "m1_relu", "m1_down", "m1_used") + Norm.NAMES)
        norm.take(nsems)
        block = ctx.enter_context(nc.Block())
        background_loads(block, (), awaited)

        @block.tensor
        def _(pe):
            for t in range(NT):
                mm = pe.matmul(c.ps[0][:, t * 16:t * 16 + E1], c.xT[:, t * P:(t + 1) * P], c.wr1[:, :], start=True, stop=True)
            mm.then_inc(done, 1)

            def up_proj(e):
                if e >= 2:
                    pe.wait_ge(act_done, e - 1)
                pe.matmul(c.ps[2 + e % 2][:, :], c.ew1[:, e, :], c.xT[:, :], start=True, stop=True).then_inc(up, 1)
            up_proj(0)
            for e in range(ne):
                if e + 1 < ne:
                    up_proj(e + 1)
                pe.wait_ge(act_done, e + 1)
                if e >= 4:
                    pe.wait_ge(used, NT * (e - 3))
                for t in range(NT):
                    mm = pe.matmul(c.ps[4 + e % 4][:, t * P:(t + 1) * P], c.qT[:, e % 2, t * P:(t + 1) * P],
                                   c.ew2[:, e, :], start=True, stop=True)
                mm.then_inc(down, 1)
            pe.wait_ge(weighted, 1)
            for t in range(NT):
                mm = pe.transpose(c.ps[1][0:ne, t * P:(t + 1) * P], c.cw[:, t, :], c.ident[:, :])
            mm.then_inc(wt, 1)
            pe.wait_ge(wtc, 1)
            for t in range(NT):
                mm = pe.matmul(c.ps[1][:, t * P:(t + 1) * P], c.cwT[:, t * P:(t + 1) * P], c.eb2[:, :],
                               start=True, stop=True)
            mm.then_inc(down, 1)
            norm.pe(pe, c, idle=3)

        @block.scalar
        def _(act):
            act.wait_ge(centred, 1)
            act.activation(c.ex[:, 0:NT, 0:E1], c.lg[:, 0:NT, 0:E1], ACT.Exp).then_inc(exped, 1)
            for e in range(ne):
                act.wait_ge(up, e + 1)
                if e >= 2:
                    act.wait_ge(down, e - 1)
                act.activation(c.qT[:, e % 2, :], c.ps[2 + e % 2][:, :], ACT.Relu, bias=c.eb1[:, e:e + 1]).then_inc(act_done, 1)
            act.wait_ge(wt, 1)
            act.copy(c.cwT[:, :], c.ps[1][0:ne, :]).then_inc(wtc, 1)
            norm.act(act, c)

        @block.vector
        def _(dve):
            v = Chain(dve, chain_v)
            dve.wait_ge(done, 1)
            br = c.br1[:, :].rearrange("p (a e) -> p a e", a=1).to_broadcast([P, NT, E1])
            v.link(dve.tensor_tensor(c.lg[:, 0:NT, 0:E1],
                                     c.ps[0][:, 0:16 * NT].rearrange("p (t e) -> p t e", e=16)[:, :, 0:E1], br, ALU.add))
            softmax_steps(dve, v, c, NT, E1, centred, exped)
            top_steps(dve, v, c, NT, E1, K1)
            v.mark(dve.memset(c.cw[:, 0:NT, E1:ne], 1.0))
            v.link(dve.tensor_tensor(c.cw[:, 0:NT, 0:E1], c.pr[:, 0:NT, 0:E1], c.sel[:, 0:NT, 0:E1], ALU.mult))
            dve.tensor_scalar(c.cw[:, 0:NT, :], c.cw[:, 0:NT, :], c.gate[:, 5:6], None, ALU.mult).then_inc(weighted, 1)
            dve.wait_ge(weighted, 1)
            for e in range(ne):
                dve.wait_ge(down, e + 1)
                if e:
                    dve.wait_ge(used, NT * e)
                for t in range(NT):
                    dve.scalar_tensor_tensor(out=c.x[:, t, :], in0=c.ps[4 + e % 4][:, t * P:(t + 1) * P],
                                             scalar=c.cw[:, t, e:e + 1], in1=c.x[:, t, :],
                                             op0=ALU.mult, op1=ALU.add).then_inc(used, 1)
            dve.wait_ge(down, ne + 1)
            dve.wait_ge(used, NT * ne)
            for t in range(NT):
                v.mark(dve.tensor_tensor(c.x[:, t, :], c.x[:, t, :], c.ps[1][:, t * P:(t + 1) * P], ALU.add))
            for t in range(NT):
                residual_stats(dve, v, c, c.x, t, v.n - NT + 1)
            norm.dve(dve, v, c)


def stage_linear(nc, c, w, bias, gate, norm):
    with ExitStack() as ctx:
        done, chain_v, *nsems = c.semaphores(nc, ("ln_done", "ln_dve") + Norm.NAMES)
        norm.take(nsems)
        block = ctx.enter_context(nc.Block())

        @block.tensor
        def _(pe):
            for t in range(NT):
                pe.matmul(c.ps[t][:, 0:D], c.xT[:, t * P:(t + 1) * P], w, start=True, stop=True).then_inc(done, 1)
            norm.pe(pe, c)

        @block.scalar
        def _(act):
            norm.act(act, c)

        @block.vector
        def _(dve):
            add_residual(dve, Chain(dve, chain_v), c, done, c.x, bias, lambda t: gate, norm)


SHARED = 2


def expert_weights(c, k):
    w = c.wa[:, k % 2, :]
    return w[:, 0:FF], w[:, FF:2 * FF], w[:, 2 * FF:3 * FF].rearrange("p (f n) -> p f n", n=D)


def expert_loads(c, A, k):
    if k < SHARED:
        a = k * FF
        srcs = (A["L3_ffn_sg"][:, a:a + FF], A["L3_ffn_su"][:, a:a + FF], A["L3_ffn_sd"][a:a + FF, :])
    else:
        srcs = (A["L3_ffn_rg"][k - SHARED], A["L3_ffn_ru"][k - SHARED], A["L3_ffn_rd"][k - SHARED])
    g, u, d = expert_weights(c, k)
    sem = c.attn_loaded[k % 2]
    return [(g, srcs[0], sem), (u, srcs[1], sem), (d, srcs[2].rearrange("(f p) n -> p f n", p=P), sem)]


def over_experts(a):
    return a[:, :].rearrange("p (n a) -> p n a", a=1).to_broadcast([P, TILES, E3])


def expert_slots(dve, c, e):
    place = last_buffers(c)[2]
    for t in range(TILES):
        last = dve.tensor_scalar(c.disp[:, e % 2, t, :], c.iota[:, 0:CAP], place[:, t, e:e + 1], None, ALU.is_equal)
    return last


def last_buffers(c):
    return c.y, c.kT[:, 5:7, :], c.rest[:, :, 0:E3], c.cwT[0:E3, :].bitcast(BF16)


def stage_route3(nc, c, A):
    nf = FF // P
    xf, xallT, place, placeT = last_buffers(c)
    xn, xnT = c.v[:, 0, :].rearrange("p (t n) -> p t n", n=D), c.roped[:, 0, :].rearrange("p (s n) -> p s n", s=2)
    high, hidden = c.v[:, 2, :], c.oT
    steps = [(k, s) for k in range(SHARED) for s in range(2)]
    with ExitStack() as ctx:
        names = ("r3_xready", "r3_ready", "r3_xturned", "r3_nturned", "r3_copied", "r3_logits", "r3_centred", "r3_exp",
                 "r3_dve", "r3_sel", "r3_count", "r3_placed", "r3_pturned", "r3_gate", "r3_up", "r3_silu", "r3_hidden",
                 "r3_down", "r3_added")
        (xready, ready, xturned, nturned, copied, lgs, centred, exped, chain_v, selected, counted, placed,
         pturned, gsem, usem, silu, hsem, down, used) = c.semaphores(nc, names)
        block = ctx.enter_context(nc.Block())

        @block.sync
        def _(sp):
            for k in range(SHARED + 1):
                if k == SHARED:
                    sp.wait_ge(down, 2)
                for dst, src, sem in expert_loads(c, A, k):
                    sp.dma_start(dst, src).then_inc(sem, 16)

        @block.tensor
        def _(pe):
            def up_proj(first, last):
                for n in range(first, last):
                    k, s = steps[n // nf]
                    f = n % nf
                    g, u, _ = expert_weights(c, k)
                    if n % (2 * nf) == 0:
                        pe.wait_ge(c.attn_loaded[k], 48)
                    if n >= 2:
                        pe.wait_ge(hsem, n - 1)
                    x = xallT[:, s, :]
                    pe.matmul(c.ps[n % 2][:, :], g[:, f * P:(f + 1) * P], x, start=True, stop=True).then_inc(gsem, 1)
                    pe.matmul(c.ps[2 + n % 2][:, :], u[:, f * P:(f + 1) * P], x, start=True, stop=True).then_inc(usem, 1)

            def down_proj(i):
                k, _ = steps[i]
                pe.wait_ge(hsem, nf * (i + 1))
                if i >= 2:
                    pe.wait_ge(used, NT * (i - 1))
                for t in range(NT):
                    for f in range(nf):
                        mm = pe.matmul(c.ps[4 + i % 2][:, t * P:(t + 1) * P],
                                       hidden[:, (i % 2) * nf + f, t * P:(t + 1) * P],
                                       expert_weights(c, k)[2][:, f, :], start=(f == 0), stop=(f == nf - 1))
                mm.then_inc(down, 1)

            keep_clock(pe, c, c.ps[6], NORM_FILL)
            for t in range(TILES):
                pe.wait_ge(xready, t + 1)
                mm = pe.transpose(c.ps[t // 4][:, (t % 4) * P:(t % 4 + 1) * P], xf[:, t, :], c.ident[:, :])
                if t % 4 == 3:
                    mm.then_inc(xturned, 1)
            pe.wait_ge(copied, 2)
            up_proj(0, 2)
            for t in range(TILES):
                pe.wait_ge(ready, t + 1)
                mm = pe.transpose(c.ps[6 + t // 4][:, (t % 4) * P:(t % 4 + 1) * P], xn[:, t, :], c.ident[:, :])
                if t % 4 == 3:
                    mm.then_inc(nturned, 1)
            pe.wait_ge(copied, 4)
            for t in range(TILES):
                mm = pe.matmul(c.ps[4][:, t * E3:(t + 1) * E3], xnT[:, t // 4, (t % 4) * P:(t % 4 + 1) * P],
                               c.wr3[:, :], start=True, stop=True)
            mm.then_inc(lgs, 1)
            up_proj(2, 4)
            down_proj(0)
            pe.wait_ge(selected, 1)
            pe.matmul(c.ps[5][:, 0:TILES * E3], c.tri_bf[:, :], c.selb[:, :, :].rearrange("p t e -> p (t e)"),
                      start=True, stop=False)
            pe.matmul(c.ps[5][:, 0:TILES * E3], c.ones_bf[:, :], c.before[:, :, :].rearrange("p t e -> p (t e)"),
                      start=False, stop=True).then_inc(counted, 1)
            up_proj(4, 6)
            up_proj(6, 8)
            pe.wait_ge(placed, 1)
            for t in range(TILES):
                mm = pe.transpose(c.ps[6 + t // 4][0:E3, (t % 4) * P:(t % 4 + 1) * P], place[:, t, :], c.ident[:, :])
            mm.then_inc(pturned, 1)
            for i in range(1, len(steps)):
                if i + 1 < len(steps):
                    up_proj((i + 1) * nf, (i + 2) * nf)
                down_proj(i)

        @block.scalar
        def _(act):
            def gates(first, last):
                for n in range(first, last):
                    act.wait_ge(gsem, n + 1)
                    if n >= 2:
                        act.wait_ge(hsem, n - 1)
                    act.activation(c.probsT[:, n % 2, :], c.ps[n % 2][:, :], ACT.Silu).then_inc(silu, 1)

            for j in range(2):
                act.wait_ge(xturned, j + 1)
                act.copy(xallT[:, j, :], c.ps[j][:, :]).then_inc(copied, 1)
            gates(0, 2)
            for j in range(2):
                act.wait_ge(nturned, j + 1)
                act.copy(xnT[:, j, :], c.ps[6 + j][:, :]).then_inc(copied, 1)
            gates(2, 3)
            act.wait_ge(centred, 1)
            act.activation(c.ex[:, :, 0:E3], c.lg[:, :, 0:E3], ACT.Exp).then_inc(exped, 1)
            gates(3, 8)
            act.wait_ge(pturned, 1)
            for j in range(2):
                act.copy(placeT[:, j * TOK:(j + 1) * TOK], c.ps[6 + j][0:E3, :])
            gates(8, nf * len(steps))

        @block.vector
        def _(dve):
            v = Chain(dve, chain_v)

            def gated(first, last):
                for n in range(first, last):
                    i = n // nf
                    dve.wait_ge(silu, n + 1)
                    dve.wait_ge(usem, n + 1)
                    if i >= 2:
                        dve.wait_ge(down, i - 1)
                    dve.tensor_tensor(hidden[:, (i % 2) * nf + n % nf, :], c.ps[2 + n % 2][:, :], c.probsT[:, n % 2, :],
                                      ALU.mult).then_inc(hsem, 1)

            def add(i):
                dve.wait_ge(down, i + 1)
                if i >= 2:
                    dve.wait_ge(used, NT * (i - 1))
                for t in range(NT):
                    x = c.x3[:, steps[i][1] * NT + t, :]
                    dve.scalar_tensor_tensor(out=x, in0=c.ps[4 + i % 2][:, t * P:(t + 1) * P],
                                             scalar=c.gate[:, 7:8], in1=x, op0=ALU.mult, op1=ALU.add).then_inc(used, 1)

            norm_steps(dve, v, c, c.x3, xf, TILES, "layer", xready)
            dve.wait_ge(xready, TILES)
            norm_steps(dve, v, c, xf, xn, TILES, "rms_eps", ready)
            gated(0, 2)
            flat = xf[:, :, :].rearrange("p t n -> p (t n)")
            v.link(dve.tensor_scalar(high.bitcast(I32), flat.bitcast(I32), HIGH_BITS, None, ALU.bitwise_and))
            dve.wait_ge(lgs, 1)
            v.link(dve.tensor_copy(c.lg[:, :, 0:E3], c.ps[4][:, 0:TILES * E3].rearrange("p (t e) -> p t e", e=E3)))
            v.link(dve.tensor_reduce(c.rm[:, :], c.lg[:, :, 0:E3], AX.X, ALU.max))
            dve.tensor_tensor(c.lg[:, :, 0:E3], c.lg[:, :, 0:E3], over_experts(c.rm), ALU.subtract).then_inc(centred, 1)
            dve.tensor_copy(c.qparts[:, 0:2, :].rearrange("p a n -> p (a n)"), high)
            gated(2, 3)
            dve.wait_ge(exped, 1)
            v.link(dve.tensor_reduce(c.rs[:, :], c.ex[:, :, 0:E3], AX.X, ALU.add))
            v.link(dve.reciprocal(c.rs[:, :], c.rs[:, :]))
            v.link(dve.tensor_tensor(c.pr[:, :, 0:E3], c.ex[:, :, 0:E3], over_experts(c.rs), ALU.mult))
            gated(3, 4)
            top_steps(dve, v, c, TILES, E3, K3)
            v.mark(dve.tensor_copy(c.selb[:, :, :], c.sel[:, :, 0:E3]))
            v.link(dve.memset(c.before[:, 0, :], 0.0))
            for t in range(1, TILES):
                last = dve.tensor_tensor(c.before[:, t, :], c.before[:, t - 1, :], c.selb[:, t - 1, :], ALU.add)
                if t < TILES - 1:
                    v.link(last)
            last.then_inc(selected, 1)
            v.link(dve.tensor_tensor(c.cw[:, :, 0:E3], c.pr[:, :, 0:E3], c.sel[:, :, 0:E3], ALU.mult))
            v.link(dve.tensor_reduce(c.rs[:, :], c.cw[:, :, 0:E3], AX.X, ALU.add))
            v.link(dve.reciprocal(c.rs[:, :], c.rs[:, :]))
            v.link(dve.tensor_tensor(c.cw[:, :, 0:E3], c.cw[:, :, 0:E3], over_experts(c.rs), ALU.mult))
            add(0)
            dve.wait_ge(counted, 1)
            v.link(dve.tensor_tensor(place, c.ps[5][:, 0:TILES * E3].rearrange("p (t e) -> p t e", e=E3),
                                     c.sel[:, :, 0:E3], ALU.mult))
            dve.tensor_scalar(place, place, -1.0, 255.0, ALU.add, ALU.min).then_inc(placed, 1)
            gated(4, 8)
            dve.tensor_scalar(c.cw[:, :, 0:E3], c.cw[:, :, 0:E3], c.gate[:, 7:8], None, ALU.mult)
            dve.tensor_tensor(c.qparts[:, 2:4, :].rearrange("p a n -> p (a n)"), flat, high, ALU.subtract)
            dve.tensor_copy(c.pick[:, :, :], c.ident_bf[0:E3, 0:E3].rearrange("p (e a) -> p e a", a=1)
                            .to_broadcast([E3, E3, P]))
            for i in range(1, len(steps)):
                if i + 1 < len(steps):
                    gated((i + 1) * nf, (i + 2) * nf)
                if i <= 2:
                    expert_slots(dve, c, i - 1)
                add(i)


def stage_experts3(nc, c, A, out):
    nf = FF // P
    placeT = last_buffers(c)[3]
    xparts = c.qparts[:, :, :].rearrange("p (j s) (t n) -> p j (s t) n", j=2, n=D)
    spread0, spread1 = (c.probsT[0:r, j:j + 2, :].rearrange("p s n -> p (s n)") for r, j in ((P, 0), (CAP - P, 2)))
    placeb, y = c.probsT[:, 6:8, :], c.acc
    tiles = ((0, P), (P, CAP))
    with ExitStack() as ctx:
        names = ("m3_placed", "m3_pcopied", "m3_spread", "m3_picked", "m3_gathered", "m3_gcopied", "m3_up", "m3_silu",
                 "m3_hidden", "m3_down", "m3_ycopied", "m3_combined", "m3_added", "m3_stored")
        (placed, pcopied, spread, picked, gathered, gcopied, up, silu, hsem, down, ycopied, combined,
         added, stored) = c.semaphores(nc, names)
        block = ctx.enter_context(nc.Block())

        @block.sync
        def _(sp):
            for e in range(1, E3):
                if e >= 2:
                    sp.wait_ge(down, e - 1)
                for dst, src, sem in expert_loads(c, A, SHARED + e):
                    sp.dma_start(dst, src).then_inc(sem, 16)
            rows = out.rearrange("b (t p) f -> p (b t) f", p=P)
            for s in range(2):
                sp.wait_ge(added, TILES * (E3 - 1) + NT * (s + 1))
                sp.dma_start(rows[:, s * NT:(s + 1) * NT, :], c.x3[:, s * NT:(s + 1) * NT, :]).then_inc(stored, 16)
            sp.wait_ge(stored, 32)

        @block.tensor
        def _(pe):
            def place_rows(e):
                if e:
                    pe.wait_ge(pcopied, e)
                for j in range(2):
                    mm = pe.matmul(c.ps[3 + j][:, :], c.pick[:, e, :], placeT[:, j * TOK:(j + 1) * TOK],
                                   start=True, stop=True)
                mm.then_inc(placed, 1)

            def gather(e):
                if e >= 2:
                    pe.wait_ge(picked, e - 1)
                if e:
                    pe.wait_ge(gcopied, e)
                for t in range(TILES):
                    for j in range(2):
                        mm = pe.matmul(c.ps[2][:, 0:CAP], xparts[:, j, t, :], c.disp[:, e % 2, t, :],
                                       start=(t == 0 and j == 0), stop=(t == TILES - 1 and j == 1))
                mm.then_inc(gathered, 1)

            def up_proj(e):
                g, u, _ = expert_weights(c, SHARED + e)
                pe.wait_ge(c.attn_loaded[e % 2], 48 * ((SHARED + e) // 2 + 1))
                pe.wait_ge(gcopied, e + 1)
                for f in range(nf):
                    n = e * nf + f
                    if n >= 2:
                        pe.wait_ge(hsem, n - 1)
                    pe.matmul(c.ps[n % 2][:, 0:CAP], g[:, f * P:(f + 1) * P], c.xT[:, 0:CAP], start=True, stop=True)
                    pe.matmul(c.ps[n % 2][:, S:S + CAP], u[:, f * P:(f + 1) * P], c.xT[:, 0:CAP],
                              start=True, stop=True).then_inc(up, 1)
                    if f == 1:
                        place_rows(e)
            gather(0)
            up_proj(0)
            for e in range(E3):
                if e + 1 < E3:
                    gather(e + 1)
                pe.wait_ge(hsem, nf * (e + 1))
                if e:
                    pe.wait_ge(ycopied, e)
                for j, (a, b) in enumerate(tiles):
                    for f in range(nf):
                        mm = pe.matmul(c.ps[5][0:b - a, j * D:(j + 1) * D], c.oT[:, (e % 2) * nf + f, a:b],
                                       expert_weights(c, SHARED + e)[2][:, f, :], start=(f == 0), stop=(f == nf - 1))
                mm.then_inc(down, 1)
                if e + 1 < E3:
                    up_proj(e + 1)
                pe.wait_ge(ycopied, e + 1)
                pe.wait_ge(spread, e + 1)
                if e:
                    pe.wait_ge(added, TILES * e)
                for t in range(TILES):
                    out = c.ps[6 + t // 4][:, (t % 4) * P:(t % 4 + 1) * P]
                    pe.matmul(out, spread0[:, t * P:(t + 1) * P], y[:, 0, :], start=True, stop=False)
                    mm = pe.matmul(out, spread1[:, t * P:(t + 1) * P], y[0:CAP - P, 1, :], start=False, stop=True)
                    if t % 4 == 3:
                        mm.then_inc(combined, 1)

        @block.scalar
        def _(act):
            def gathered_out(e):
                act.wait_ge(gathered, e + 1)
                if e:
                    act.wait_ge(up, nf * e)
                act.copy(c.xT[:, 0:CAP], c.ps[2][:, 0:CAP]).then_inc(gcopied, 1)

            def gates(e):
                for f in range(nf):
                    n = e * nf + f
                    act.wait_ge(up, n + 1)
                    if n >= 2:
                        act.wait_ge(hsem, n - 1)
                    act.activation(c.probsT[:, 4 + n % 2, 0:CAP], c.ps[n % 2][:, 0:CAP], ACT.Silu).then_inc(silu, 1)
            gathered_out(0)
            gates(0)
            for e in range(E3):
                act.wait_ge(placed, e + 1)
                if e:
                    act.wait_ge(spread, e)
                act.copy(placeb[:, 0, :], c.ps[3][:, :])
                act.copy(placeb[:, 1, :], c.ps[4][:, :]).then_inc(pcopied, 1)
                if e + 1 < E3:
                    gathered_out(e + 1)
                act.wait_ge(down, e + 1)
                if e:
                    act.wait_ge(combined, 2 * e)
                act.copy(y[:, 0, :], c.ps[5][:, 0:D])
                act.copy(y[0:CAP - P, 1, :], c.ps[5][0:CAP - P, D:2 * D]).then_inc(ycopied, 1)
                if e + 1 < E3:
                    gates(e + 1)

        @block.vector
        def _(dve):
            def gated(e):
                if e >= 2:
                    dve.wait_ge(down, e - 1)
                for f in range(nf):
                    n = e * nf + f
                    dve.wait_ge(silu, n + 1)
                    dve.tensor_tensor(c.oT[:, (e % 2) * nf + f, 0:CAP], c.ps[n % 2][:, S:S + CAP],
                                      c.probsT[:, 4 + n % 2, 0:CAP], ALU.mult).then_inc(hsem, 1)
            gated(0)
            for e in range(E3):
                dve.wait_ge(pcopied, e + 1)
                if e:
                    dve.wait_ge(combined, 2 * e)
                flat = placeb.rearrange("p s n -> p (s n)")
                dve.tensor_scalar(spread0, flat, c.slot[:, 0:1], None, ALU.is_equal)
                dve.tensor_scalar(spread1, flat[0:CAP - P, :], c.slot[0:CAP - P, 1:2], None,
                                  ALU.is_equal).then_inc(spread, 1)
                if e + 2 < E3:
                    dve.wait_ge(gathered, e + 1)
                    expert_slots(dve, c, e + 2).then_inc(picked, 1)
                if e + 1 < E3:
                    gated(e + 1)
                if e:
                    dve.wait_ge(added, TILES * e)
                for t in range(TILES):
                    dve.wait_ge(combined, 2 * e + t // 4 + 1)
                    x = c.x3[:, t, :]
                    dve.scalar_tensor_tensor(out=x, in0=c.ps[6 + t // 4][:, (t % 4) * P:(t % 4 + 1) * P],
                                             scalar=c.cw[:, t, e:e + 1], in1=x,
                                             op0=ALU.mult, op1=ALU.add).then_inc(added, 1)


def attention_loads(c, A, k):
    l, cross = k // 2, k % 2
    w, sem = c.wa[:, cross, :], c.attn_loaded[cross]
    names = ("cWq", "cWk", "cWv", "cWo") if cross else ("Wq", "Wk", "Wv", "Wo")
    parts = [A["L2_xattn_" + n][l] for n in names]
    return [(w[:, j * INNER:(j + 1) * INNER], parts[j], sem) for j in range(3)] + [
        (w[:, 3 * INNER:].rearrange("p (f n) -> p f n", n=D), parts[3].rearrange("(f p) n -> p f n", p=P), sem)]


def ff_loads(c, A, l):
    return [(c.wff1[:, :], A["L2_xattn_ff_w1"][l], c.ff_loaded),
            (c.wff2[:, :, :], A["L2_xattn_ff_w2"][l].rearrange("(f p) n -> p f n", p=P), c.ff_loaded),
            (c.bff2[:, :], A["L2_xattn_ff_b2"][l].partition_broadcast(P), c.ff_loaded)]


def flamingo_kernel(nc, A, out):
    with ExitStack() as ctx:
        ctx.enter_context(nc.allow_non_contiguous_dma(reason="broadcast rows, some hundred elements"))
        c = allocate(nc, ctx)
        stage_setup(nc, c, A)
        with nc.Fori(0, HALVES) as half:
            stage_load(nc, c, A, half, Norm(c.x, "layer", values=Values(c.w0, GN * P)))

            stage_narrow_qkv(nc, c, c.w0r, c.w0r, None, awaited=[(c.constants, c.n_constants)],
                             fetch=attention_loads(c, A, 0) + attention_loads(c, A, 1) + ff_loads(c, A, 0))
            stage_heads(nc, c, narrow_units(c, lambda b, t: c.m_len[:, b, :]), 4, float(D) ** -0.5, late=True)
            stage_turn_back(nc, c, GN, DK, c.gate[:, 0:1], Norm(c.x, "layer"))
            stage_gelu_ffn(nc, c, c.w1_0, c.b1_0, c.w2_0, c.b2_0[:, :], c.x, lambda t: c.cw[:, t, 0:1],
                           Norm(c.x, "layer"), routed=True)

            stage_heads(nc, c, single_units(c), 1, float(D) ** -0.5)
            stage_turn_back(nc, c, 1, P, c.gate[:, 1:2], Norm(c.x, "layer"))
            stage_moe1(nc, c, Norm(c.x, "rms", c.nw[:, 0:1], inner=True), awaited=[(c.attn_loaded[0], 64)])

            for l in range(2):
                for cross in range(2):
                    k = 2 * l + cross
                    w = c.wa[:, cross, :]
                    stage_wide_qkv(nc, c, w, cross,
                                   fetch={1: attention_loads(c, A, 2), 2: ff_loads(c, A, 1)}.get(k, ()))
                    stage_heads(nc, c, wide_units(c, None if cross else lambda b, t: c.m_key[:, b, :]), 2,
                                float(DH) ** -0.5)
                    values = None if cross else Values(c.wa[:, 1, 2 * INNER:3 * INNER], INNER,
                                                       (c.attn_loaded[1], 64 * (l + 1)))
                    stage_out(nc, c, w[:, 3 * INNER:].rearrange("p (f n) -> p f n", n=D), FT, c.u,
                              c.bo2[:, k, :], None, Norm(c.u, "rms", c.nw[:, 2 * (cross + 1) + l:2 * (cross + 1) + l + 1],
                                                       values=values),
                              awaited=[(c.ff_loaded, 48 * (l + 1)) if cross else (c.attn_loaded[1], 64 * (l + 1))])
                stage_gelu_ffn(nc, c, c.wff1, c.bff1[:, l, :], c.wff2, c.bff2[:, :], c.u, None,
                               Norm(c.u, "rms", c.nw[:, 6:7] if l else c.nw[:, 1:2]),
                               fetch=() if l else attention_loads(c, A, 3),
                               awaited=() if l else [(c.attn_loaded[0], 128)])
            stage_linear(nc, c, c.proj[:, :], c.projb[:, :], c.gate[:, 2:3], Norm(c.x, "layer"))
            stage_linear(nc, c, c.signT[:, :], None, c.gate[:, 6:7],
                         Norm(c.x, "layer", values=Values(c.w3[:, 2, :], GN * P)))

            stage_narrow_qkv(nc, c, c.w3[:, 0, :], c.w3[:, 1, :], c.b3)
            stage_heads(nc, c, narrow_units(c, lambda b, t: c.m_full[:, b * QT + t, :]), 4, float(DK) ** -0.5,
                        out_bias=lambda g: c.b3[:, 2, g % GN:g % GN + 1], late=True)
            stage_out(nc, c, c.wo3, GN, c.x, c.bo3[:, :], lambda t: c.gate[:, 3:4],
                      keep=c.x3[:, bass.ds(half * NT, NT), :])

            nc.gpsimd.sem_clear(range(c.attn_loaded[0].num, c.sems[1][-1].num + 1))
            nc.all_engine_barrier()

        stage_route3(nc, c, A)
        stage_experts3(nc, c, A, out)


def kernel(**inputs):
    import numpy as np
    import concourse.bacc as bacc
    from concourse import mybir as mb
    from concourse.bass_utils import run_bass_kernel_spmd

    nc = bacc.Bacc("TRN2", target_bir_lowering=False, num_devices=1)
    arrays, A = {}, {}

    def give(name, a):
        a = np.ascontiguousarray(a)
        if a.dtype == np.bool_:
            a = a.view(np.uint8)
        arrays[f"in_{name}"] = a
        A[name] = nc.dram_tensor(f"in_{name}", a.shape, mb.dt.from_np(a.dtype), kind="ExternalInput").ap()

    for name, a in inputs.items():
        give(name, a)
    inv = (1.0 / np.float32(10000.0) ** (np.arange(0, ROT, 2, dtype=np.float32) / np.float32(ROT))).astype(np.float32)
    f = np.arange(S, dtype=np.float32)[:, None] * inv[None, :]
    cos, sin = np.cos(f), np.sin(f)
    give("rope_table", np.concatenate([cos, cos, -sin, sin], axis=1).astype(np.float32))
    row = np.arange(P)
    low_q, low_k = row // (2 * DK) % 2, row // DK % 2
    give("part_table", np.stack([low_q, 1 - 2 * low_q, low_k, 1 - 2 * low_k], axis=1).astype(np.float32))
    out = nc.dram_tensor("out_0", (B, S, D), F32, kind="ExternalOutput").ap()
    flamingo_kernel(nc, A, out)
    r = run_bass_kernel_spmd(nc, [arrays], core_ids=[0])
    return r.results[0]["out_0"]
```
